# Optimizing a Trainium2 kernel written in Bass

```python
import numpy as np
import jax
import jax.numpy as jnp

def _softmax(x, axis=-1):
    return jax.nn.softmax(x, axis=axis)

def _gelu(x):
    return jax.nn.gelu(x, approximate=True)

def _silu(x):
    return jax.nn.silu(x)

def _sigmoid(x):
    return jax.nn.sigmoid(x)

def _layernorm(x, axis=-1, eps=1e-05):
    m = jnp.mean(x, axis=axis, keepdims=True)
    v = jnp.var(x, axis=axis, keepdims=True)
    return (x - m) / jnp.sqrt(v + eps)

def _scatter_add(tgt, idx, src, axis=0):
    return tgt.at[idx].add(src)

def _segment_sum(src, seg, n):
    return jax.ops.segment_sum(src, seg, n)
kernel_name = 'mk_flamingo_gated_d2_seqx_r8_2b9ef7'

def setup_inputs(seed: int=0):
    np.random.seed(seed)
    _w = jnp.asarray

    def _rec_inputs():
        import jax
        import jax.numpy as jnp
        _rk = jax.random.key(seed)
        x = 7.22e-05 + 1 * jax.random.normal(jax.random.fold_in(_rk, 1), (2, 512, 128), jnp.float32)
        _lenS = 512 - jax.random.randint(jax.random.fold_in(_rk, 7), (2,), 0, max(1, 512 // 4) + 1, jnp.int32)
        _lenS2 = 77 - jax.random.randint(jax.random.fold_in(_rk, 8), (2,), 0, max(1, 77 // 4) + 1, jnp.int32)
        _ctx_1024P = jax.random.normal(jax.random.fold_in(_rk, 11), (2, 16, 128), jnp.float32)
        _ctx_1024c = jax.random.dirichlet(jax.random.fold_in(_rk, 511), 0.3 * jnp.ones((16,), jnp.float32), (2, 77))
        _ctx_1024t = jnp.einsum('bsk,bkd->bsd', _ctx_1024c, _ctx_1024P)
        _ctx_1024t = _ctx_1024t * jax.lax.rsqrt(jnp.mean(jnp.square(_ctx_1024t)) + 1e-12) * 0.953939
        ctx_1024 = 4.13588e-05 + 0.999923 * (_ctx_1024t + 0.3 * jax.random.normal(jax.random.fold_in(_rk, 611), (2, 77, 128), jnp.float32))
        _validS = jnp.arange(512)[None, :] < _lenS[:, None]
        _validS2 = jnp.arange(77)[None, :] < _lenS2[:, None]
        _causal = jnp.tril(jnp.ones((512, 512), dtype=bool))
        mask_BxS2_bk0 = jnp.logical_not(jnp.broadcast_to(_validS2[:, :], (2, 77)))
        _g = jax.random.normal(jax.random.fold_in(_rk, 9001), (2, 2), jnp.float32)
        _g = jnp.sign(_g) * jnp.maximum(jnp.abs(_g), 1.0) + (_g == 0) * 1.0
        g_xattn = _g[0]
        g_ffn = _g[1]
        return (x, ctx_1024, mask_BxS2_bk0, g_xattn, g_ffn)
    x, ctx_1024, mask_BxS2_bk0, g_xattn, g_ffn = _rec_inputs()

    def _L0_xattn_setup():
        import jax, jax.numpy as jnp
        import numpy as np
        import math
        B, T, D = (2, 512, 128)
        HD = D // 2
        DEPTH = 12
        LAMBDA_INIT = 0.8 - 0.6 * math.exp(-0.3 * DEPTH)
        SCALING = HD ** (-0.5)
        EPS = 1e-05
        key = jax.random.key(seed)
        ks = jax.random.split(key, 11)
        f32 = jnp.float32
        return {'q': jax.random.normal(ks[0], (B, T, D), f32), 'k': jax.random.normal(ks[1], (B, T, D), f32), 'v': jax.random.normal(ks[2], (B, T, D), f32), 'Wq': jax.random.normal(ks[3], (D, D), f32) * 0.02, 'Wk': jax.random.normal(ks[4], (HD, D), f32) * 0.02, 'Wv': jax.random.normal(ks[5], (D, D), f32) * 0.02, 'Wo': jax.random.normal(ks[6], (D, D), f32) * 0.02, 'lambda_q1': jax.random.normal(ks[7], (HD,), f32) * 0.1, 'lambda_k1': jax.random.normal(ks[8], (HD,), f32) * 0.1, 'lambda_q2': jax.random.normal(ks[9], (HD,), f32) * 0.1, 'lambda_k2': jax.random.normal(ks[10], (HD,), f32) * 0.1}
    _L0_xattn_all = _L0_xattn_setup()
    _L0_xattn_in = {k: v for k, v in _L0_xattn_all.items() if k in ('Wq', 'Wk', 'Wv', 'Wo', 'lambda_q1', 'lambda_k1', 'lambda_q2', 'lambda_k2')}
    del _L0_xattn_all

    def _L0_ffn_setup():
        import jax, jax.numpy as jnp
        import numpy as np
        TOP_P = 0.8
        B, T, H, F, E = (2, 256, 128, 512, 8)
        key = jax.random.key(seed)
        k0, k1, k2, k3 = jax.random.split(key, 4)
        x = jax.random.normal(k0, (B, T, H), jnp.float32)
        Wr = jax.random.normal(k1, (H, E), jnp.float32) * 0.02
        br = jnp.zeros((E,), jnp.float32)
        W1 = jax.random.normal(k2, (E, H, F), jnp.float32) * 0.02
        b1 = jnp.zeros((E, F), jnp.float32)
        W2 = jax.random.normal(k3, (E, F, H), jnp.float32) * 0.02
        b2 = jnp.zeros((E, H), jnp.float32)
        return {'x': x, 'Wr': Wr, 'br': br, 'W1': W1, 'b1': b1, 'W2': W2, 'b2': b2}
    _L0_ffn_all = _L0_ffn_setup()
    _L0_ffn_in = {k: v for k, v in _L0_ffn_all.items() if k in ('Wr', 'br', 'W1', 'b1', 'W2', 'b2')}
    del _L0_ffn_all

    def _L1_xattn_setup():
        import jax, jax.numpy as jnp
        import numpy as np
        B, N, M, DIM, H, DH = (2, 256, 256, 128, 16, 64)
        INNER = H * DH
        key = jax.random.key(seed)
        ks = jax.random.split(key, 6)
        x = jax.random.normal(ks[0], (B, N, DIM), dtype=jnp.float32)
        cond = jax.random.normal(ks[1], (B, M, DIM), dtype=jnp.float32)
        mask = jax.random.randint(ks[2], (B, M), 0, 2) > 0
        s = 0.02
        Wq = jax.random.normal(ks[3], (DIM, INNER), dtype=jnp.float32) * s
        Wkv = jax.random.normal(ks[4], (DIM, 2 * INNER), dtype=jnp.float32) * s
        Wo = jax.random.normal(ks[5], (INNER, DIM), dtype=jnp.float32) * s
        bo = jnp.zeros((DIM,), dtype=jnp.float32)
        return {'x': x, 'cond': cond, 'mask': mask, 'Wq': Wq, 'Wkv': Wkv, 'Wo': Wo, 'bo': bo}
    _L1_xattn_all = _L1_xattn_setup()
    _L1_xattn_in = {k: v for k, v in _L1_xattn_all.items() if k in ('Wq', 'Wkv', 'Wo', 'bo')}
    del _L1_xattn_all

    def _L1_ffn_setup():
        import jax, jax.numpy as jnp
        import numpy as np
        QMAX = 127.0

        def _ste_round(v):
            return v + jax.lax.stop_gradient(jnp.round(v) - v)

        def _act_fake_quant(x, clip_factor):
            scale = jax.nn.sigmoid(clip_factor) * jnp.max(jnp.abs(x)) / QMAX
            return jnp.clip(_ste_round(x / scale), -QMAX - 1.0, QMAX) * scale

        def _weight_fake_quant(w):
            scale = jnp.max(jnp.abs(w), axis=1, keepdims=True) / QMAX
            return jnp.clip(_ste_round(w / scale), -QMAX - 1.0, QMAX) * scale
        key = jax.random.key(seed)
        k1, k2, k3, k4 = jax.random.split(key, 4)
        B, S, H, I = (8, 1024, 128, 352)
        return {'x': jax.random.normal(k1, (B, S, H), dtype=jnp.float32), 'clip_x': jnp.full((1,), 4.0, dtype=jnp.float32), 'clip_down': jnp.full((1,), 4.0, dtype=jnp.float32), 'w_gate': jax.random.normal(k2, (I, H), dtype=jnp.float32) * 0.02, 'w_up': jax.random.normal(k3, (I, H), dtype=jnp.float32) * 0.02, 'w_down': jax.random.normal(k4, (H, I), dtype=jnp.float32) * 0.02}
    _L1_ffn_all = _L1_ffn_setup()
    _L1_ffn_in = {k: v for k, v in _L1_ffn_all.items() if k in ('clip_x', 'clip_down', 'w_gate', 'w_up', 'w_down')}
    del _L1_ffn_all
    return {'x': x, 'ctx_1024': ctx_1024, 'mask_BxS2_bk0': mask_BxS2_bk0, 'g_xattn': g_xattn, 'g_ffn': g_ffn, 'L0_xattn_Wq': _L0_xattn_in['Wq'], 'L0_xattn_Wk': _L0_xattn_in['Wk'], 'L0_xattn_Wv': _L0_xattn_in['Wv'], 'L0_xattn_Wo': _L0_xattn_in['Wo'], 'L0_xattn_lambda_q1': _L0_xattn_in['lambda_q1'], 'L0_xattn_lambda_k1': _L0_xattn_in['lambda_k1'], 'L0_xattn_lambda_q2': _L0_xattn_in['lambda_q2'], 'L0_xattn_lambda_k2': _L0_xattn_in['lambda_k2'], 'L0_ffn_Wr': _L0_ffn_in['Wr'], 'L0_ffn_br': _L0_ffn_in['br'], 'L0_ffn_W1': _L0_ffn_in['W1'], 'L0_ffn_b1': _L0_ffn_in['b1'], 'L0_ffn_W2': _L0_ffn_in['W2'], 'L0_ffn_b2': _L0_ffn_in['b2'], 'L1_xattn_Wq': _L1_xattn_in['Wq'], 'L1_xattn_Wkv': _L1_xattn_in['Wkv'], 'L1_xattn_Wo': _L1_xattn_in['Wo'], 'L1_xattn_bo': _L1_xattn_in['bo'], 'L1_ffn_clip_x': _L1_ffn_in['clip_x'], 'L1_ffn_clip_down': _L1_ffn_in['clip_down'], 'L1_ffn_w_gate': _L1_ffn_in['w_gate'], 'L1_ffn_w_up': _L1_ffn_in['w_up'], 'L1_ffn_w_down': _L1_ffn_in['w_down']}

def reference(x, ctx_1024, mask_BxS2_bk0, g_xattn, g_ffn, L0_xattn_Wq, L0_xattn_Wk, L0_xattn_Wv, L0_xattn_Wo, L0_xattn_lambda_q1, L0_xattn_lambda_k1, L0_xattn_lambda_q2, L0_xattn_lambda_k2, L0_ffn_Wr, L0_ffn_br, L0_ffn_W1, L0_ffn_b1, L0_ffn_W2, L0_ffn_b2, L1_xattn_Wq, L1_xattn_Wkv, L1_xattn_Wo, L1_xattn_bo, L1_ffn_clip_x, L1_ffn_clip_down, L1_ffn_w_gate, L1_ffn_w_up, L1_ffn_w_down):
    import jax
    import jax.numpy as jnp

    def _L0_xattn_ref(q, k, v, Wq, Wk, Wv, Wo, lambda_q1, lambda_k1, lambda_q2, lambda_k2):
        import jax, jax.numpy as jnp
        import numpy as np
        import math
        B, T, D = (2, 512, 128)
        HD = D // 2
        DEPTH = 12
        LAMBDA_INIT = 0.8 - 0.6 * math.exp(-0.3 * DEPTH)
        SCALING = HD ** (-0.5)
        EPS = 1e-05
        b, t, d = q.shape
        s = k.shape[1]
        qp = (q @ Wq.T).reshape(b, t, 2, HD).transpose(0, 2, 1, 3) * SCALING
        kp = k @ Wk.T
        scores = jnp.einsum('bhtd,bsd->bhts', qp, kp)
        scores = jax.nn.softmax(scores.astype(jnp.float32), axis=-1).astype(qp.dtype)
        lam1 = jnp.exp(jnp.sum(lambda_q1 * lambda_k1))
        lam2 = jnp.exp(jnp.sum(lambda_q2 * lambda_k2))
        lam = lam1 - lam2 + LAMBDA_INIT
        attn_w = scores[:, 0] - lam * scores[:, 1]
        vp = v @ Wv.T
        attn = jnp.einsum('bts,bsd->btd', attn_w, vp)
        rms = jax.lax.rsqrt(jnp.mean(jnp.square(attn), axis=-1, keepdims=True) + EPS)
        attn = attn * rms * (1.0 - LAMBDA_INIT)
        return attn @ Wo.T

    def _L0_ffn_ref(x, Wr, br, W1, b1, W2, b2):
        import jax, jax.numpy as jnp
        import numpy as np
        TOP_P = 0.8
        B, T, H, F, E = (2, 256, 128, 512, 8)
        probs = jax.nn.softmax(x @ Wr + br, axis=-1)
        sorted_idx = jnp.argsort(-probs, axis=-1)
        sorted_probs = jnp.take_along_axis(probs, sorted_idx, axis=-1)
        cum = jnp.cumsum(sorted_probs, axis=-1)
        mask = cum < TOP_P
        mask = mask.at[..., 0].set(True)
        inv = jnp.argsort(sorted_idx, axis=-1)
        keep = jnp.take_along_axis(mask, inv, axis=-1)
        gate = probs * keep
        h = jax.nn.relu(jnp.einsum('bth,ehf->betf', x, W1) + b1[None, :, None, :])
        y = jnp.einsum('betf,efh->beth', h, W2) + b2[None, :, None, :]
        return jnp.einsum('bte,beth->bth', gate, y)

    def _L1_xattn_ref(x, cond, mask, Wq, Wkv, Wo, bo):
        import jax, jax.numpy as jnp
        import numpy as np
        B, N, M, DIM, H, DH = (2, 256, 256, 128, 16, 64)
        INNER = H * DH
        b, n, _ = x.shape
        m = cond.shape[1]
        scale = DH ** (-0.5)
        q = (x @ Wq).reshape(b, n, H, DH).transpose(0, 2, 1, 3)
        kv = cond @ Wkv
        k, v = jnp.split(kv, 2, axis=-1)
        k = k.reshape(b, m, H, DH).transpose(0, 2, 1, 3)
        v = v.reshape(b, m, H, DH).transpose(0, 2, 1, 3)
        q = q * scale
        dots = jnp.einsum('bhid,bhjd->bhij', q, k)
        neg = -jnp.finfo(dots.dtype).max
        dots = jnp.where(mask[:, None, None, :], dots, neg)
        causal = jnp.triu(jnp.ones((n, m), dtype=bool), k=m - n + 1)
        dots = jnp.where(causal[None, None, :, :], neg, dots)
        attn = jax.nn.softmax(dots, axis=-1)
        out = jnp.einsum('bhij,bhjd->bhid', attn, v)
        out = out.transpose(0, 2, 1, 3).reshape(b, n, INNER)
        return out @ Wo + bo

    def _L1_ffn_ref(x, clip_x, clip_down, w_gate, w_up, w_down):
        import jax, jax.numpy as jnp
        import numpy as np
        QMAX = 127.0

        def _ste_round(v):
            return v + jax.lax.stop_gradient(jnp.round(v) - v)

        def _act_fake_quant(x, clip_factor):
            scale = jax.nn.sigmoid(clip_factor) * jnp.max(jnp.abs(x)) / QMAX
            return jnp.clip(_ste_round(x / scale), -QMAX - 1.0, QMAX) * scale

        def _weight_fake_quant(w):
            scale = jnp.max(jnp.abs(w), axis=1, keepdims=True) / QMAX
            return jnp.clip(_ste_round(w / scale), -QMAX - 1.0, QMAX) * scale
        xq = _act_fake_quant(x, clip_x[0])
        gate = jnp.einsum('bsh,ih->bsi', xq, _weight_fake_quant(w_gate))
        up = jnp.einsum('bsh,ih->bsi', xq, _weight_fake_quant(w_up))
        h = _act_fake_quant(jax.nn.silu(gate) * up, clip_down[0])
        return jnp.einsum('bsi,hi->bsh', h, _weight_fake_quant(w_down))
    x = x + jnp.tanh(g_xattn[0]) * _L0_xattn_ref(_layernorm(x, axis=-1), ctx_1024, ctx_1024, L0_xattn_Wq, L0_xattn_Wk, L0_xattn_Wv, L0_xattn_Wo, L0_xattn_lambda_q1, L0_xattn_lambda_k1, L0_xattn_lambda_q2, L0_xattn_lambda_k2)
    x = x + jnp.tanh(g_ffn[0]) * _L0_ffn_ref(_layernorm(x, axis=-1), L0_ffn_Wr, L0_ffn_br, L0_ffn_W1, L0_ffn_b1, L0_ffn_W2, L0_ffn_b2)
    x = x + jnp.tanh(g_xattn[1]) * _L1_xattn_ref(_layernorm(x, axis=-1), ctx_1024, mask_BxS2_bk0, L1_xattn_Wq, L1_xattn_Wkv, L1_xattn_Wo, L1_xattn_bo)
    x = x + jnp.tanh(g_ffn[1]) * _L1_ffn_ref(_layernorm(x, axis=-1), L1_ffn_clip_x, L1_ffn_clip_down, L1_ffn_w_gate, L1_ffn_w_up, L1_ffn_w_down)
    return x

_drawn_inputs = setup_inputs


def setup_inputs(seed=0):
    import zlib

    import numpy as np

    out = dict(_drawn_inputs(seed))
    spreads = {'g_ffn': (-1.0, 0.6),
     'L0_ffn_br': (0.0, 0.511),
     'L0_ffn_b1': (0.0, 0.8),
     'L0_ffn_b2': (0.0, 0.354),
     'L1_xattn_bo': (0.0, 0.1)}
    factors = {'L0_xattn_Wq': 8.0,
     'L0_xattn_Wk': 8.0,
     'L0_xattn_lambda_q1': 64.0,
     'L0_xattn_lambda_k1': 64.0,
     'L0_xattn_lambda_q2': 8.0,
     'L0_xattn_lambda_k2': 8.0,
     'L0_ffn_Wr': 3.36,
     'L0_ffn_W1': 3.72,
     'L0_ffn_W2': 2.937,
     'L1_xattn_Wq': 64.0,
     'L1_ffn_w_gate': 6.422,
     'L1_ffn_w_up': 5.902,
     'L1_ffn_w_down': 5.924}
    for name, (base, spread) in spreads.items():
        noise = np.random.default_rng([zlib.crc32(name.encode()), seed]).standard_normal(out[name].shape)
        drawn = base * np.exp(spread * noise) if base else spread * noise
        out[name] = jnp.asarray(drawn.astype(out[name].dtype))
    for name, factor in factors.items():
        out[name] = (out[name] * factor).astype(out[name].dtype)
    return out
```

```python
import math
from contextlib import ExitStack

import concourse.bass as bass
from concourse import mybir

F32 = mybir.dt.float32
F32R = mybir.dt.float32r
BF16 = mybir.dt.bfloat16
U8 = mybir.dt.uint8
ALU = mybir.AluOpType
ACT = mybir.ActivationFunctionType
AX = mybir.AxisListType.X

P = 128
B, N, D = 2, 512, 128
S = 77
T = B * N
NTILE = T // P
HD = D // 2
E, F = 8, 512
FT = F // P
H1, DH = 16, 64
INNER = H1 * DH
NI = INNER // P
HS = H1 * S
NB = -(-HS // P)
I = 352
IT = 3
ILAST = I - 2 * P

LAMBDA_INIT = 0.8 - 0.6 * math.exp(-0.3 * 12)
EPS = 1e-5
TOP_P = 0.8
QMAX = 127.0
MAGIC = 1.5 * 2.0 ** 23
NEG = -3.4028234663852886e38

CH_T0 = [0, 2, 5]
CH_NT = [2, 3, 3]
CAUSAL = S - N + 1
assert (N // P - 1) * P - 1 + CAUSAL <= 0, "rows before the last tile see no context token"

HG = [(0, 6), (6, 6), (12, 4)]
G3 = [(0, 3), (3, 3), (6, 2)]


def build(nc, x, ctx_in, mask, g_xattn, g_ffn, Wq0, Wk0, Wv0, Wo0, lq1, lk1, lq2, lk2,
          Wr, br, W1, b1, W2, b2, Wq1, Wkv1, Wo1, bo, clip_x, clip_down, w_gate, w_up, w_down, out):
    st = ExitStack()
    with st:
        def sb(name, shape, dt=F32):
            return st.enter_context(nc.sbuf_tensor(name, shape, dt))

        def sem(name):
            return st.enter_context(nc.semaphore(name))

        ps = st.enter_context(nc.psum_tensor("ps", [P, 8, 512], F32))
        gates_dram = nc.dram_tensor("gates_dram", (E, T), F32).ap()

        ident = sb("ident", [P, P])
        tie = sb("tie", [P, E, E])
        mhalf = sb("mhalf", [P, NTILE])
        gsc = sb("gsc", [P, 6])
        gth = sb("gth", [P, 6])
        ghalf = sb("ghalf", [P, 6])
        tgli = sb("tgli", [P, 1])
        sig127 = sb("sig127", [P, 2])
        lam_in = sb("lam_in", [P, 4, HD])
        lam_pr = sb("lam_pr", [P, 2, HD])
        lam_s = sb("lam_s", [P, 2])
        lam_e = sb("lam_e", [P, 2])
        nlam = sb("nlam", [P, 1])
        br_bc = sb("br_bc", [P, E])
        bo_bc = sb("bo_bc", [P, D])
        mask_u8 = sb("mask_u8", [P, B, S], U8)
        maskadd = sb("maskadd", [P, B, S])

        xs = sb("xs", [P, NTILE, D])
        xn = sb("xn", [P, NTILE, D])
        stats = sb("stats", [P, NTILE, 6])
        mv = sb("mv", [P, NTILE, 2])
        ve = sb("ve", [P, NTILE])
        rstd = sb("rstd", [P, NTILE])

        ctx_sb = sb("ctx_sb", [S, B, D])
        wk0_sb = sb("wk0_sb", [HD, D])
        wv0_sb = sb("wv0_sb", [P, D])
        wo0_sb = sb("wo0_sb", [P, D])
        wq0_sb = sb("wq0_sb", [P, D])
        b1_sb = sb("b1_sb", [E * FT, P])
        b2_sb = sb("b2_sb", [E, P])
        prepT = sb("prepT", [P, 410])
        wobT = sb("wobT", [P, 168])
        ctxT = prepT[:, 0:B * S]
        wkT2 = prepT[:, 154:282]
        wvT = prepT[:, 282:410]
        woT = wobT[:, 0:P]
        b1T = wobT[:, P:P + E * FT]
        b2T = wobT[:, P + E * FT:P + E * FT + E]
        kv0T = sb("kv0T", [P, 2, B * S])
        A0 = sb("A0", [P, B, 2, S])
        VV = sb("VV", [S, B, 2, D])
        xT = sb("xT", [P, T])
        nmx0 = sb("nmx0", [P, NTILE * 2])
        E0 = sb("E0", [P, NTILE, 2, S])
        se0 = sb("se0", [P, NTILE * 2])
        rc0 = sb("rc0", [P, NTILE * 2])
        Wt = sb("Wt", [P, NTILE, S])
        wT = sb("wT", [S, NTILE, P])
        sq = sb("sq", [P, 3 * D])
        ss = sb("ss", [P, NTILE])
        rms = sb("rms", [P, NTILE])

        wr_sb = sb("wr_sb", [P, E])
        xhi = sb("xhi", [P, T], F32R)
        xlo = sb("xlo", [P, T], F32R)
        lg = sb("lg", [P, NTILE, E])
        lmx = sb("lmx", [P, NTILE])
        lsum = sb("lsum", [P, NTILE])
        pr = sb("pr", [P, NTILE, E])
        dif = sb("dif", [P, NTILE, E, E])
        cum = sb("cum", [P, NTILE, E])
        lone = sb("lone", [P, NTILE, E])
        gate = sb("gate", [P, NTILE, E])
        gateT = sb("gateT", [E, T])
        G = sb("G", [P, 2, 768])
        w1raw = sb("w1raw", [P, 2, F])
        w2raw = sb("w2raw", [P, 2, FT, D])
        w1hi = sb("w1hi", [P, 2, F], F32R)
        w1lo = sb("w1lo", [P, 2, F], F32R)
        w2hi = sb("w2hi", [P, 2, FT, D], F32R)
        w2lo = sb("w2lo", [P, 2, FT, D], F32R)
        b1cur = sb("b1cur", [P, 2, FT])
        h32 = sb("h32", [P, 4, 384])
        hhi = sb("hhi", [P, 4, 384], F32R)
        hlo = sb("hlo", [P, 4, 384], F32R)
        ytmp = sb("ytmp", [P, 2, 384])
        acc = sb("acc", [P, T])

        l1w = sb("l1w", [P, 3 * INNER])
        wq1_sb = l1w[:, 0:INNER]
        wkv1_sb = l1w[:, INNER:3 * INNER]
        wo1_sb = sb("wo1_sb", [P, NI, D])
        wq1T = sb("wq1T", [P, NI, D])
        kv1T = sb("kv1T", [P, 2, NI, B * S])
        kT1, vT1 = kv1T[:, 0, :, :], kv1T[:, 1, :, :]
        A1 = sb("A1", [P, B, H1, S])
        VOT = sb("VOT", [P, B, H1 * S])
        VO = sb("VO", [P, B, NB, D])
        usum = sb("usum", [P, B])
        urow = sb("urow", [P, B, D])
        tbo = sb("tbo", [P, D])
        xn3T = xT
        SC = sb("SC", [P, H1, S])
        PR = sb("PR", [P, H1 * S])
        PT = sb("PT", [P, NB, P])
        nmx1 = sb("nmx1", [P, B, H1])
        se1 = sb("se1", [P, B, H1])
        rc1 = sb("rc1", [P, B, H1])

        wgu_raw = sb("wgu_raw", [P, 2, IT, D])
        wd_raw = sb("wd_raw", [P, I])
        wmx = sb("wmx", [P, 7])
        wsc = sb("wsc", [P, 7])
        winv = sb("winv", [P, 7])
        wqf = sb("wqf", [P, 2, IT, D])
        wdqf = sb("wdqf", [P, I])
        wguT = sb("wguT", [P, 2, IT, P], BF16)
        wdT = sb("wdT", [P, IT, D], BF16)
        sdg = sb("sdg", [P, D])
        xmx = sb("xmx", [P, 1])
        xmxa = sb("xmxa", [P, 1])
        sx = sb("sx", [P, 1])
        sxi = sb("sxi", [P, 1])
        qT = sb("qT", [P, T], BF16)
        gsx = sb("gsx", [P, 3])
        gsx2 = sb("gsx2", [P, 3])
        hsc = sb("hsc", [P, 3])
        th = sb("th", [P, 2, 512])
        hq = l1w[:].rearrange("p (i t) -> p i t", i=IT)
        hmx = sb("hmx", [P, IT * 2])
        hmxr = sb("hmxr", [P, 1])
        hmxa = sb("hmxa", [P, 1])
        sh = sb("sh", [P, 1])
        shi = sb("shi", [P, 1])
        hqb = kv1T[:].rearrange("p a i b -> p (a i b)")[:, 0:IT * T // 2].bitcast(BF16).rearrange(
            "p (i t) -> p i t", i=IT)
        otmp = xT[:].rearrange("p (t d) -> p t d", d=D)

        names = """acc_zero x_loaded0 x_loaded1 x_loaded2 early_loaded smalls_loaded bias_loaded l1w_loaded ffnw_loaded
            router_loaded pool_const mask_ready pad_ready gates_ready dve_step
            small_pe prep_evac_a prep_evac_d kv0_ready kv0_evac a0_ready a0_evac_a a0_evac_d vv_evac
            ve_ready rstd_ready xn_ready xt_ready xt_evac sc0_ready nmx0_ready exp0_ready w_ready wt_ready wt_evac
            pv_ready sq_ready ms_ready rms_ready x1_ready x2t_ready xhi_ready xlo_ready
            logit_ready lgsub_ready lgexp_ready gate_ready gt_ready gt_evac gt_stored
            prep_ready pevac_a pevac_d
            acct_ready x2_ready
            wmx_ready wqf_ready wq_ready wq_evac sd_ready sd_evac u_ready usum_ready u_evac
            sc1_ready nmx1_ready exp1_ready pr_ready pt_ready pt_evac_a pt_evac_d pv1_ready x3_ready
            xmx_ready xmxa_ready sx_ready qf_ready qt_ready q_ready gu_ready th_ready h_ready hmx_ready hmxa_ready
            shi_ready hqf_ready hqb_ready dn_ready out_ready out_stored pool_step""".split()
        s = {n: sem(n) for n in names}
        pass_names = "wraw_loaded0 wraw_loaded1 whi_ready w1_split w2_split g_loaded0 g_loaded1 up_done h32_ready hi_ready b1_ready lo_dve lo_pool down_done y_mul y_done".split()
        sp_ = [{n: sem(f"p{k}_{n}") for n in pass_names} for k in range(2)]

        PASS_CH = [[0], [1, 2]]
        SETS = [4, 2]
        LAG = [3, 2]
        POOL_LO = [[], [(1, 1), (3, 1)]]

        def tok(c):
            return CH_T0[c] * P, CH_NT[c] * P

        def lo_count(k, e, ft, ci):
            order = [(f, c) for f in range(FT) for c in range(len(PASS_CH[k]))]
            pool = (ft, ci) in POOL_LO[k]
            mine = [u for u in order if (u in POOL_LO[k]) == pool]
            return sp_[k]["lo_pool" if pool else "lo_dve"], len(mine) * e + mine.index((ft, ci)) + 1

        def h_slot(k, ft, ci):
            return (ft % SETS[k]) * len(PASS_CH[k]) + ci

        def up_bank(k, ft, ci):
            return h_slot(k, ft, ci)

        def y_bank(k, slot, ci):
            return 4 + slot * len(PASS_CH[k]) + ci

        def earlier(e, ft, back):
            m = ft - back
            return e + m // FT, m % FT, not (isinstance(e, int) and FT * e + m < 0)

        PVB = [(6, 7), (3, 4), (5, 0)]
        X2B = [0, 1, 2]
        SCB = [1, 2, 3]
        GUB = 2
        PREP_BANKS = [6, 7]
        PREP = ([("wqT", 0, 4, 0), ("wqT", 4, 4, 0)] + [("kT", a, n, 0) for a, n in G3]
                + [("vT", a, n, 0) for a, n in G3] + [("A", a, n, par) for par in range(2) for a, n in G3]
                + [("VOT", a, n, par) for par in range(2) for a, n in G3]
                + [("VO", a, n, b) for b in range(B) for a, n in ((0, 4), (4, 4), (8, 1), (9, 1))])
        PREP_A0 = [k[0] for k in PREP].index("A")
        PREP_V0 = [k[0] for k in PREP].index("VOT")
        PREP_B0 = [k[0] for k in PREP].index("VO")
        s["dve_sc1"] = sem("dve_sc1")

        def prep_evacs(eng, mine):
            def copy(dst, src, scale=1.0):
                if mine == 0:
                    return eng.activation(dst, src, ACT.Copy, scale=scale)
                if scale != 1.0:
                    return eng.tensor_scalar(dst, src, scale, None, ALU.mult)
                return eng.tensor_copy(dst, src)

            for u, (kind, n0, cnt, par) in enumerate(PREP):
                if u % 2 != mine:
                    continue
                bank = PREP_BANKS[u % 2]
                eng.wait_ge(s["prep_ready"], u + 1)
                if kind == "wqT":
                    last = copy(wq1T[:, n0:n0 + cnt, :].rearrange("p i d -> p (i d)"), ps[:, bank, 0:cnt * P])
                elif kind in ("kT", "vT"):
                    dst = (kT1 if kind == "kT" else vT1)[:, n0:n0 + cnt, :]
                    last = copy(dst.rearrange("p i d -> p (i d)"), ps[:, bank, 0:cnt * B * S])
                elif kind in ("A", "VOT"):
                    src = ps[:, bank, 0:cnt * B * S].rearrange("p (i b s) -> p i b s", b=B, s=S)
                    dst = A1[:] if kind == "A" else VOT[:].rearrange("p b (h s) -> p b h s", s=S)
                    dst = dst.rearrange("p b (i two) s -> p i two b s", two=2)[:, n0:n0 + cnt, par, :, :]
                    last = copy(dst, src, DH ** -0.5 if kind == "A" else 1.0)
                else:
                    w = min(P, HS - n0 * P)
                    last = copy(VO[0:w, par, n0:n0 + cnt, :].rearrange("p j d -> p (j d)"), ps[0:w, bank, 0:cnt * P])
                last.then_inc(s["pevac_a" if mine == 0 else "pevac_d"], 1)

        block = st.enter_context(nc.Block())

        @block.sync
        def _(eng):
            xv = x.rearrange("b (t p) d -> p b t d", p=P)
            eng.dma_start(xs[:, 0:2, :], xv[:, :, 3, :]).then_inc(s["x_loaded0"], 16)
            eng.dma_start(xs[:, 2:5, :], xv[:, 0, 0:3, :]).then_inc(s["x_loaded1"], 16)
            eng.dma_start(xs[:, 5:8, :], xv[:, 1, 0:3, :]).then_inc(s["x_loaded2"], 16)

            def load_expert(k, e, slot):
                if not isinstance(e, int) or e >= 2:
                    eng.wait_ge(sp_[k]["w2_split"], e - 1)
                eng.dma_start(w1raw[:, slot, :], W1[bass.ds(e, 1), :, :].rearrange("a p f -> p (a f)")).then_inc(
                    sp_[k][f"wraw_loaded{slot}"], 16)
                eng.dma_start(w2raw[:, slot, :, :],
                              W2[bass.ds(e, 1), :, :].rearrange("a (t p) d -> p (a t) d", p=P)).then_inc(
                    sp_[k][f"wraw_loaded{slot}"], 16)

            def load_gates(k, e, slot):
                t0, w = tok(PASS_CH[k][0])[0], sum(tok(c)[1] for c in PASS_CH[k])
                if not isinstance(e, int) or e >= 2:
                    eng.wait_ge(sp_[k]["y_mul"], len(PASS_CH[k]) * (e - 1))
                eng.dma_start(G[:, slot, 0:w],
                              gates_dram[bass.ds(e, 1), t0:t0 + w].broadcast_to([P, w])).then_inc(
                    sp_[k][f"g_loaded{slot}"], 16)

            load_expert(0, 0, 0)
            eng.dma_start(wr_sb[:], Wr).then_inc(s["router_loaded"], 16)
            load_expert(0, 1, 1)
            eng.dma_start(wq1_sb[:], Wq1).then_inc(s["l1w_loaded"], 16)
            eng.dma_start(wkv1_sb[:], Wkv1).then_inc(s["l1w_loaded"], 16)
            eng.dma_start(wo1_sb[:], Wo1.rearrange("(i p) d -> p i d", p=P)).then_inc(s["l1w_loaded"], 16)
            for n, w in enumerate((w_gate, w_up)):
                eng.dma_start(wgu_raw[:, n, 0:2, :], w[0:2 * P, :].rearrange("(t p) d -> p t d", p=P)).then_inc(
                    s["ffnw_loaded"], 16)
                eng.dma_start(wgu_raw[0:ILAST, n, 2, :], w[2 * P:I, :]).then_inc(s["ffnw_loaded"], 16)
            eng.dma_start(wd_raw[:], w_down).then_inc(s["ffnw_loaded"], 16)

            eng.wait_ge(s["gt_evac"], 2)
            eng.dma_start(gates_dram, gateT[:]).then_inc(s["gt_stored"], 16)
            eng.wait_ge(s["gt_stored"], 16)
            for k in range(2):
                if k == 1:
                    eng.wait_ge(sp_[0]["w2_split"], E)
                    eng.wait_ge(sp_[0]["y_mul"], E)
                    load_expert(1, 0, 0)
                    load_expert(1, 1, 1)
                load_gates(k, 0, 0)
                load_gates(k, 1, 1)
                with eng.Fori(2, E - 1, 2) as e:
                    for slot in range(2):
                        load_expert(k, e + slot, slot)
                        load_gates(k, e + slot, slot)

            ov = out.rearrange("b (t p) d -> p b t d", p=P)
            for n, (dst, src) in enumerate(((ov[:, :, 3, :], xs[:, 0:2, :]), (ov[:, 0, 0:3, :], xs[:, 2:5, :]),
                                            (ov[:, 1, 0:3, :], xs[:, 5:8, :]))):
                eng.wait_ge(s["out_ready"], 1 if n == 0 else 2)
                eng.dma_start(dst, src).then_inc(s["out_stored"], 16)
            eng.wait_ge(s["out_stored"], 48)

        @block.gpsimd
        def _(eng):
            steps = [0]

            def step(ins):
                steps[0] += 1
                ins.then_inc(s["pool_step"], 1)
                eng.wait_ge(s["pool_step"], steps[0])

            step(eng.memset(ident[:], 0.0))
            eng.affine_select(out=ident[:], in_=ident[:], compare_op=ALU.not_equal, fill=1.0, base=0,
                              pattern=[[-1, P]], channel_multiplier=1).then_inc(s["pool_const"], 1)
            for src, dst in ((g_xattn, gsc[:, 0:2]), (g_ffn, gsc[:, 2:4]), (clip_x, gsc[:, 4:5]),
                             (clip_down, gsc[:, 5:6]), (br, br_bc[:]), (bo, bo_bc[:]),
                             (lq1, lam_in[:, 0, :]), (lq2, lam_in[:, 1, :]), (lk1, lam_in[:, 2, :]),
                             (lk2, lam_in[:, 3, :]), (mask.rearrange("b s -> (b s)"), mask_u8[:].rearrange("p b s -> p (b s)"))):
                eng.dma_start(dst, src.partition_broadcast(P)).then_inc(s["smalls_loaded"], 16)
            eng.memset(mhalf[:], -0.5).then_inc(s["pool_const"], 1)
            eng.memset(acc[:], 0.0).then_inc(s["acc_zero"], 1)
            step(eng.memset(tie[:], -1e-37))
            eng.affine_select(out=tie[:], in_=tie[:], compare_op=ALU.is_ge, fill=0.0, base=0,
                              pattern=[[1, E], [-1, E]], channel_multiplier=0).then_inc(s["pool_const"], 1)

            def inv_root(c, src, dst, ready, done):
                t0, nt = CH_T0[c], CH_NT[c]
                eng.wait_ge(*ready)
                eng.tensor_tensor(dst[:, t0:t0 + nt], src[:, t0:t0 + nt], mhalf[:, t0:t0 + nt], ALU.pow).then_inc(done, 1)

            step(eng.memset(mhalf[:, 0:1], -0.5))
            for c in range(3):
                inv_root(c, ve, rstd, (s["ve_ready"], c + 1), s["rstd_ready"])
            eng.wait_ge(s["rstd_ready"], 3)
            eng.memset(wgu_raw[ILAST:P, :, 2, :], 1.0).then_inc(s["pad_ready"], 1)
            eng.wait_ge(s["pad_ready"], 1)

            eng.wait_ge(s["smalls_loaded"], 16 * 11)
            step(eng.tensor_scalar(maskadd[:], mask_u8[:], -1.0, -NEG, ALU.add, ALU.mult))
            eng.affine_select(out=maskadd[:], in_=maskadd[:], compare_op=ALU.is_ge, fill=NEG,
                              base=(N // P - 1) * P + CAUSAL - 1, pattern=[[0, B], [-1, S]],
                              channel_multiplier=1).then_inc(s["mask_ready"], 1)
            for c in range(3):
                t0, nt = CH_T0[c], CH_NT[c]
                eng.wait_ge(s["sq_ready"], c + 1)
                step(eng.tensor_scalar(ve[:, t0:t0 + nt], ss[:, t0:t0 + nt], 1.0 / D, EPS, ALU.mult, ALU.add))
                eng.tensor_tensor(rms[:, t0:t0 + nt], ve[:, t0:t0 + nt], mhalf[:, t0:t0 + nt], ALU.pow).then_inc(
                    s["rms_ready"], 1)
            for c in range(3):
                inv_root(c, ve, rstd, (s["ve_ready"], 3 + c + 1), s["rstd_ready"])

            def split_low(k, e, slot):
                eng.wait_ge(sp_[k]["whi_ready"], 2 * e + 1)
                if not isinstance(e, int) or e >= 2:
                    eng.wait_ge(sp_[k]["up_done"], len(PASS_CH[k]) * FT * (e - 1))
                eng.tensor_tensor(w1lo[:, slot, :], w1raw[:, slot, :], w1hi[:, slot, :].bitcast(F32),
                                  ALU.subtract).then_inc(sp_[k]["w1_split"], 1)
                eng.wait_ge(sp_[k]["whi_ready"], 2 * e + 2)
                if not isinstance(e, int) or e >= 2:
                    eng.wait_ge(sp_[k]["down_done"], len(PASS_CH[k]) * FT * (e - 1))
                eng.tensor_tensor(w2lo[:, slot, :, :], w2raw[:, slot, :, :], w2hi[:, slot, :, :].bitcast(F32),
                                  ALU.subtract).then_inc(sp_[k]["w2_split"], 1)

            def expert(k, e, slot):
                nch = len(PASS_CH[k])
                for ft in range(FT):
                    if ft == 2:
                        if isinstance(e, int):
                            if e + 1 < E and e >= 1:
                                split_low(k, e + 1, 1 - slot)
                        else:
                            split_low(k, e + 1, 1 - slot)
                    for ci in range(nch):
                        if (ft, ci) in POOL_LO[k]:
                            w = tok(PASS_CH[k][ci])[1]
                            hs = h_slot(k, ft, ci)
                            eng.wait_ge(sp_[k]["hi_ready"], nch * (FT * e + ft) + ci + 1)
                            eng.tensor_tensor(hlo[:, hs, 0:w], h32[:, hs, 0:w], hhi[:, hs, 0:w].bitcast(F32),
                                              ALU.subtract).then_inc(lo_count(k, 0, ft, ci)[0], 1)

            for k in range(2):
                if k == 1:
                    eng.wait_ge(sp_[0]["up_done"], FT * E)
                    eng.wait_ge(sp_[0]["down_done"], FT * E)
                split_low(k, 0, 0)
                split_low(k, 1, 1)
                expert(k, 0, 0)
                expert(k, 1, 1)
                with eng.Fori(2, E - 3, 2) as e:
                    for slot in range(2):
                        expert(k, e + slot, slot)
                expert(k, E - 2, 0)
                expert(k, E - 1, 1)
                for c in PASS_CH[k]:
                    if k == 0:
                        inv_root(c, ve, rstd, (s["ve_ready"], 7), s["rstd_ready"])

            for n, c in enumerate((1, 2, 0)):
                inv_root(c, ve, rstd, (s["ve_ready"], 8 + n), s["rstd_ready"])

            eng.wait_ge(s["wmx_ready"], 1)
            for n in range(2):
                for t in range(IT):
                    c = n * IT + t
                    eng.tensor_scalar(wqf[:, n, t, :], wgu_raw[:, n, t, :], winv[:, c:c + 1], MAGIC, ALU.mult, ALU.add)
            eng.tensor_scalar(wdqf[:], wd_raw[:], winv[:, 6:7], MAGIC, ALU.mult, ALU.add).then_inc(s["wqf_ready"], 1)

            RMAX = bass.bass_isa.ReduceOp.absmax
            eng.wait_ge(s["xmx_ready"], 1)
            eng.partition_all_reduce(xmxa[:], xmx[:], P, RMAX).then_inc(s["xmxa_ready"], 1)
            eng.wait_ge(s["hmx_ready"], 1)
            eng.partition_all_reduce(hmxa[:], hmxr[:], P, RMAX).then_inc(s["hmxa_ready"], 1)

        @block.scalar
        def _(eng):
            eng.dma_start(ctx_sb[:], ctx_in.rearrange("b s d -> s b d")).then_inc(s["early_loaded"], 16)
            eng.dma_start(wk0_sb[:], Wk0).then_inc(s["early_loaded"], 16)
            eng.dma_start(wv0_sb[:], Wv0).then_inc(s["early_loaded"], 16)
            eng.dma_start(wo0_sb[:], Wo0).then_inc(s["early_loaded"], 16)
            eng.dma_start(wq0_sb[:], Wq0).then_inc(s["early_loaded"], 16)
            eng.dma_start(b1_sb[:], b1.rearrange("e (t p) -> (e t) p", p=P)).then_inc(s["early_loaded"], 16)
            eng.dma_start(b2_sb[:], b2).then_inc(s["early_loaded"], 16)

            eng.wait_ge(s["small_pe"], 1)
            eng.activation(prepT[:], ps[:, 6, 0:410], ACT.Copy).then_inc(s["prep_evac_a"], 1)
            eng.wait_ge(s["kv0_ready"], 1)
            eng.activation(kv0T[:].rearrange("p a b -> p (a b)"), ps[:, 5, 0:2 * B * S], ACT.Copy).then_inc(s["kv0_evac"], 1)

            eng.wait_ge(s["smalls_loaded"], 16 * 11)
            eng.activation(gth[:, 0:4], gsc[:, 0:4], ACT.Tanh)
            eng.activation(gth[:, 4:6], gsc[:, 4:6], ACT.Tanh, scale=0.5).then_inc(s["mask_ready"], 1)
            eng.wait_ge(s["usum_ready"], 1)
            eng.activation(lam_e[:], lam_s[:], ACT.Exp).then_inc(s["lgsub_ready"], 1)

            eng.wait_ge(s["a0_ready"], 1)
            eng.activation(A0[:, :, 0, :], ps[:, 6, 0:B * S].rearrange("p (b s) -> p b s", b=B), ACT.Copy,
                           scale=HD ** -0.5).then_inc(s["a0_evac_a"], 1)
            vvp = ps[0:S, 4, :].rearrange("p (b a d) -> p b a d", b=B, a=2)
            eng.activation(VV[:, :, 0, :], vvp[:, :, 0, :], ACT.Copy)
            eng.wait_ge(s["lgexp_ready"], 1)
            eng.activation(VV[:, :, 1, :], vvp[:, :, 1, :], ACT.Copy, scale=tgli[0:S, :]).then_inc(s["vv_evac"], 1)

            def xt_evac(c):
                t0, w = tok(c)
                eng.wait_ge(s["xt_ready"], c + 1)
                eng.activation(xT[:, t0:t0 + w], ps[:, c, 0:w], ACT.Copy).then_inc(s["xt_evac"], 1)

            def exps(c):
                eng.wait_ge(s["nmx0_ready"], c + 1)
                for j in range(CH_NT[c]):
                    for h in range(2):
                        i = 2 * (CH_T0[c] + j) + h
                        last = eng.activation(E0[:, CH_T0[c] + j, h, :], ps[:, 3 + c, (2 * j + h) * S:(2 * j + h + 1) * S],
                                              ACT.Exp, bias=nmx0[:, i:i + 1], accum_out=se0[:, i:i + 1])
                last.then_inc(s["exp0_ready"], 1)

            def wt_evac(c):
                t0, nt = CH_T0[c], CH_NT[c]
                eng.wait_ge(s["wt_ready"], c + 1)
                eng.activation(wT[:, t0:t0 + nt, :].rearrange("p t d -> p (t d)"), ps[0:S, c, 0:nt * P],
                               ACT.Copy).then_inc(s["wt_evac"], 1)

            def squares(c):
                eng.wait_ge(s["pv_ready"], c + 1)
                for j in range(CH_NT[c]):
                    last = eng.activation(sq[:, j * D:(j + 1) * D], ps[:, PVB[c][0], j * D:(j + 1) * D], ACT.Square,
                                          accum_out=ss[:, CH_T0[c] + j:CH_T0[c] + j + 1])
                last.then_inc(s["sq_ready"], 1)

            for c in range(3):
                xt_evac(c)
            exps(0)
            exps(1)
            wt_evac(0)
            exps(2)
            wt_evac(1)
            squares(0)
            wt_evac(2)
            eng.wait_ge(s["sq_ready"], 1)
            squares(1)
            eng.wait_ge(s["sq_ready"], 2)
            squares(2)

            def split_high(k, e, slot):
                eng.wait_ge(sp_[k][f"wraw_loaded{slot}"], 16 * (e - slot) + 32)
                if not isinstance(e, int) or e >= 2:
                    eng.wait_ge(sp_[k]["up_done"], len(PASS_CH[k]) * FT * (e - 1))
                eng.activation(w1hi[:, slot, :], w1raw[:, slot, :], ACT.Copy).then_inc(sp_[k]["whi_ready"], 1)
                if not isinstance(e, int) or e >= 2:
                    eng.wait_ge(sp_[k]["down_done"], len(PASS_CH[k]) * FT * (e - 1))
                eng.activation(w2hi[:, slot, :, :].rearrange("p t d -> p (t d)"),
                               w2raw[:, slot, :, :].rearrange("p t d -> p (t d)"), ACT.Copy).then_inc(sp_[k]["whi_ready"], 1)

            split_high(0, 0, 0)
            split_high(0, 1, 1)

            prep_evacs(eng, 0)

            for c in range(3):
                t0, w = tok(c)
                eng.wait_ge(s["x2t_ready"], c + 1)
                eng.activation(xhi[:, t0:t0 + w], ps[:, X2B[c], 0:w], ACT.Copy).then_inc(s["xhi_ready"], 1)
            eng.wait_ge(s["lgsub_ready"], 2)
            eng.activation(pr[:], lg[:], ACT.Exp).then_inc(s["lgexp_ready"], 1)
            for i in range(2):
                eng.wait_ge(s["gt_ready"], i + 1)
                eng.activation(gateT[:, i * 512:(i + 1) * 512], ps[0:E, 4 + i, :], ACT.Copy).then_inc(s["gt_evac"], 1)

            def expert(k, e, slot):
                nch = len(PASS_CH[k])
                eng.wait_ge(sp_[k]["b1_ready"], e + 1)
                for ft in range(FT):
                    for ci in range(nch):
                        w = tok(PASS_CH[k][ci])[1]
                        hs = h_slot(k, ft, ci)
                        eng.wait_ge(sp_[k]["up_done"], nch * (FT * e + ft) + ci + 1)
                        e0, f0, there = earlier(e, ft, SETS[k])
                        if there:
                            eng.wait_ge(*lo_count(k, e0, f0, ci))
                        eng.activation(h32[:, hs, 0:w], ps[:, up_bank(k, ft, ci), 0:w], ACT.Relu,
                                       bias=b1cur[:, slot, ft:ft + 1]).then_inc(sp_[k]["h32_ready"], 1)
                    if ft == 2:
                        if isinstance(e, int):
                            if e + 1 < E and e >= 1:
                                split_high(k, e + 1, 1 - slot)
                        else:
                            split_high(k, e + 1, 1 - slot)

            for k in range(2):
                if k == 1:
                    eng.wait_ge(sp_[0]["down_done"], FT * E)
                    split_high(1, 0, 0)
                    split_high(1, 1, 1)
                expert(k, 0, 0)
                expert(k, 1, 1)
                with eng.Fori(2, E - 3, 2) as e:
                    for slot in range(2):
                        expert(k, e + slot, slot)
                expert(k, E - 2, 0)
                expert(k, E - 1, 1)

            eng.wait_ge(s["xt_ready"], 4)
            eng.activation(xT[:, 0:2 * P], ps[:, 0, 0:2 * P], ACT.Copy).then_inc(s["xt_evac"], 1)
            eng.wait_ge(s["u_ready"], 1)
            for b in range(B):
                last = eng.activation(urow[:, b, :], ps[:, 7, b * P:(b + 1) * P], ACT.Copy, scale=gth[:, 1:2])
            last.then_inc(s["u_evac"], 1)
            for b in range(B):
                eng.wait_ge(s["nmx1_ready"], b + 1)
                if b == 1:
                    eng.wait_ge(s["pt_ready"], 1)
                for h in range(H1):
                    last = eng.activation(PR[:, h * S:(h + 1) * S], SC[:, h, :], ACT.Exp, bias=nmx1[:, b, h:h + 1],
                                          accum_out=se1[:, b, h:h + 1])
                last.then_inc(s["exp1_ready"], 1)
                eng.wait_ge(s["pt_ready"], b + 1)
                eng.activation(PT[:, 0:4, :].rearrange("p j d -> p (j d)"), ps[:, 4, :], ACT.Copy)
                eng.activation(PT[:, 8:NB, :].rearrange("p j d -> p (j d)"), ps[:, 6, 0:256], ACT.Copy).then_inc(
                    s["pt_evac_a"], 1)

            eng.wait_ge(s["wq_ready"], 1)
            for n in range(2):
                eng.activation(wguT[:, n, :, :].rearrange("p t d -> p (t d)"), ps[:, n, 0:IT * P], ACT.Copy, bias=-MAGIC)
            eng.activation(wdT[:, 0:2, :].rearrange("p t d -> p (t d)"), ps[:, 2, 0:2 * P], ACT.Copy, bias=-MAGIC)
            eng.activation(wdT[0:ILAST, 2, :], ps[0:ILAST, 2, 2 * P:3 * P], ACT.Copy, bias=-MAGIC).then_inc(s["wq_evac"], 1)
            eng.wait_ge(s["sd_ready"], 1)
            eng.activation(sdg[:], ps[:, 3, 0:D], ACT.Copy, scale=gth[:, 3:4]).then_inc(s["sd_evac"], 1)
            for u in range(2 * IT):
                half, it = divmod(u, IT)
                rows = P if it < 2 else ILAST
                eng.wait_ge(s["gu_ready"], u + 1)
                if u >= 2:
                    eng.wait_ge(s["h_ready"], u - 1)
                eng.activation(th[0:rows, u % 2, :], ps[0:rows, 2 * (u % 3) + GUB, :], ACT.Tanh,
                               scale=gsx[0:rows, it:it + 1]).then_inc(s["th_ready"], 1)

        @block.tensor
        def _(eng):
            def tr(dst, src, n=P):
                return eng.transpose(dst, src, ident[0:n, 0:n])

            def mm(dst, lhsT, rhs, start=True, stop=True, **kw):
                return eng.matmul(dst, lhsT, rhs, start=start, stop=stop, **kw)

            eng.wait_ge(s["pool_const"], 1)
            eng.wait_ge(s["early_loaded"], 16 * 7)
            tr(ps[:, 6, 0:S], ctx_sb[:, 0, :], S)
            tr(ps[:, 6, S:2 * S], ctx_sb[:, 1, :], S)
            tr(ps[:, 6, 154:218], wk0_sb[:], HD)
            tr(ps[:, 6, 218:282], wk0_sb[:], HD)
            tr(ps[:, 6, 282:410], wv0_sb[:])
            tr(ps[:, 7, 0:P], wo0_sb[:])
            tr(ps[:, 7, P:P + E * FT], b1_sb[:], E * FT)
            tr(ps[:, 7, P + E * FT:P + E * FT + E], b2_sb[:], E).then_inc(s["small_pe"], 1)
            eng.wait_ge(s["prep_evac_a"], 1)
            mm(ps[:, 5, 0:B * S], wkT2, ctxT)
            mm(ps[:, 5, B * S:2 * B * S], wvT, ctxT).then_inc(s["kv0_ready"], 1)
            for b in range(B):
                mm(ps[0:S, 4, b * 256:b * 256 + P], ctxT[:, b * S:(b + 1) * S], wvT)
            eng.wait_ge(s["kv0_evac"], 1)
            eng.wait_ge(s["prep_evac_d"], 1)
            for h in range(2):
                mm(ps[:, 6 + h, 0:B * S], wq0_sb[h * HD:(h + 1) * HD, :], kv0T[h * HD:(h + 1) * HD, 0, :])
            for b in range(B):
                last = mm(ps[0:S, 4, b * 256 + P:b * 256 + 2 * P], kv0T[:, 1, b * S:(b + 1) * S], woT)
            last.then_inc(s["a0_ready"], 1)

            def transposes(c, bank, n):
                eng.wait_ge(s["xn_ready"], n)
                for j in range(CH_NT[c]):
                    last = tr(ps[:, bank, j * P:(j + 1) * P], xn[:, CH_T0[c] + j, :])
                return last

            def batch(c, j):
                return j if c == 0 else c - 1

            for c in range(3):
                transposes(c, c, c + 1).then_inc(s["xt_ready"], 1)
            eng.wait_ge(s["a0_evac_a"], 1)
            eng.wait_ge(s["a0_evac_d"], 1)
            eng.wait_ge(s["vv_evac"], 1)
            for c in range(3):
                eng.wait_ge(s["xt_evac"], c + 1)
                for j in range(CH_NT[c]):
                    t = CH_T0[c] + j
                    last = mm(ps[:, 3 + c, j * 2 * S:(j + 1) * 2 * S], xT[:, t * P:(t + 1) * P],
                              A0[:, batch(c, j), :, :].rearrange("p h s -> p (h s)"))
                last.then_inc(s["sc0_ready"], 1)
            for c in range(3):
                eng.wait_ge(s["w_ready"], c + 1)
                for j in range(CH_NT[c]):
                    last = tr(ps[0:S, c, j * P:(j + 1) * P], Wt[:, CH_T0[c] + j, :])
                last.then_inc(s["wt_ready"], 1)
                eng.wait_ge(s["wt_evac"], c + 1)
                for a in range(2):
                    for j in range(CH_NT[c]):
                        last = mm(ps[:, PVB[c][a], j * P:(j + 1) * P], wT[:, CH_T0[c] + j, :], VV[:, batch(c, j), a, :])
                last.then_inc(s["pv_ready"], 1)

            eng.wait_ge(s["l1w_loaded"], 48)
            eng.wait_ge(s["x1_ready"], 3)
            u = 0
            for kind, n0, cnt, par in PREP:
                bank = PREP_BANKS[u % 2]
                if u >= 2:
                    eng.wait_ge(s["pevac_a" if u % 2 == 0 else "pevac_d"], (u - 2) // 2 + 1)
                if u == PREP_A0:
                    eng.wait_ge(s["pevac_a"], (PREP_A0 + 1) // 2)
                    eng.wait_ge(s["pevac_d"], PREP_A0 // 2)
                if u == PREP_V0:
                    eng.wait_ge(s["pevac_a"], (PREP_V0 + 1) // 2)
                    eng.wait_ge(s["pevac_d"], PREP_V0 // 2)
                if u == PREP_B0:
                    eng.wait_ge(s["pevac_a"], (PREP_B0 + 1) // 2)
                    eng.wait_ge(s["pevac_d"], PREP_B0 // 2)
                for m in range(cnt):
                    i = n0 + m
                    if kind == "wqT":
                        last = tr(ps[:, bank, m * P:(m + 1) * P], wq1_sb[:, i * P:(i + 1) * P])
                    elif kind in ("kT", "vT"):
                        o = (INNER if kind == "vT" else 0) + i * P
                        last = mm(ps[:, bank, m * B * S:(m + 1) * B * S], wkv1_sb[:, o:o + P], ctxT)
                    elif kind == "A":
                        last = mm(ps[:, bank, m * B * S:(m + 1) * B * S], wq1T[par * DH:(par + 1) * DH, i, :],
                                  kT1[par * DH:(par + 1) * DH, i, :])
                    elif kind == "VOT":
                        last = mm(ps[:, bank, m * B * S:(m + 1) * B * S], wo1_sb[par * DH:(par + 1) * DH, i, :],
                                  vT1[par * DH:(par + 1) * DH, i, :])
                    else:
                        w = min(P, HS - i * P)
                        last = tr(ps[0:w, bank, m * P:(m + 1) * P], VOT[:, par, i * P:i * P + w])
                last.then_inc(s["prep_ready"], 1)
                u += 1

            for c in range(3):
                transposes(c, X2B[c], 3 + c + 1).then_inc(s["x2t_ready"], 1)
            eng.wait_ge(s["router_loaded"], 16)
            for c in range(3):
                eng.wait_ge(s["xlo_ready"], c + 1)
                for j in range(CH_NT[c]):
                    t = CH_T0[c] + j
                    last = mm(ps[:, 3, t * E:(t + 1) * E], xT[:, t * P:(t + 1) * P], wr_sb[:])
            last.then_inc(s["logit_ready"], 1)
            eng.wait_ge(s["gate_ready"], 1)
            for t in range(NTILE):
                last = tr(ps[0:E, 4 + t // 4, (t % 4) * P:(t % 4 + 1) * P], gate[:, t, :])
                if t % 4 == 3:
                    last.then_inc(s["gt_ready"], 1)
            eng.wait_ge(s["gt_evac"], 2)

            def up(k, e, ft, slot):
                nch = len(PASS_CH[k])
                if ft == 0:
                    eng.wait_ge(sp_[k]["w1_split"], e + 1)
                e0, f0, there = earlier(e, ft, SETS[k])
                if there:
                    eng.wait_ge(sp_[k]["h32_ready"], nch * (FT * e0 + f0 + 1))
                wh, wl = w1hi[:, slot, ft * P:(ft + 1) * P], w1lo[:, slot, ft * P:(ft + 1) * P]
                for ci in range(nch):
                    t0, w = tok(PASS_CH[k][ci])
                    dst = ps[:, up_bank(k, ft, ci), 0:w]
                    mm(dst, wh, xhi[:, t0:t0 + w], True, False)
                    mm(dst, wh, xlo[:, t0:t0 + w], False, False)
                    mm(dst, wl, xhi[:, t0:t0 + w], False, True).then_inc(sp_[k]["up_done"], 1)

            def down(k, e, ft, slot):
                nch = len(PASS_CH[k])
                if ft == 0:
                    eng.wait_ge(sp_[k]["w2_split"], e + 1)
                    if not isinstance(e, int) or e >= 2:
                        eng.wait_ge(sp_[k]["y_mul"], nch * (e - 1))
                wh, wl = w2hi[:, slot, ft, :], w2lo[:, slot, ft, :]
                for ci in range(nch):
                    w = tok(PASS_CH[k][ci])[1]
                    hs = h_slot(k, ft, ci)
                    dst = ps[:, y_bank(k, slot, ci), 0:w]
                    eng.wait_ge(*lo_count(k, e, ft, ci))
                    mm(dst, wh, hhi[:, hs, 0:w], ft == 0, False)
                    mm(dst, wh, hlo[:, hs, 0:w], False, False)
                    mm(dst, wl, hhi[:, hs, 0:w], False, ft == FT - 1).then_inc(sp_[k]["down_done"], 1)

            def expert(k, e, slot):
                for ft in range(FT):
                    up(k, e, ft, slot)
                    e0, f0, there = earlier(e, ft, LAG[k])
                    if there:
                        down(k, e0, f0, slot if ft >= LAG[k] else 1 - slot)

            for k in range(2):
                expert(k, 0, 0)
                expert(k, 1, 1)
                with eng.Fori(2, E - 1, 2) as e:
                    for slot in range(2):
                        expert(k, e + slot, slot)
                for back in range(LAG[k], 0, -1):
                    down(k, E - 1, FT - back, 1)
                if k == 0:
                    eng.wait_ge(sp_[0]["y_done"], E)
                    for t in range(2):
                        last = tr(ps[:, 6, t * P:(t + 1) * P], acc[:, t * P:(t + 1) * P])
                    last.then_inc(s["acct_ready"], 1)
                else:
                    eng.wait_ge(sp_[1]["y_done"], 2 * E)
                    for c in (1, 2):
                        for j in range(3):
                            t = CH_T0[c] + j
                            last = tr(ps[:, c, j * P:(j + 1) * P], acc[:, t * P:(t + 1) * P])
                        last.then_inc(s["acct_ready"], 1)

            eng.wait_ge(s["usum_ready"], 2)
            for b in range(B):
                last = mm(ps[:, 7, b * P:(b + 1) * P], usum[:, b:b + 1].broadcast_to([P, P]), ident[:])
            last.then_inc(s["u_ready"], 1)
            transposes(0, 0, 7).then_inc(s["xt_ready"], 1)
            eng.wait_ge(s["xt_evac"], 4)
            eng.wait_ge(s["x2_ready"], 2)
            for b in range(B):
                for gi, (h0, nh) in enumerate(HG):
                    if b == 1:
                        eng.wait_ge(s["dve_sc1"], gi + 1)
                    mm(ps[:, 3 * 0 + SCB[gi], 0:nh * S], xT[:, b * P:(b + 1) * P],
                       A1[:, b, h0:h0 + nh, :].rearrange("p h s -> p (h s)")).then_inc(s["sc1_ready"], 1)
            for b in range(B):
                eng.wait_ge(s["pr_ready"], b + 1)
                if b == 1:
                    eng.wait_ge(s["pt_evac_a"], 1)
                    eng.wait_ge(s["pt_evac_d"], 1)
                for j in range(NB):
                    w = min(P, HS - j * P)
                    last = tr(ps[0:w, 4 + j // 4, (j % 4) * P:(j % 4 + 1) * P], PR[:, j * P:j * P + w])
                last.then_inc(s["pt_ready"], 1)
                eng.wait_ge(s["pt_evac_a"], b + 1)
                eng.wait_ge(s["pt_evac_d"], b + 1)
                for j in range(NB):
                    w = min(P, HS - j * P)
                    last = mm(ps[:, 7, b * P:(b + 1) * P] if b == 0 else ps[:, 3, 0:P], PT[0:w, j, :], VO[0:w, b, j, :],
                              j == 0, j == NB - 1)
                last.then_inc(s["pv1_ready"], 1)

            eng.wait_ge(s["wqf_ready"], 1)
            for n in range(2):
                for t in range(IT):
                    tr(ps[:, n, t * P:(t + 1) * P], wqf[:, n, t, :])
            for t in range(IT):
                w = P if t < 2 else ILAST
                last = tr(ps[0:w, 2, t * P:(t + 1) * P], wdqf[:, t * P:t * P + w])
            last.then_inc(s["wq_ready"], 1)
            eng.wait_ge(s["x3_ready"], B)
            mm(ps[:, 3, 0:D], wsc[:, 6:7].broadcast_to([P, P]), ident[:]).then_inc(s["sd_ready"], 1)
            eng.wait_ge(s["wq_evac"], 1)
            eng.wait_ge(s["sd_evac"], 1)
            for half in range(2):
                eng.wait_ge(s["qf_ready"], 1)
                for j in range(4):
                    last = tr(ps[:, half, j * P:(j + 1) * P], xn[:, 4 * half + j, :])
                last.then_inc(s["qt_ready"], 1)
            for u in range(2 * IT):
                half, it = divmod(u, IT)
                rows = P if it < 2 else ILAST
                eng.wait_ge(s["q_ready"], half + 1)
                if u >= 3:
                    eng.wait_ge(s["h_ready"], u - 2)
                for n in range(2):
                    last = mm(ps[0:rows, 2 * (u % 3) + GUB + n, :], wguT[:, n, it, 0:rows], qT[:, half * 512:(half + 1) * 512])
                last.then_inc(s["gu_ready"], 1)
            eng.wait_ge(s["hqb_ready"], 1)
            for t in range(NTILE):
                for it in range(IT):
                    rows = P if it < 2 else ILAST
                    last = mm(ps[:, t // 4, (t % 4) * P:(t % 4 + 1) * P], hqb[0:rows, it, t * P:(t + 1) * P],
                              wdT[0:rows, it, :], it == 0, it == IT - 1)
                if t % 4 == 3:
                    last.then_inc(s["dn_ready"], 1)

        @block.vector
        def _(eng):
            steps = [0]

            def step(ins):
                steps[0] += 1
                ins.then_inc(s["dve_step"], 1)
                return steps[0]

            def after(n):
                eng.wait_ge(s["dve_step"], n)

            def norm_stats(c):
                t0, nt = CH_T0[c], CH_NT[c]
                for j in range(t0, t0 + nt):
                    last = eng.bn_stats(stats[:, j, :], xs[:, j, :])
                after(step(last))
                for j in range(t0, t0 + nt):
                    last = eng.bn_aggr(mv[:, j, :], stats[:, j, :])
                after(step(last))
                eng.tensor_scalar(ve[:, t0:t0 + nt], mv[:, t0:t0 + nt, 1], EPS, None, ALU.add).then_inc(s["ve_ready"], 1)

            def normalise(c, n):
                eng.wait_ge(s["rstd_ready"], n)
                for j in range(CH_T0[c], CH_T0[c] + CH_NT[c]):
                    last = eng.tensor_scalar(xn[:, j, :], xs[:, j, :], mv[:, j, 0:1], rstd[:, j:j + 1],
                                             ALU.subtract, ALU.mult)
                return last

            for c in range(3):
                eng.wait_ge(s[f"x_loaded{c}"], 16)
                norm_stats(c)
            eng.wait_ge(s["small_pe"], 1)
            eng.tensor_copy(wobT[:], ps[:, 7, 0:168]).then_inc(s["prep_evac_d"], 1)
            normalise(0, 1).then_inc(s["xn_ready"], 1)
            eng.wait_ge(s["smalls_loaded"], 16 * 11)
            after(step(eng.tensor_tensor(lam_pr[:], lam_in[:, 0:2, :], lam_in[:, 2:4, :], ALU.mult)))
            eng.tensor_reduce(lam_s[:], lam_pr[:], AX, ALU.add).then_inc(s["usum_ready"], 1)
            normalise(1, 2).then_inc(s["xn_ready"], 1)
            eng.wait_ge(s["mask_ready"], 1)
            eng.wait_ge(s["lgsub_ready"], 1)
            n = step(eng.tensor_tensor(nlam[:], lam_e[:, 1:2], lam_e[:, 0:1], ALU.subtract))
            eng.tensor_scalar(sig127[:], gth[:, 4:6], 0.5 / QMAX, 0.5 / QMAX, ALU.mult, ALU.add)
            eng.tensor_scalar(tgli[:], gth[:, 0:1], 1.0 - LAMBDA_INIT, None, ALU.mult).then_inc(s["lgexp_ready"], 1)
            after(n)
            lam_step = step(eng.tensor_scalar(nlam[:], nlam[:], LAMBDA_INIT, None, ALU.subtract))
            normalise(2, 3).then_inc(s["xn_ready"], 1)
            eng.wait_ge(s["a0_ready"], 1)
            eng.tensor_scalar(A0[:, :, 1, :], ps[:, 7, 0:B * S].rearrange("p (b s) -> p b s", b=B), HD ** -0.5, None,
                              ALU.mult).then_inc(s["a0_evac_d"], 1)

            def row_max(c):
                nt = CH_NT[c]
                eng.wait_ge(s["sc0_ready"], c + 1)
                eng.tensor_reduce(nmx0[:, 2 * CH_T0[c]:2 * (CH_T0[c] + nt)],
                                  ps[:, 3 + c, 0:nt * 2 * S].rearrange("p (h s) -> p h s", s=S), AX, ALU.max,
                                  negate=True).then_inc(s["nmx0_ready"], 1)

            def weights(c):
                t0, nt = CH_T0[c], CH_NT[c]
                eng.wait_ge(s["exp0_ready"], c + 1)
                after(step(eng.reciprocal(rc0[:, 2 * t0:2 * (t0 + nt)], se0[:, 2 * t0:2 * (t0 + nt)])))
                ev = E0[:, t0:t0 + nt, :, :].rearrange("p t h s -> p (t h) s")
                after(step(eng.tensor_tensor(ev, ev, rc0[:, 2 * t0:2 * (t0 + nt)].unsqueeze(2).broadcast_to([P, 2 * nt, S]),
                                             ALU.mult)))
                after(lam_step)
                eng.scalar_tensor_tensor(Wt[:, t0:t0 + nt, :], E0[:, t0:t0 + nt, 1, :], nlam[:],
                                         E0[:, t0:t0 + nt, 0, :], ALU.mult, ALU.add).then_inc(s["w_ready"], 1)

            def residual1(c):
                eng.wait_ge(s["rms_ready"], c + 1)
                for j in range(CH_NT[c]):
                    t = CH_T0[c] + j
                    last = eng.scalar_tensor_tensor(xs[:, t, :], ps[:, PVB[c][1], j * P:(j + 1) * P], rms[:, t:t + 1],
                                                    xs[:, t, :], ALU.mult, ALU.add)
                last.then_inc(s["x1_ready"], 1)
                eng.wait_ge(s["x1_ready"], c + 1)
                norm_stats(c)

            row_max(0)
            row_max(1)
            weights(0)
            row_max(2)
            weights(1)
            weights(2)
            for c in range(3):
                residual1(c)
            for c in range(3):
                normalise(c, 4 + c).then_inc(s["xn_ready"], 1)
            prep_evacs(eng, 1)
            for c in range(3):
                t0, w = tok(c)
                eng.wait_ge(s["xhi_ready"], c + 1)
                eng.tensor_copy(xT[:, t0:t0 + w], ps[:, X2B[c], 0:w])
                eng.tensor_tensor(xlo[:, t0:t0 + w], ps[:, X2B[c], 0:w], xhi[:, t0:t0 + w].bitcast(F32),
                                  ALU.subtract).then_inc(s["xlo_ready"], 1)

            eng.wait_ge(s["logit_ready"], 1)
            after(step(eng.tensor_tensor(lg[:], ps[:, 3, 0:NTILE * E].rearrange("p (t e) -> p t e", e=E),
                                         br_bc[:].unsqueeze(1).broadcast_to([P, NTILE, E]), ALU.add)))
            after(step(eng.tensor_reduce(lmx[:], lg[:], AX, ALU.max)))
            eng.tensor_tensor(lg[:], lg[:], lmx[:].unsqueeze(2).broadcast_to([P, NTILE, E]), ALU.subtract).then_inc(
                s["lgsub_ready"], 1)
            eng.wait_ge(s["lgexp_ready"], 2)
            after(step(eng.tensor_reduce(lsum[:], pr[:], AX, ALU.add)))
            after(step(eng.reciprocal(lmx[:], lsum[:])))
            after(step(eng.tensor_tensor(pr[:], pr[:], lmx[:].unsqueeze(2).broadcast_to([P, NTILE, E]), ALU.mult)))
            pk = pr[:].unsqueeze(2).broadcast_to([P, NTILE, E, E])
            pe_ = pr[:].unsqueeze(3).broadcast_to([P, NTILE, E, E])
            eng.wait_ge(s["pool_const"], 3)
            after(step(eng.tensor_tensor(dif[:], pk, pe_, ALU.subtract)))
            after(step(eng.tensor_tensor(dif[:], dif[:], tie[:].unsqueeze(1).broadcast_to([P, NTILE, E, E]), ALU.is_gt)))
            after(step(eng.tensor_tensor(dif[:], dif[:], pk, ALU.mult)))
            after(step(eng.tensor_reduce(cum[:], dif[:], AX, ALU.add)))
            after(step(eng.tensor_tensor(lone[:], cum[:], pr[:], ALU.is_le)))
            after(step(eng.scalar_tensor_tensor(cum[:], cum[:], TOP_P, lone[:], ALU.is_lt, ALU.max)))
            eng.tensor_tensor(gate[:], cum[:], pr[:], ALU.mult).then_inc(s["gate_ready"], 1)

            def bias_of(k, e, slot):
                eng.tensor_scalar(b1cur[:, slot, :], b1T[:, bass.ds(FT * e, FT)], 1.0, None, ALU.mult).then_inc(
                    sp_[k]["b1_ready"], 1)

            def expert(k, e, slot):
                nch = len(PASS_CH[k])
                for ft in range(FT):
                    for ci in range(nch):
                        w = tok(PASS_CH[k][ci])[1]
                        hs = h_slot(k, ft, ci)
                        n = nch * (FT * e + ft) + ci + 1
                        eng.wait_ge(sp_[k]["h32_ready"], n)
                        e0, f0, there = earlier(e, ft, SETS[k])
                        if there:
                            eng.wait_ge(sp_[k]["down_done"], nch * (FT * e0 + f0) + ci + 1)
                        eng.tensor_copy(hhi[:, hs, 0:w], h32[:, hs, 0:w]).then_inc(sp_[k]["hi_ready"], 1)
                        if (ft, ci) not in POOL_LO[k]:
                            eng.wait_ge(sp_[k]["hi_ready"], n)
                            eng.tensor_tensor(hlo[:, hs, 0:w], h32[:, hs, 0:w], hhi[:, hs, 0:w].bitcast(F32),
                                              ALU.subtract).then_inc(sp_[k]["lo_dve"], 1)
                    if ft == 2 and (1 <= e < E - 1 if isinstance(e, int) else True):
                        bias_of(k, e + 1, 1 - slot)
                    if ft == LAG[k] and not (isinstance(e, int) and e == 0):
                        take_y(k, e - 1, 1 - slot)

            def take_y(k, e, slot):
                nch = len(PASS_CH[k])
                t00 = tok(PASS_CH[k][0])[0]
                eng.wait_ge(sp_[k][f"g_loaded{slot}"], 8 * (e - slot) + 16)
                for ci in range(nch):
                    t0, w = tok(PASS_CH[k][ci])
                    eng.wait_ge(sp_[k]["down_done"], nch * (FT * e + FT - 1) + ci + 1)
                    if not isinstance(e, int) or e >= 1:
                        eng.wait_ge(sp_[k]["y_done"], nch * (e - 1) + ci + 1)
                    eng.scalar_tensor_tensor(ytmp[:, ci, 0:w],
                                             ps[:, y_bank(k, slot, ci), 0:w], b2T[:, bass.ds(e, 1)],
                                             G[:, slot, t0 - t00:t0 - t00 + w], ALU.add, ALU.mult).then_inc(
                        sp_[k]["y_mul"], 1)
                for ci in range(nch):
                    t0, w = tok(PASS_CH[k][ci])
                    eng.wait_ge(sp_[k]["y_mul"], nch * e + ci + 1)
                    eng.tensor_tensor(acc[:, t0:t0 + w], acc[:, t0:t0 + w], ytmp[:, ci, 0:w], ALU.add).then_inc(
                        sp_[k]["y_done"], 1)

            eng.wait_ge(s["acc_zero"], 1)
            for k in range(2):
                bias_of(k, 0, 0)
                bias_of(k, 1, 1)
                expert(k, 0, 0)
                expert(k, 1, 1)
                with eng.Fori(2, E - 3, 2) as e:
                    for slot in range(2):
                        expert(k, e + slot, slot)
                expert(k, E - 2, 0)
                expert(k, E - 1, 1)
                take_y(k, E - 1, 1)
                if k == 0:
                    eng.wait_ge(s["acct_ready"], 1)
                    after(step(eng.scalar_tensor_tensor(xs[:, 0:2, :], ps[:, 6, 0:2 * P].rearrange("p (t d) -> p t d", d=D),
                                                        gth[:, 2:3], xs[:, 0:2, :], ALU.mult, ALU.add)))
                    norm_stats(0)
                    normalise(0, 7).then_inc(s["xn_ready"], 1)

            after(step(eng.tensor_reduce(usum[:], VOT[:], AX, ALU.add)))
            eng.tensor_scalar(usum[:], usum[:], 1.0 / S, None, ALU.mult).then_inc(s["usum_ready"], 1)
            tbo_step = step(eng.tensor_scalar(tbo[:], bo_bc[:], gth[:, 1:2], None, ALU.mult))
            eng.wait_ge(s["ffnw_loaded"], 16 * 5)
            eng.wait_ge(s["pad_ready"], 1)
            eng.tensor_reduce(wmx[:, 0:6], wgu_raw[:].rearrange("p n t d -> p (n t) d"), AX, ALU.max, apply_absolute_value=True)
            after(step(eng.tensor_reduce(wmx[:, 6:7], wd_raw[:], AX, ALU.max, apply_absolute_value=True)))
            after(step(eng.tensor_scalar(wsc[:], wmx[:], 1.0 / QMAX, None, ALU.mult)))
            eng.reciprocal(winv[:], wsc[:]).then_inc(s["wmx_ready"], 1)
            for c in (1, 2):
                eng.wait_ge(s["acct_ready"], 1 + c)
                t0, nt = CH_T0[c], CH_NT[c]
                eng.scalar_tensor_tensor(xs[:, t0:t0 + nt, :], ps[:, c, 0:nt * P].rearrange("p (t d) -> p t d", d=D),
                                         gth[:, 2:3], xs[:, t0:t0 + nt, :], ALU.mult, ALU.add).then_inc(s["x2_ready"], 1)
            eng.wait_ge(s["u_evac"], 1)
            after(tbo_step)
            for c in (1, 2):
                t0, nt = CH_T0[c], CH_NT[c]
                row = urow[:, c - 1, :]
                eng.wait_ge(s["x2_ready"], c)
                n2 = step(eng.tensor_tensor(xs[:, t0:t0 + nt, :], xs[:, t0:t0 + nt, :],
                                            row.unsqueeze(1).broadcast_to([P, nt, D]), ALU.add))
            after(n2)
            for c in (1, 2):
                t0, nt = CH_T0[c], CH_NT[c]
                n = step(eng.tensor_tensor(xs[:, t0:t0 + nt, :], xs[:, t0:t0 + nt, :],
                                           tbo[:].unsqueeze(1).broadcast_to([P, nt, D]), ALU.add))
            after(n)
            norm_stats(1)
            norm_stats(2)
            normalise(1, 8)
            last_n = step(normalise(2, 9))
            after(step(eng.tensor_tensor(xs[:, 0:2, :], xs[:, 0:2, :], tbo[:].unsqueeze(1).broadcast_to([P, 2, D]), ALU.add)))

            eng.wait_ge(s["mask_ready"], 2)
            for b in range(B):
                if b == 1:
                    eng.wait_ge(s["exp1_ready"], 1)
                for gi, (h0, nh) in enumerate(HG):
                    eng.wait_ge(s["sc1_ready"], 3 * b + gi + 1)
                    eng.tensor_tensor(SC[:, h0:h0 + nh, :], ps[:, SCB[gi], 0:nh * S].rearrange("p (h s) -> p h s", s=S),
                                      maskadd[:, b, :].unsqueeze(1).broadcast_to([P, nh, S]), ALU.add).then_inc(
                        s["dve_sc1"], 1)
                eng.wait_ge(s["dve_sc1"], 3 * b + 3)
                eng.tensor_reduce(nmx1[:, b, :], SC[:], AX, ALU.max, negate=True).then_inc(s["nmx1_ready"], 1)
                eng.wait_ge(s["exp1_ready"], b + 1)
                after(step(eng.reciprocal(rc1[:, b, :], se1[:, b, :])))
                prv = PR[:].rearrange("p (h s) -> p h s", s=S)
                eng.tensor_tensor(prv, prv, rc1[:, b, :].unsqueeze(2).broadcast_to([P, H1, S]), ALU.mult).then_inc(
                    s["pr_ready"], 1)
                eng.wait_ge(s["pt_ready"], b + 1)
                eng.tensor_copy(PT[:, 4:8, :].rearrange("p j d -> p (j d)"), ps[:, 5, :]).then_inc(s["pt_evac_d"], 1)
                eng.wait_ge(s["pv1_ready"], b + 1)
                src = ps[:, 7, b * P:(b + 1) * P] if b == 0 else ps[:, 3, 0:P]
                eng.scalar_tensor_tensor(xs[:, b, :], src, gth[:, 1:2], xs[:, b, :], ALU.mult, ALU.add).then_inc(
                    s["x3_ready"], 1)
            eng.wait_ge(s["x3_ready"], B)
            norm_stats(0)
            after(step(normalise(0, 10)))
            after(last_n)
            eng.tensor_reduce(xmx[:], xn[:], mybir.AxisListType.XY, ALU.max, apply_absolute_value=True).then_inc(
                s["xmx_ready"], 1)
            eng.wait_ge(s["xmxa_ready"], 1)
            after(step(eng.tensor_tensor(sx[:], xmxa[:], sig127[:, 0:1], ALU.mult)))
            after(step(eng.reciprocal(sxi[:], sx[:])))
            eng.tensor_scalar(xn[:], xn[:], sxi[:], MAGIC, ALU.mult, ALU.add).then_inc(s["qf_ready"], 1)
            n = step(eng.tensor_scalar(gsx[:], wsc[:, 0:3], sx[:], 0.5, ALU.mult, ALU.mult))
            n = step(eng.tensor_scalar(gsx2[:], wsc[:, 3:6], sx[:], None, ALU.mult))
            eng.memset(hmx[:], 0.0)
            after(n)
            after(step(eng.tensor_tensor(hsc[:], gsx[:], gsx2[:], ALU.mult)))
            for half in range(2):
                eng.wait_ge(s["qt_ready"], half + 1)
                q = qT[:, half * 512:(half + 1) * 512]
                after(step(eng.tensor_scalar(q, ps[:, half, :], MAGIC, QMAX, ALU.subtract, ALU.min)))
                eng.tensor_scalar(q, q, -QMAX - 1.0, None, ALU.max).then_inc(s["q_ready"], 1)
            for u in range(2 * IT):
                half, it = divmod(u, IT)
                rows = P if it < 2 else ILAST
                bank = 2 * (u % 3) + GUB
                hv = hq[0:rows, it, half * 512:(half + 1) * 512]
                eng.wait_ge(s["th_ready"], u + 1)
                after(step(eng.scalar_tensor_tensor(hv, th[0:rows, u % 2, :], 1.0, ps[0:rows, bank, :], ALU.add, ALU.mult)))
                eng.scalar_tensor_tensor(hv, hv, hsc[0:rows, it:it + 1], ps[0:rows, bank + 1, :], ALU.mult,
                                         ALU.mult).then_inc(s["h_ready"], 1)
                eng.wait_ge(s["h_ready"], u + 1)
                n = step(eng.tensor_reduce(hmx[0:rows, u:u + 1], hv, AX, ALU.max, apply_absolute_value=True))
            after(n)
            eng.tensor_reduce(hmxr[:], hmx[:], AX, ALU.max).then_inc(s["hmx_ready"], 1)
            eng.wait_ge(s["hmxa_ready"], 1)
            after(step(eng.tensor_tensor(sh[:], hmxa[:], sig127[:, 1:2], ALU.mult)))
            after(step(eng.reciprocal(shi[:], sh[:])))
            for it in range(IT):
                rows = P if it < 2 else ILAST
                after(step(eng.tensor_scalar(hq[0:rows, it, :], hq[0:rows, it, :], shi[0:rows, :], MAGIC, ALU.mult, ALU.add)))
                after(step(eng.tensor_scalar(hqb[0:rows, it, :], hq[0:rows, it, :], MAGIC, QMAX, ALU.subtract, ALU.min)))
                last = eng.tensor_scalar(hqb[0:rows, it, :], hqb[0:rows, it, :], -QMAX - 1.0, None, ALU.max)
            last.then_inc(s["hqb_ready"], 1)
            eng.wait_ge(s["sd_evac"], 1)
            for half in range(2):
                eng.wait_ge(s["dn_ready"], half + 1)
                o = otmp[:, 4 * half:4 * half + 4, :]
                after(step(eng.scalar_tensor_tensor(o, ps[:, half, :].rearrange("p (t d) -> p t d", d=D), sh[:],
                                                    sdg[:].unsqueeze(1).broadcast_to([P, 4, D]), ALU.mult, ALU.mult)))
                eng.tensor_tensor(xs[:, 4 * half:4 * half + 4, :], xs[:, 4 * half:4 * half + 4, :], o, ALU.add).then_inc(
                    s["out_ready"], 1)


_INS = ["x", "ctx_1024", "mask_BxS2_bk0", "g_xattn", "g_ffn", "L0_xattn_Wq", "L0_xattn_Wk", "L0_xattn_Wv", "L0_xattn_Wo",
        "L0_xattn_lambda_q1", "L0_xattn_lambda_k1", "L0_xattn_lambda_q2", "L0_xattn_lambda_k2",
        "L0_ffn_Wr", "L0_ffn_br", "L0_ffn_W1", "L0_ffn_b1", "L0_ffn_W2", "L0_ffn_b2",
        "L1_xattn_Wq", "L1_xattn_Wkv", "L1_xattn_Wo", "L1_xattn_bo",
        "L1_ffn_clip_x", "L1_ffn_clip_down", "L1_ffn_w_gate", "L1_ffn_w_up", "L1_ffn_w_down"]


def kernel(**inputs):
    import numpy as _np
    import concourse.bacc as _bacc
    from concourse import mybir as _mybir
    from concourse.bass_utils import run_bass_kernel_spmd as _run

    nc = _bacc.Bacc("TRN2", target_bir_lowering=False, num_devices=1)
    arrays, args = {}, []
    for name in _INS:
        a = _np.ascontiguousarray(inputs[name])
        arrays[f"in_{name}"] = a
        args.append(nc.dram_tensor(f"in_{name}", a.shape, _mybir.dt.from_np(a.dtype), kind="ExternalInput").ap())
    args.append(nc.dram_tensor("out_0", (B, N, D), F32, kind="ExternalOutput").ap())
    build(nc, *args)
    r = _run(nc, [arrays], core_ids=[0])
    return r.results[0]["out_0"]
```

```python
import math
from contextlib import ExitStack

import concourse.bass as bass
from concourse import mybir

F32 = mybir.dt.float32
F32R = mybir.dt.float32r
BF16 = mybir.dt.bfloat16
U8 = mybir.dt.uint8
ALU = mybir.AluOpType
ACT = mybir.ActivationFunctionType
AX = mybir.AxisListType.X

P = 128
B, N, D = 2, 512, 128
S = 77
T = B * N
NTILE = T // P
HD = D // 2
E, F = 8, 512
FT = F // P
H1, DH = 16, 64
INNER = H1 * DH
NI = INNER // P
HS = H1 * S
NB = -(-HS // P)
I = 352
IT = 3
ILAST = I - 2 * P

LAMBDA_INIT = 0.8 - 0.6 * math.exp(-0.3 * 12)
EPS = 1e-5
TOP_P = 0.8
QMAX = 127.0
MAGIC = 1.5 * 2.0 ** 23
NEG = -3.4028234663852886e38

CH_T0 = [0, 2, 5]
CH_NT = [2, 3, 3]
CAUSAL = S - N + 1
assert (N // P - 1) * P - 1 + CAUSAL <= 0, "rows before the last tile see no context token"

HG = [(0, 6), (6, 6), (12, 4)]
G3 = [(0, 3), (3, 3), (6, 2)]

EARLY = dict(ctxT=B * S, wkT2=2 * HD, wvT=D, woT=D, wq=D)
LATE = dict(b1T=E * FT, b2T=E, wr=E, gsc=6, br=E, bo=D, lam=4 * HD)


def ranges(widths):
    at, found = 0, {}
    for name, w in widths.items():
        found[name] = (at, at + w)
        at += w
    return found, at


def build(nc, x, early, late, mask, l1w_in, ffnw_in, experts, out):
    st = ExitStack()
    with st:
        def sb(name, shape, dt=F32):
            return st.enter_context(nc.sbuf_tensor(name, shape, dt))

        def sem(name):
            return st.enter_context(nc.semaphore(name))

        ps = st.enter_context(nc.psum_tensor("ps", [P, 8, 512], F32))
        gates_dram = nc.dram_tensor("gates_dram", (E, T), F32).ap()

        ident = sb("ident", [P, P])
        tie = sb("tie", [P, E, E])
        mhalf = sb("mhalf", [P, NTILE])
        early_at, early_w = ranges(EARLY)
        late_at, late_w = ranges(LATE)
        early_sb = sb("early_sb", [P, early_w])
        late_sb = sb("late_sb", [P, late_w])

        def of(t, at, name):
            return t[:, at[name][0]:at[name][1]]

        ctxT, wkT2, wvT, woT, wq0_sb = (of(early_sb, early_at, n) for n in EARLY)
        b1T, b2T, wr_sb, gsc, br_bc, bo_bc, lam_flat = (of(late_sb, late_at, n) for n in LATE)
        lam_in = lam_flat.rearrange("p (a d) -> p a d", a=4)
        gth = sb("gth", [P, 6])
        tgli = sb("tgli", [P, 1])
        sig127 = sb("sig127", [P, 2])
        lam_pr = sb("lam_pr", [P, 2, HD])
        lam_s = sb("lam_s", [P, 2])
        lam_e = sb("lam_e", [P, 2])
        nlam = sb("nlam", [P, 1])
        mask_u8 = sb("mask_u8", [P, B, S], U8)
        maskadd = sb("maskadd", [P, B, S])

        xs = sb("xs", [P, NTILE, D])
        xn = sb("xn", [P, NTILE, D])
        stats = sb("stats", [P, NTILE, 6])
        mv = sb("mv", [P, NTILE, 2])
        ve = sb("ve", [P, NTILE])
        rstd = sb("rstd", [P, NTILE])

        kv0T = sb("kv0T", [P, 2, B * S])
        A0 = sb("A0", [P, B, 2, S])
        VV = sb("VV", [S, B, 2, D])
        xT = sb("xT", [P, T])
        nmx0 = sb("nmx0", [P, NTILE * 2])
        se0 = sb("se0", [P, NTILE * 2])
        rc0 = sb("rc0", [P, NTILE * 2])
        ss = sb("ss", [P, NTILE])
        ms = sb("ms", [P, NTILE])
        rms = sb("rms", [P, NTILE])

        xhi = sb("xhi", [P, T], F32R)
        xlo = sb("xlo", [P, T], F32R)
        lg = sb("lg", [P, NTILE, E])
        lmx = sb("lmx", [P, NTILE])
        lsum = sb("lsum", [P, NTILE])
        pr = sb("pr", [P, NTILE, E])
        dif = sb("dif", [P, NTILE, E, E])
        cum = sb("cum", [P, NTILE, E])
        lone = sb("lone", [P, NTILE, E])
        gate = sb("gate", [P, NTILE, E])
        gateT = sb("gateT", [E, T])
        G = sb("G", [P, 2, T])
        raw = sb("raw", [P, 2, F + FT * D])
        w1hi = sb("w1hi", [P, 2, F], F32R)
        w1lo = sb("w1lo", [P, 2, F], F32R)
        w2hi = sb("w2hi", [P, 2, FT * D], F32R)
        w2lo = sb("w2lo", [P, 2, FT * D], F32R)
        b1cur = sb("b1cur", [P, 2, FT])
        h32 = sb("h32", [P, 4, 512])
        hhi = sb("hhi", [P, 4, 512], F32R)
        hlo = sb("hlo", [P, 4, 512], F32R)
        ytmp = sb("ytmp", [P, 2, 512])
        acc = sb("acc", [P, T])

        l1w = sb("l1w", [P, 4 * INNER])
        wq1T = l1w[:, 0:INNER].rearrange("p (i d) -> p i d", i=NI)
        wkv1_sb = l1w[:, INNER:3 * INNER]
        wo1_sb = l1w[:, 3 * INNER:].rearrange("p (i d) -> p i d", i=NI)
        kv1T = sb("kv1T", [P, 2, NI, B * S])
        kT1, vT1 = kv1T[:, 0, :, :], kv1T[:, 1, :, :]
        A1 = sb("A1", [P, B, H1, S])
        VOT = sb("VOT", [P, B, H1 * S])
        VO = sb("VO", [P, B, NB, D])
        usum = sb("usum", [P, B])
        urow = sb("urow", [P, B, D])
        tbo = sb("tbo", [P, D])
        SC = sb("SC", [P, B, H1, S])
        PR = sb("PR", [P, B, H1 * S])
        PT = sb("PT", [P, NB, P])
        E0 = SC[:, 0, :, :].rearrange("p (t two) s -> p t two s", two=2)
        Wt = PR[:, 1, 0:NTILE * S].rearrange("p (t s) -> p t s", s=S)
        wT = VO[0:S, 0, 0:NTILE, :]
        sq = VO[:, 1, 0:NTILE, :]
        uscr = PR[:, 0, :]
        nmx1 = sb("nmx1", [P, B, H1])
        se1 = sb("se1", [P, B, H1])
        rc1 = sb("rc1", [P, B, H1])

        wf_raw = sb("wf_raw", [P, 2 * IT * D + I])
        wmx = sb("wmx", [P, 7])
        wsc = sb("wsc", [P, 7])
        winv = sb("winv", [P, 7])
        wqf = sb("wqf", [P, 2 * IT * D + I])
        wguT = sb("wguT", [P, 2, IT, P], BF16)
        wdT = sb("wdT", [P, IT, D], BF16)
        sdg = sb("sdg", [P, D])
        sdgs = sb("sdgs", [P, D])
        xmx = sb("xmx", [P, 2])
        xmxa = sb("xmxa", [P, 2])
        sx = sb("sx", [P, 1])
        sxi = sb("sxi", [P, 1])
        qT = sb("qT", [P, T], BF16)
        gsx = sb("gsx", [P, 6])
        sl = ytmp
        hq = l1w[:, 0:IT * T].rearrange("p (i t) -> p i t", i=IT)
        hmx = sb("hmx", [P, IT * 2])
        hmxr = sb("hmxr", [P, 1])
        hmxa = sb("hmxa", [P, 1])
        sh = sb("sh", [P, 1])
        shi = sb("shi", [P, 1])
        hqb = kv1T[:].rearrange("p a i b -> p (a i b)")[:, 0:IT * T // 2].bitcast(BF16).rearrange(
            "p (i t) -> p i t", i=IT)
        otmp = xT[:].rearrange("p (t d) -> p t d", d=D)

        names = """acc_zero x_loaded0 x_loaded1 x_loaded2 early_loaded late_loaded mask_loaded l1wa_loaded l1wb_loaded
            ffnw_loaded pool_const mask_ready dve_step pool_step
            lam_summed tanh_ready lam_exp tgli_ready kv0_ready kv0_evac a0_ready a0_evac_a a0_evac_d vv_evac
            ve_ready rstd_ready xn_ready xt_ready xt_evac sc0_ready nmx0_ready exp0_ready w_ready wt_ready wt_evac
            pv_ready sq_ready rms_ready x1_ready x2t_ready xhi_ready xlo_ready xt2_evac
            logit_ready lgsub_ready lgexp_ready gate_ready gt_ready gt_evac gt_stored
            prep_ready pevac_a pevac_d usum_ready u_ready urow_ready row_added
            acct_ready x2_ready vo_ready vo_evac
            wmx_ready wqf_ready wq_ready wq_evac sd_ready sd_evac
            sc1_ready sc1_masked nmx1_ready exp1_ready pr_ready pt_ready pt_evac_a pt_evac_d pv1_ready x3_ready
            xmx_ready xmxa_ready sxi_ready qf_a qf_d qt_ready q_ready gu_ready sl_ready h_ready hmx_ready hmxa_ready
            shi_ready hqf_ready hqb_ready dn_ready o_ready out_ready_p out_ready_d out_stored
            raw_loaded0 raw_loaded1 g_loaded0 g_loaded1 whi_ready w1_split w2_split up_done h32_ready hi_ready
            b1_ready lo_dve lo_pool down_done y_mul y_done""".split()
        s = {n: sem(n) for n in names}

        LAG = 2
        POOL_LO = [(0, 1), (1, 1), (3, 1)]

        def lo_count(e, ft, ci):
            pool = (ft, ci) in POOL_LO
            mine = [(f, c) for f in range(FT) for c in range(2) if ((f, c) in POOL_LO) == pool]
            return s["lo_pool" if pool else "lo_dve"], len(mine) * e + mine.index((ft, ci)) + 1

        def h_slot(ft, ci):
            return (ft % 2) * 2 + ci

        def y_bank(slot, ci):
            return 4 + slot * 2 + ci

        def earlier(e, ft, back):
            m = ft - back
            return e + m // FT, m % FT, not (isinstance(e, int) and FT * e + m < 0)

        def fixed(e):
            return isinstance(e, int)

        def tok(c):
            return CH_T0[c] * P, CH_NT[c] * P

        PVB = [(3, 0), (4, 1), (5, 2)]
        X2B = [3, 4, 5]
        SCB = [[2, 3, 4], [5, 6, 7]]
        VOU = [(b, j0, nj) for b in range(B) for j0, nj in ((0, 4), (4, 4), (8, 2))]
        VOB = [0, 1]
        GUB = 2
        PREP = ([("kT", a, n, 0) for a, n in G3] + [("A", a, n, par) for par in range(2) for a, n in G3]
                + [("vT", a, n, 0) for a, n in G3] + [("VOT", a, n, par) for par in range(2) for a, n in G3])
        PREP_FIRST = {kind: [k[0] for k in PREP].index(kind) for kind in ("A", "vT", "VOT")}

        def prep_evacs(eng, mine, lo, hi):
            def copy(dst, src, scale=1.0):
                if mine == 0:
                    return eng.activation(dst, src, ACT.Copy, scale=scale)
                if scale != 1.0:
                    return eng.tensor_scalar(dst, src, scale, None, ALU.mult)
                return eng.tensor_copy(dst, src)

            for u in range(lo, hi):
                if u % 2 != mine:
                    continue
                kind, n0, cnt, par = PREP[u]
                eng.wait_ge(s["prep_ready"], u + 1)
                if kind in ("kT", "vT"):
                    dst = (kT1 if kind == "kT" else vT1)[:, n0:n0 + cnt, :]
                    last = copy(dst.rearrange("p i d -> p (i d)"), ps[:, 6 + u % 2, 0:cnt * B * S])
                else:
                    src = ps[:, 6 + u % 2, 0:cnt * B * S].rearrange("p (i b s) -> p i b s", b=B, s=S)
                    dst = A1[:] if kind == "A" else VOT[:].rearrange("p b (h s) -> p b h s", s=S)
                    dst = dst.rearrange("p b (i two) s -> p i two b s", two=2)[:, n0:n0 + cnt, par, :, :]
                    last = copy(dst, src, DH ** -0.5 if kind == "A" else 1.0)
                last.then_inc(s["pevac_a" if mine == 0 else "pevac_d"], 1)

        block = st.enter_context(nc.Block())

        @block.sync
        def _(eng):
            xv = x.rearrange("b (t p) d -> p b t d", p=P)
            eng.dma_start(xs[:, 0:2, :], xv[:, :, 3, :]).then_inc(s["x_loaded0"], 16)
            eng.dma_start(early_sb[:], early).then_inc(s["early_loaded"], 16)
            eng.dma_start(xs[:, 2:5, :], xv[:, 0, 0:3, :]).then_inc(s["x_loaded1"], 16)
            eng.dma_start(xs[:, 5:8, :], xv[:, 1, 0:3, :]).then_inc(s["x_loaded2"], 16)
            eng.dma_start(late_sb[:], late).then_inc(s["late_loaded"], 16)
            eng.dma_start(l1w[:, 0:2 * INNER], l1w_in[:, 0:2 * INNER]).then_inc(s["l1wa_loaded"], 16)

            def load_expert(e, slot):
                if not fixed(e) or e >= 2:
                    eng.wait_ge(s["w2_split"], e - 1)
                eng.dma_start(raw[:, slot, :], experts[bass.ds(e, 1), :, :].rearrange("a p f -> p (a f)")).then_inc(
                    s[f"raw_loaded{slot}"], 16)

            def load_gates(e, slot):
                if not fixed(e) or e >= 2:
                    eng.wait_ge(s["y_mul"], 2 * (e - 1))
                eng.dma_start(G[:, slot, :], gates_dram[bass.ds(e, 1), :].broadcast_to([P, T])).then_inc(
                    s[f"g_loaded{slot}"], 16)

            load_expert(0, 0)
            eng.dma_start(l1w[:, 2 * INNER:], l1w_in[:, 2 * INNER:]).then_inc(s["l1wb_loaded"], 16)
            load_expert(1, 1)
            eng.dma_start(mask_u8[:].rearrange("p b s -> p (b s)"), mask).then_inc(s["mask_loaded"], 16)
            eng.dma_start(wf_raw[:], ffnw_in).then_inc(s["ffnw_loaded"], 16)

            eng.wait_ge(s["gt_evac"], 2)
            eng.dma_start(gates_dram, gateT[:]).then_inc(s["gt_stored"], 16)
            eng.wait_ge(s["gt_stored"], 16)
            load_gates(0, 0)
            load_gates(1, 1)
            with eng.Fori(2, E - 1, 2) as e:
                for slot in range(2):
                    load_expert(e + slot, slot)
                    load_gates(e + slot, slot)

            ov = out.rearrange("b (t p) d -> p b t d", p=P)
            eng.wait_ge(s["out_ready_p"], 1)
            eng.dma_start(ov[:, :, 3, :], xs[:, 0:2, :]).then_inc(s["out_stored"], 16)
            eng.dma_start(ov[:, 0, 0:2, :], xs[:, 2:4, :]).then_inc(s["out_stored"], 16)
            eng.wait_ge(s["out_ready_d"], 1)
            eng.dma_start(ov[:, 0, 2, :], xs[:, 4, :]).then_inc(s["out_stored"], 16)
            eng.dma_start(ov[:, 1, 0:3, :], xs[:, 5:8, :]).then_inc(s["out_stored"], 16)
            eng.wait_ge(s["out_stored"], 64)

        @block.gpsimd
        def _(eng):
            steps = [0]

            def step(ins):
                steps[0] += 1
                ins.then_inc(s["pool_step"], 1)
                eng.wait_ge(s["pool_step"], steps[0])

            def inv_root(c, n):
                t0, nt = CH_T0[c], CH_NT[c]
                eng.wait_ge(s["ve_ready"], n)
                eng.tensor_tensor(rstd[:, t0:t0 + nt], ve[:, t0:t0 + nt], mhalf[:, t0:t0 + nt], ALU.pow).then_inc(
                    s["rstd_ready"], 1)

            step(eng.memset(mhalf[:], -0.5))
            step(eng.memset(ident[:], 0.0))
            eng.affine_select(out=ident[:], in_=ident[:], compare_op=ALU.not_equal, fill=1.0, base=0,
                              pattern=[[-1, P]], channel_multiplier=1).then_inc(s["pool_const"], 1)
            for c in range(3):
                inv_root(c, c + 1)
            eng.memset(acc[:], 0.0).then_inc(s["acc_zero"], 1)
            step(eng.memset(tie[:], -1e-37))
            eng.affine_select(out=tie[:], in_=tie[:], compare_op=ALU.is_ge, fill=0.0, base=0,
                              pattern=[[1, E], [-1, E]], channel_multiplier=0).then_inc(s["pool_const"], 1)

            def split_low(e, slot):
                eng.wait_ge(s["whi_ready"], 2 * e + 1)
                if not fixed(e) or e >= 2:
                    eng.wait_ge(s["up_done"], 2 * FT * (e - 1))
                eng.tensor_tensor(w1lo[:, slot, :], raw[:, slot, 0:F], w1hi[:, slot, :].bitcast(F32),
                                  ALU.subtract).then_inc(s["w1_split"], 1)
                eng.wait_ge(s["whi_ready"], 2 * e + 2)
                if not fixed(e) or e >= 2:
                    eng.wait_ge(s["down_done"], 2 * FT * (e - 1))
                eng.tensor_tensor(w2lo[:, slot, :], raw[:, slot, F:], w2hi[:, slot, :].bitcast(F32),
                                  ALU.subtract).then_inc(s["w2_split"], 1)

            def inv_rms(c):
                t0, nt = CH_T0[c], CH_NT[c]
                eng.wait_ge(s["sq_ready"], c + 1)
                step(eng.tensor_scalar(ms[:, t0:t0 + nt], ss[:, t0:t0 + nt], 1.0 / D, EPS, ALU.mult, ALU.add))
                eng.tensor_tensor(rms[:, t0:t0 + nt], ms[:, t0:t0 + nt], mhalf[:, t0:t0 + nt], ALU.pow).then_inc(
                    s["rms_ready"], 1)

            inv_rms(0)
            inv_rms(1)
            inv_root(0, 4)
            inv_rms(2)
            inv_root(1, 5)
            inv_root(2, 6)
            split_low(0, 0)
            split_low(1, 1)
            eng.wait_ge(s["mask_loaded"], 16)
            step(eng.tensor_scalar(maskadd[:], mask_u8[:], -1.0, -NEG, ALU.add, ALU.mult))
            eng.affine_select(out=maskadd[:], in_=maskadd[:], compare_op=ALU.is_ge, fill=NEG,
                              base=(N // P - 1) * P + CAUSAL - 1, pattern=[[0, B], [-1, S]],
                              channel_multiplier=1).then_inc(s["mask_ready"], 1)

            def expert(e, slot):
                for ft in range(FT):
                    if ft == 2 and (1 <= e < E - 1 if fixed(e) else True):
                        split_low(e + 1, 1 - slot)
                    for ci in range(2):
                        if (ft, ci) in POOL_LO:
                            hs = h_slot(ft, ci)
                            eng.wait_ge(s["hi_ready"], 2 * (FT * e + ft) + ci + 1)
                            eng.tensor_tensor(hlo[:, hs, :], h32[:, hs, :], hhi[:, hs, :].bitcast(F32),
                                              ALU.subtract).then_inc(s["lo_pool"], 1)

            expert(0, 0)
            for b in range(B):
                t0, nt = CH_T0[1 + b], CH_NT[1 + b]
                eng.wait_ge(s["urow_ready"], b + 1)
                eng.tensor_tensor(xs[:, t0:t0 + nt, :], xs[:, t0:t0 + nt, :],
                                  urow[:, b, :].unsqueeze(1).broadcast_to([P, nt, D]), ALU.add).then_inc(s["row_added"], 1)
            expert(1, 1)
            with eng.Fori(2, E - 3, 2) as e:
                for slot in range(2):
                    expert(e + slot, slot)
            eng.wait_ge(s["wmx_ready"], 1)
            for c in range(7):
                w = D if c < 6 else I
                last = eng.tensor_scalar(wqf[:, c * D:c * D + w], wf_raw[:, c * D:c * D + w], winv[:, c:c + 1], MAGIC,
                                         ALU.mult, ALU.add)
            last.then_inc(s["wqf_ready"], 1)
            expert(E - 2, 0)
            expert(E - 1, 1)
            for n, c in enumerate((0, 1, 2, 0)):
                inv_root(c, 7 + n)

            RMAX = bass.bass_isa.ReduceOp.absmax
            eng.wait_ge(s["xmx_ready"], 1)
            eng.partition_all_reduce(xmxa[:], xmx[:], P, RMAX).then_inc(s["xmxa_ready"], 1)
            eng.wait_ge(s["hmx_ready"], 1)
            eng.partition_all_reduce(hmxa[:], hmxr[:], P, RMAX).then_inc(s["hmxa_ready"], 1)
            eng.wait_ge(s["o_ready"], 1)
            eng.tensor_tensor(xs[:, 0:4, :], xs[:, 0:4, :], otmp[:, 0:4, :], ALU.add).then_inc(s["out_ready_p"], 1)

        @block.scalar
        def _(eng):
            eng.wait_ge(s["kv0_ready"], 1)
            eng.activation(kv0T[:].rearrange("p a b -> p (a b)"), ps[:, 7, 0:2 * B * S], ACT.Copy).then_inc(s["kv0_evac"], 1)
            eng.wait_ge(s["late_loaded"], 16)
            eng.activation(gth[:, 0:4], gsc[:, 0:4], ACT.Tanh)
            eng.activation(gth[:, 4:6], gsc[:, 4:6], ACT.Tanh, scale=0.5).then_inc(s["tanh_ready"], 1)
            eng.wait_ge(s["a0_ready"], 1)
            eng.activation(A0[:, :, 0, :], ps[:, 6, 0:B * S].rearrange("p (b s) -> p b s", b=B), ACT.Copy,
                           scale=HD ** -0.5).then_inc(s["a0_evac_a"], 1)

            def xt_evac(c):
                t0, w = tok(c)
                eng.wait_ge(s["xt_ready"], c + 1)
                eng.activation(xT[:, t0:t0 + w], ps[:, c, 0:w], ACT.Copy).then_inc(s["xt_evac"], 1)

            def exps(c):
                eng.wait_ge(s["nmx0_ready"], c + 1)
                for j in range(CH_NT[c]):
                    for h in range(2):
                        i = 2 * (CH_T0[c] + j) + h
                        last = eng.activation(E0[:, CH_T0[c] + j, h, :], ps[:, 3 + c, (2 * j + h) * S:(2 * j + h + 1) * S],
                                              ACT.Exp, bias=nmx0[:, i:i + 1], accum_out=se0[:, i:i + 1])
                last.then_inc(s["exp0_ready"], 1)

            def wt_evac(c):
                t0, nt = CH_T0[c], CH_NT[c]
                eng.wait_ge(s["wt_ready"], c + 1)
                eng.activation(wT[:, t0:t0 + nt, :].rearrange("p t d -> p (t d)"), ps[0:S, c, 0:nt * P],
                               ACT.Copy).then_inc(s["wt_evac"], 1)

            def squares(c):
                eng.wait_ge(s["pv_ready"], c + 1)
                for j in range(CH_NT[c]):
                    t = CH_T0[c] + j
                    last = eng.activation(sq[:, t, :], ps[:, PVB[c][0], j * D:(j + 1) * D], ACT.Square,
                                          accum_out=ss[:, t:t + 1])
                last.then_inc(s["sq_ready"], 1)

            def split_high(e, slot):
                eng.wait_ge(s[f"raw_loaded{slot}"], 8 * (e - slot) + 16)
                if not fixed(e) or e >= 2:
                    eng.wait_ge(s["up_done"], 2 * FT * (e - 1))
                eng.activation(w1hi[:, slot, :], raw[:, slot, 0:F], ACT.Copy).then_inc(s["whi_ready"], 1)
                if not fixed(e) or e >= 2:
                    eng.wait_ge(s["down_done"], 2 * FT * (e - 1))
                eng.activation(w2hi[:, slot, :], raw[:, slot, F:], ACT.Copy).then_inc(s["whi_ready"], 1)

            for c in range(3):
                xt_evac(c)
            vvp = ps[0:S, 5, :].rearrange("p (b a d) -> p b a d", b=B, a=2)
            eng.activation(VV[:, :, 0, :], vvp[:, :, 0, :], ACT.Copy)
            eng.wait_ge(s["tgli_ready"], 1)
            eng.activation(VV[:, :, 1, :], vvp[:, :, 1, :], ACT.Copy, scale=tgli[0:S, :]).then_inc(s["vv_evac"], 1)
            eng.wait_ge(s["lam_summed"], 1)
            eng.activation(lam_e[:], lam_s[:], ACT.Exp).then_inc(s["lam_exp"], 1)
            exps(0)
            exps(1)
            prep_evacs(eng, 0, 0, 3)
            wt_evac(0)
            exps(2)
            prep_evacs(eng, 0, 3, 5)
            squares(0)
            wt_evac(1)
            squares(1)
            prep_evacs(eng, 0, 5, 7)
            wt_evac(2)
            squares(2)
            prep_evacs(eng, 0, 7, 12)
            split_high(0, 0)
            split_high(1, 1)
            prep_evacs(eng, 0, 12, 18)
            for c in range(3):
                t0, w = tok(c)
                eng.wait_ge(s["x2t_ready"], c + 1)
                eng.activation(xhi[:, t0:t0 + w], ps[:, X2B[c], 0:w], ACT.Copy).then_inc(s["xhi_ready"], 1)
            for c in range(3):
                t0, w = tok(c)
                eng.wait_ge(s["xlo_ready"], c + 1)
                eng.activation(xT[:, t0:t0 + w], ps[:, X2B[c], 0:w], ACT.Copy).then_inc(s["xt2_evac"], 1)

            def expert(e, slot):
                eng.wait_ge(s["b1_ready"], e + 1)
                for ft in range(FT):
                    for ci in range(2):
                        hs = h_slot(ft, ci)
                        eng.wait_ge(s["up_done"], 2 * (FT * e + ft) + ci + 1)
                        e0, f0, there = earlier(e, ft, 2)
                        if there:
                            eng.wait_ge(*lo_count(e0, f0, ci))
                        eng.activation(h32[:, hs, :], ps[:, hs, :], ACT.Relu,
                                       bias=b1cur[:, slot, ft:ft + 1]).then_inc(s["h32_ready"], 1)
                    if fixed(e) and (e, ft) == (0, 0):
                        eng.wait_ge(s["pevac_d"], len(PREP) // 2)
                        eng.activation(uscr[:], VOT[:, 0, :], ACT.Copy, scale=1.0 / S, accum_out=usum[:, 0:1]).then_inc(
                            s["usum_ready"], 1)
                        eng.wait_ge(s["usum_ready"], 1)
                        eng.activation(uscr[:], VOT[:, 1, :], ACT.Copy, scale=1.0 / S, accum_out=usum[:, 1:2]).then_inc(
                            s["usum_ready"], 1)
                    if fixed(e) and (e, ft) == (0, 1):
                        eng.wait_ge(s["lgsub_ready"], 1)
                        eng.activation(pr[:], lg[:], ACT.Exp).then_inc(s["lgexp_ready"], 1)
                    if fixed(e) and (e, ft) == (1, 0):
                        for i in range(2):
                            eng.wait_ge(s["gt_ready"], i + 1)
                            eng.activation(gateT[:, i * 512:(i + 1) * 512], ps[0:E, 6 + i, :], ACT.Copy).then_inc(
                                s["gt_evac"], 1)
                    if ft == 2 and (1 <= e < E - 1 if fixed(e) else True):
                        split_high(e + 1, 1 - slot)

            expert(0, 0)
            expert(1, 1)
            with eng.Fori(2, E - 3, 2) as e:
                for slot in range(2):
                    expert(e + slot, slot)
            expert(E - 2, 0)
            expert(E - 1, 1)

            for v, (b, j0, nj) in enumerate(VOU):
                eng.wait_ge(s["vo_ready"], v + 1)
                full = min(nj, HS // P - j0)
                last = eng.activation(VO[:, b, j0:j0 + full, :].rearrange("p j d -> p (j d)"), ps[:, VOB[v % 2], 0:full * P],
                                      ACT.Copy)
                if full < nj:
                    w = HS % P
                    last = eng.activation(VO[0:w, b, j0 + full, :], ps[0:w, VOB[v % 2], full * P:(full + 1) * P], ACT.Copy)
                last.then_inc(s["vo_evac"], 1)
                if v == 1:
                    eng.wait_ge(s["xt_ready"], 4)
                    eng.activation(xT[:, 0:2 * P], ps[:, 5, 0:2 * P], ACT.Copy).then_inc(s["xt_evac"], 1)
            eng.wait_ge(s["nmx1_ready"], 1)
            for h in range(H1):
                last = eng.activation(PR[:, 0, h * S:(h + 1) * S], SC[:, 0, h, :], ACT.Exp, bias=nmx1[:, 0, h:h + 1],
                                      accum_out=se1[:, 0, h:h + 1])
            last.then_inc(s["exp1_ready"], 1)
            eng.wait_ge(s["nmx1_ready"], 2)
            eng.activation(PR[:, 1, :], SC[:, 1, :, :].rearrange("p h s -> p (h s)"), ACT.Exp).then_inc(s["exp1_ready"], 1)
            for b in range(B):
                eng.wait_ge(s["pt_ready"], b + 1)
                if b == 1:
                    eng.wait_ge(s["pv1_ready"], 1)
                eng.activation(PT[:, 0:4, :].rearrange("p j d -> p (j d)"), ps[:, 2, :], ACT.Copy)
                eng.activation(PT[:, 8, :], ps[:, 4, 0:P], ACT.Copy)
                w = HS % P
                eng.activation(PT[0:w, 9, :], ps[0:w, 4, P:2 * P], ACT.Copy).then_inc(s["pt_evac_a"], 1)
            eng.wait_ge(s["wq_ready"], 1)
            for n in range(2):
                eng.activation(wguT[:, n, :, :].rearrange("p t d -> p (t d)"), ps[:, 6 + n, 0:IT * P], ACT.Copy, bias=-MAGIC)
            eng.activation(wdT[:, 0:2, :].rearrange("p t d -> p (t d)"), ps[:, 5, 0:2 * P], ACT.Copy, bias=-MAGIC)
            eng.activation(wdT[0:ILAST, 2, :], ps[0:ILAST, 5, 2 * P:3 * P], ACT.Copy, bias=-MAGIC).then_inc(s["wq_evac"], 1)
            eng.wait_ge(s["sd_ready"], 1)
            eng.activation(sdg[:], ps[:, 5, 3 * P:4 * P], ACT.Copy, scale=gth[:, 3:4]).then_inc(s["sd_evac"], 1)

            eng.wait_ge(s["sxi_ready"], 1)
            eng.activation(xn[:, 4:8, :], xn[:, 4:8, :], ACT.Copy, scale=sxi[:], bias=MAGIC).then_inc(s["qf_a"], 1)
            for u in range(2 * IT):
                half, it = divmod(u, IT)
                rows = P if it < 2 else ILAST
                eng.wait_ge(s["gu_ready"], u + 1)
                if u >= 2:
                    eng.wait_ge(s["h_ready"], u - 1)
                eng.activation(sl[0:rows, u % 2, :], ps[0:rows, 2 * (u % 3) + GUB, :], ACT.Silu,
                               scale=gsx[0:rows, it:it + 1]).then_inc(s["sl_ready"], 1)
            eng.wait_ge(s["shi_ready"], 1)
            for half in range(2):
                for it in range(IT):
                    rows = P if it < 2 else ILAST
                    hv = hq[0:rows, it, half * 512:(half + 1) * 512]
                    eng.activation(hv, hv, ACT.Copy, scale=shi[0:rows, :], bias=MAGIC).then_inc(s["hqf_ready"], 1)

        @block.tensor
        def _(eng):
            def tr(dst, src, n=P):
                return eng.transpose(dst, src, ident[0:n, 0:n])

            def mm(dst, lhsT, rhs, start=True, stop=True):
                return eng.matmul(dst, lhsT, rhs, start=start, stop=stop)

            eng.wait_ge(s["early_loaded"], 16)
            mm(ps[:, 7, 0:B * S], wkT2, ctxT)
            mm(ps[:, 7, B * S:2 * B * S], wvT, ctxT).then_inc(s["kv0_ready"], 1)
            for b in range(B):
                mm(ps[0:S, 5, b * 256:b * 256 + P], ctxT[:, b * S:(b + 1) * S], wvT)
            eng.wait_ge(s["kv0_evac"], 1)
            for h in range(2):
                mm(ps[:, 6 + h, 0:B * S], wq0_sb[h * HD:(h + 1) * HD, :], kv0T[h * HD:(h + 1) * HD, 0, :])
            for b in range(B):
                last = mm(ps[0:S, 5, b * 256 + P:b * 256 + 2 * P], kv0T[:, 1, b * S:(b + 1) * S], woT)
            last.then_inc(s["a0_ready"], 1)

            eng.wait_ge(s["pool_const"], 1)

            def transposes(c, bank, n):
                eng.wait_ge(s["xn_ready"], n)
                for j in range(CH_NT[c]):
                    last = tr(ps[:, bank, j * P:(j + 1) * P], xn[:, CH_T0[c] + j, :])
                return last

            def batch(c, j):
                return j if c == 0 else c - 1

            def scores(c):
                eng.wait_ge(s["xt_evac"], c + 1)
                for j in range(CH_NT[c]):
                    t = CH_T0[c] + j
                    last = mm(ps[:, 3 + c, j * 2 * S:(j + 1) * 2 * S], xT[:, t * P:(t + 1) * P],
                              A0[:, batch(c, j), :, :].rearrange("p h s -> p (h s)"))
                last.then_inc(s["sc0_ready"], 1)

            def attend(c):
                eng.wait_ge(s["w_ready"], c + 1)
                for j in range(CH_NT[c]):
                    last = tr(ps[0:S, c, j * P:(j + 1) * P], Wt[:, CH_T0[c] + j, :])
                last.then_inc(s["wt_ready"], 1)
                eng.wait_ge(s["wt_evac"], c + 1)
                for a in range(2):
                    for j in range(CH_NT[c]):
                        last = mm(ps[:, PVB[c][a], j * P:(j + 1) * P], wT[:, CH_T0[c] + j, :], VV[:, batch(c, j), a, :])
                last.then_inc(s["pv_ready"], 1)

            def prep(lo, hi):
                for u in range(lo, hi):
                    kind, n0, cnt, par = PREP[u]
                    if u == 0:
                        eng.wait_ge(s["l1wa_loaded"], 16)
                    if u == PREP_FIRST["vT"]:
                        eng.wait_ge(s["l1wb_loaded"], 16)
                    if u in (PREP_FIRST["A"], PREP_FIRST["VOT"]):
                        eng.wait_ge(s["pevac_a"], (u + 1) // 2)
                        eng.wait_ge(s["pevac_d"], u // 2)
                    elif u >= 2:
                        eng.wait_ge(s["pevac_a" if u % 2 == 0 else "pevac_d"], (u - 2) // 2 + 1)
                    for m in range(cnt):
                        i = n0 + m
                        dst = ps[:, 6 + u % 2, m * B * S:(m + 1) * B * S]
                        rows = slice(par * DH, (par + 1) * DH)
                        if kind in ("kT", "vT"):
                            o = (INNER if kind == "vT" else 0) + i * P
                            last = mm(dst, wkv1_sb[:, o:o + P], ctxT)
                        elif kind == "A":
                            last = mm(dst, wq1T[rows, i, :], kT1[rows, i, :])
                        else:
                            last = mm(dst, wo1_sb[rows, i, :], vT1[rows, i, :])
                    last.then_inc(s["prep_ready"], 1)

            for c in range(3):
                transposes(c, c, c + 1).then_inc(s["xt_ready"], 1)
            eng.wait_ge(s["a0_evac_a"], 1)
            eng.wait_ge(s["a0_evac_d"], 1)
            scores(0)
            scores(1)
            eng.wait_ge(s["vv_evac"], 1)
            scores(2)
            prep(0, 3)
            attend(0)
            prep(3, 5)
            attend(1)
            prep(5, 7)
            attend(2)
            prep(7, 12)
            eng.wait_ge(s["x1_ready"], 1)
            transposes(0, X2B[0], 4).then_inc(s["x2t_ready"], 1)
            prep(12, 15)
            transposes(1, X2B[1], 5).then_inc(s["x2t_ready"], 1)
            prep(15, 18)
            transposes(2, X2B[2], 6).then_inc(s["x2t_ready"], 1)

            def up(e, ft, slot):
                if ft == 0:
                    eng.wait_ge(s["w1_split"], e + 1)
                if fixed(e) and e == 0 and ft < 2:
                    eng.wait_ge(s["x1_ready"], 3)
                    eng.wait_ge(s["xlo_ready"], 3)
                    if ft == 1:
                        eng.wait_ge(s["xt2_evac"], 3)
                e0, f0, there = earlier(e, ft, 2)
                if there:
                    eng.wait_ge(s["h32_ready"], 2 * (FT * e0 + f0 + 1))
                wh, wl = w1hi[:, slot, ft * P:(ft + 1) * P], w1lo[:, slot, ft * P:(ft + 1) * P]
                for ci in range(2):
                    t = slice(ci * 512, (ci + 1) * 512)
                    dst = ps[:, h_slot(ft, ci), :]
                    mm(dst, wh, xhi[:, t], True, False)
                    mm(dst, wh, xlo[:, t], False, False)
                    mm(dst, wl, xhi[:, t], False, True).then_inc(s["up_done"], 1)

            def down(e, ft, slot):
                if ft == 0:
                    eng.wait_ge(s["w2_split"], e + 1)
                    if not fixed(e) or e >= 2:
                        eng.wait_ge(s["y_mul"], 2 * (e - 1))
                    if fixed(e) and e == 1:
                        eng.wait_ge(s["gt_evac"], 2)
                wh, wl = w2hi[:, slot, ft * D:(ft + 1) * D], w2lo[:, slot, ft * D:(ft + 1) * D]
                for ci in range(2):
                    hs = h_slot(ft, ci)
                    dst = ps[:, y_bank(slot, ci), :]
                    eng.wait_ge(*lo_count(e, ft, ci))
                    mm(dst, wh, hhi[:, hs, :], ft == 0, False)
                    mm(dst, wh, hlo[:, hs, :], False, False)
                    mm(dst, wl, hhi[:, hs, :], False, ft == FT - 1).then_inc(s["down_done"], 1)

            def expert(e, slot):
                for ft in range(FT):
                    up(e, ft, slot)
                    e0, f0, there = earlier(e, ft, LAG)
                    if there:
                        down(e0, f0, slot if ft >= LAG else 1 - slot)
                    if fixed(e) and (e, ft) == (0, 1):
                        for t in range(NTILE):
                            last = mm(ps[:, 7, t * E:(t + 1) * E], xT[:, t * P:(t + 1) * P], wr_sb)
                        last.then_inc(s["logit_ready"], 1)
                        eng.wait_ge(s["usum_ready"], 2)
                        for b in range(B):
                            last = mm(ps[:, 6, b * P:(b + 1) * P], usum[:, b:b + 1].broadcast_to([P, P]), ident[:])
                        last.then_inc(s["u_ready"], 1)
                    if fixed(e) and (e, ft) == (1, 0):
                        eng.wait_ge(s["gate_ready"], 1)
                        for t in range(NTILE):
                            last = tr(ps[0:E, 6 + t // 4, (t % 4) * P:(t % 4 + 1) * P], gate[:, t, :])
                            if t % 4 == 3:
                                last.then_inc(s["gt_ready"], 1)

            expert(0, 0)
            expert(1, 1)
            with eng.Fori(2, E - 1, 2) as e:
                for slot in range(2):
                    expert(e + slot, slot)
            for back in range(LAG, 0, -1):
                down(E - 1, FT - back, 1)
            for half in range(2):
                eng.wait_ge(s["y_done"], 2 * (E - 1) + half + 1)
                for j in range(4):
                    t = 4 * half + j
                    last = tr(ps[:, 2 + half, j * P:(j + 1) * P], acc[:, t * P:(t + 1) * P])
                last.then_inc(s["acct_ready"], 1)

            def vo(lo, hi):
                for v in range(lo, hi):
                    b, j0, nj = VOU[v]
                    if v >= 2:
                        eng.wait_ge(s["vo_evac"], v - 1)
                    for m in range(nj):
                        w = min(P, HS - (j0 + m) * P)
                        last = tr(ps[0:w, VOB[v % 2], m * P:(m + 1) * P], VOT[:, b, (j0 + m) * P:(j0 + m) * P + w])
                    last.then_inc(s["vo_ready"], 1)

            vo(0, 2)
            transposes(0, 5, 7).then_inc(s["xt_ready"], 1)
            eng.wait_ge(s["xt_evac"], 4)
            eng.wait_ge(s["x2_ready"], 3)
            for b in range(B):
                if b == 1:
                    vo(2, 3)
                for gi, (h0, nh) in enumerate(HG):
                    mm(ps[:, SCB[b][gi], 0:nh * S], xT[:, b * P:(b + 1) * P],
                       A1[:, b, h0:h0 + nh, :].rearrange("p h s -> p (h s)")).then_inc(s["sc1_ready"], 1)
            vo(3, 6)
            eng.wait_ge(s["wqf_ready"], 1)
            eng.wait_ge(s["sc1_masked"], 6)
            for n in range(2):
                for t in range(IT):
                    c = n * IT + t
                    tr(ps[:, 6 + n, t * P:(t + 1) * P], wqf[:, c * D:(c + 1) * D])
            eng.wait_ge(s["vo_evac"], 6)
            for t in range(IT):
                w = P if t < 2 else ILAST
                last = tr(ps[0:w, 5, t * P:(t + 1) * P], wqf[:, 6 * D + t * P:6 * D + t * P + w])
            last.then_inc(s["wq_ready"], 1)
            mm(ps[:, 5, 3 * P:4 * P], wsc[:, 6:7].broadcast_to([P, P]), ident[:]).then_inc(s["sd_ready"], 1)
            for b in range(B):
                eng.wait_ge(s["pr_ready"], b + 1)
                if b == 1:
                    eng.wait_ge(s["pt_evac_a"], 1)
                    eng.wait_ge(s["pt_evac_d"], 1)
                for j in range(NB):
                    w = min(P, HS - j * P)
                    last = tr(ps[0:w, 2 + j // 4, (j % 4) * P:(j % 4 + 1) * P], PR[:, b, j * P:j * P + w])
                last.then_inc(s["pt_ready"], 1)
                eng.wait_ge(s["pt_evac_a"], b + 1)
                eng.wait_ge(s["pt_evac_d"], b + 1)
                for j in range(NB):
                    w = min(P, HS - j * P)
                    last = mm(ps[:, b, 0:P], PT[0:w, j, :], VO[0:w, b, j, :], j == 0, j == NB - 1)
                last.then_inc(s["pv1_ready"], 1)

            eng.wait_ge(s["wq_evac"], 1)
            eng.wait_ge(s["sd_evac"], 1)
            eng.wait_ge(s["x3_ready"], B)
            for half in range(2):
                eng.wait_ge(s["qf_d" if half == 0 else "qf_a"], 1)
                for j in range(4):
                    last = tr(ps[:, half, j * P:(j + 1) * P], xn[:, 4 * half + j, :])
                last.then_inc(s["qt_ready"], 1)
            for u in range(2 * IT):
                half, it = divmod(u, IT)
                rows = P if it < 2 else ILAST
                eng.wait_ge(s["q_ready"], half + 1)
                if u >= 3:
                    eng.wait_ge(s["h_ready"], u - 2)
                for n in range(2):
                    last = mm(ps[0:rows, 2 * (u % 3) + GUB + n, :], wguT[:, n, it, 0:rows], qT[:, half * 512:(half + 1) * 512])
                last.then_inc(s["gu_ready"], 1)
            for half in range(2):
                eng.wait_ge(s["hqb_ready"], IT * (half + 1))
                for t in range(4 * half, 4 * half + 4):
                    for it in range(IT):
                        rows = P if it < 2 else ILAST
                        last = mm(ps[:, half, (t % 4) * P:(t % 4 + 1) * P], hqb[0:rows, it, t * P:(t + 1) * P],
                                  wdT[0:rows, it, :], it == 0, it == IT - 1)
                last.then_inc(s["dn_ready"], 1)

        @block.vector
        def _(eng):
            steps = [0]

            def step(ins):
                steps[0] += 1
                ins.then_inc(s["dve_step"], 1)
                return steps[0]

            def after(n):
                eng.wait_ge(s["dve_step"], n)

            def norm_stats(c):
                t0, nt = CH_T0[c], CH_NT[c]
                for j in range(t0, t0 + nt):
                    last = eng.bn_stats(stats[:, j, :], xs[:, j, :])
                after(step(last))
                for j in range(t0, t0 + nt):
                    last = eng.bn_aggr(mv[:, j, :], stats[:, j, :])
                after(step(last))
                eng.tensor_scalar(ve[:, t0:t0 + nt], mv[:, t0:t0 + nt, 1], EPS, None, ALU.add).then_inc(s["ve_ready"], 1)

            def normalise(c, n):
                eng.wait_ge(s["rstd_ready"], n)
                for j in range(CH_T0[c], CH_T0[c] + CH_NT[c]):
                    last = eng.tensor_scalar(xn[:, j, :], xs[:, j, :], mv[:, j, 0:1], rstd[:, j:j + 1],
                                             ALU.subtract, ALU.mult)
                return last

            for c in range(3):
                eng.wait_ge(s[f"x_loaded{c}"], 16)
                norm_stats(c)
            for c in range(2):
                normalise(c, c + 1).then_inc(s["xn_ready"], 1)
            eng.wait_ge(s["late_loaded"], 16)
            after(step(eng.tensor_tensor(lam_pr[:], lam_in[:, 0:2, :], lam_in[:, 2:4, :], ALU.mult)))
            eng.tensor_reduce(lam_s[:], lam_pr[:], AX, ALU.add).then_inc(s["lam_summed"], 1)
            eng.wait_ge(s["tanh_ready"], 1)
            eng.tensor_scalar(sig127[:], gth[:, 4:6], 0.5 / QMAX, 0.5 / QMAX, ALU.mult, ALU.add)
            tbo_step = step(eng.tensor_scalar(tbo[:], bo_bc, gth[:, 1:2], None, ALU.mult))
            eng.tensor_scalar(tgli[:], gth[:, 0:1], 1.0 - LAMBDA_INIT, None, ALU.mult).then_inc(s["tgli_ready"], 1)
            eng.wait_ge(s["a0_ready"], 1)
            eng.tensor_scalar(A0[:, :, 1, :], ps[:, 7, 0:B * S].rearrange("p (b s) -> p b s", b=B), HD ** -0.5, None,
                              ALU.mult).then_inc(s["a0_evac_d"], 1)
            normalise(2, 3).then_inc(s["xn_ready"], 1)

            def row_max(c):
                nt = CH_NT[c]
                eng.wait_ge(s["sc0_ready"], c + 1)
                eng.tensor_reduce(nmx0[:, 2 * CH_T0[c]:2 * (CH_T0[c] + nt)],
                                  ps[:, 3 + c, 0:nt * 2 * S].rearrange("p (h s) -> p h s", s=S), AX, ALU.max,
                                  negate=True).then_inc(s["nmx0_ready"], 1)

            def weights(c):
                t0, nt = CH_T0[c], CH_NT[c]
                eng.wait_ge(s["exp0_ready"], c + 1)
                after(step(eng.reciprocal(rc0[:, 2 * t0:2 * (t0 + nt)], se0[:, 2 * t0:2 * (t0 + nt)])))
                ev = E0[:, t0:t0 + nt, :, :].rearrange("p t h s -> p (t h) s")
                after(step(eng.tensor_tensor(ev, ev, rc0[:, 2 * t0:2 * (t0 + nt)].unsqueeze(2).broadcast_to([P, 2 * nt, S]),
                                             ALU.mult)))
                eng.scalar_tensor_tensor(Wt[:, t0:t0 + nt, :], E0[:, t0:t0 + nt, 1, :], nlam[:],
                                         E0[:, t0:t0 + nt, 0, :], ALU.mult, ALU.add).then_inc(s["w_ready"], 1)

            def residual1(c):
                eng.wait_ge(s["rms_ready"], c + 1)
                for j in range(CH_NT[c]):
                    t = CH_T0[c] + j
                    last = eng.scalar_tensor_tensor(xs[:, t, :], ps[:, PVB[c][1], j * P:(j + 1) * P], rms[:, t:t + 1],
                                                    xs[:, t, :], ALU.mult, ALU.add)
                last.then_inc(s["x1_ready"], 1)
                eng.wait_ge(s["x1_ready"], c + 1)
                norm_stats(c)

            row_max(0)
            row_max(1)
            eng.wait_ge(s["lam_exp"], 1)
            after(step(eng.tensor_tensor(nlam[:], lam_e[:, 1:2], lam_e[:, 0:1], ALU.subtract)))
            after(step(eng.tensor_scalar(nlam[:], nlam[:], LAMBDA_INIT, None, ALU.subtract)))
            weights(0)
            row_max(2)
            prep_evacs(eng, 1, 0, 3)
            weights(1)
            prep_evacs(eng, 1, 3, 5)
            weights(2)
            prep_evacs(eng, 1, 5, 7)
            residual1(0)
            residual1(1)
            normalise(0, 4).then_inc(s["xn_ready"], 1)
            residual1(2)
            normalise(1, 5).then_inc(s["xn_ready"], 1)
            prep_evacs(eng, 1, 7, 12)

            def low_input(c):
                t0, w = tok(c)
                eng.wait_ge(s["xhi_ready"], c + 1)
                eng.tensor_tensor(xlo[:, t0:t0 + w], ps[:, X2B[c], 0:w], xhi[:, t0:t0 + w].bitcast(F32),
                                  ALU.subtract).then_inc(s["xlo_ready"], 1)

            normalise(2, 6).then_inc(s["xn_ready"], 1)
            prep_evacs(eng, 1, 12, 18)
            for c in range(3):
                low_input(c)

            pk = pr[:].unsqueeze(2).broadcast_to([P, NTILE, E, E])
            pe_ = pr[:].unsqueeze(3).broadcast_to([P, NTILE, E, E])

            def router(part):
                if part == 1:
                    eng.wait_ge(s["logit_ready"], 1)
                    after(step(eng.tensor_tensor(lg[:], ps[:, 7, 0:NTILE * E].rearrange("p (t e) -> p t e", e=E),
                                                 br_bc.unsqueeze(1).broadcast_to([P, NTILE, E]), ALU.add)))
                    after(step(eng.tensor_reduce(lmx[:], lg[:], AX, ALU.max)))
                    eng.tensor_tensor(lg[:], lg[:], lmx[:].unsqueeze(2).broadcast_to([P, NTILE, E]),
                                      ALU.subtract).then_inc(s["lgsub_ready"], 1)
                if part == 2:
                    eng.wait_ge(s["lgexp_ready"], 1)
                    after(step(eng.tensor_reduce(lsum[:], pr[:], AX, ALU.add)))
                    after(step(eng.reciprocal(lmx[:], lsum[:])))
                    after(step(eng.tensor_tensor(pr[:], pr[:], lmx[:].unsqueeze(2).broadcast_to([P, NTILE, E]), ALU.mult)))
                    eng.wait_ge(s["pool_const"], 2)
                    after(step(eng.tensor_tensor(dif[:], pk, pe_, ALU.subtract)))
                    after(step(eng.tensor_tensor(dif[:], dif[:], tie[:].unsqueeze(1).broadcast_to([P, NTILE, E, E]),
                                                 ALU.is_gt)))
                if part == 3:
                    after(step(eng.tensor_tensor(dif[:], dif[:], pk, ALU.mult)))
                    after(step(eng.tensor_reduce(cum[:], dif[:], AX, ALU.add)))
                    after(step(eng.tensor_tensor(lone[:], cum[:], pr[:], ALU.is_le)))
                    after(step(eng.scalar_tensor_tensor(cum[:], cum[:], TOP_P, lone[:], ALU.is_lt, ALU.max)))
                    eng.tensor_tensor(gate[:], cum[:], pr[:], ALU.mult).then_inc(s["gate_ready"], 1)

            def bias_of(e, slot):
                eng.tensor_scalar(b1cur[:, slot, :], b1T[:, bass.ds(FT * e, FT)], 1.0, None, ALU.mult).then_inc(
                    s["b1_ready"], 1)

            def expert(e, slot):
                for ft in range(FT):
                    for ci in range(2):
                        hs = h_slot(ft, ci)
                        n = 2 * (FT * e + ft) + ci + 1
                        eng.wait_ge(s["h32_ready"], n)
                        e0, f0, there = earlier(e, ft, 2)
                        if there:
                            eng.wait_ge(s["down_done"], 2 * (FT * e0 + f0) + ci + 1)
                        eng.tensor_copy(hhi[:, hs, :], h32[:, hs, :]).then_inc(s["hi_ready"], 1)
                        if (ft, ci) not in POOL_LO:
                            eng.wait_ge(s["hi_ready"], n)
                            eng.tensor_tensor(hlo[:, hs, :], h32[:, hs, :], hhi[:, hs, :].bitcast(F32),
                                              ALU.subtract).then_inc(s["lo_dve"], 1)
                    if ft == 2 and (1 <= e < E - 1 if fixed(e) else True):
                        bias_of(e + 1, 1 - slot)
                    if ft == (3 if fixed(e) and e == 1 else 2) and not (fixed(e) and e == 0):
                        take_y(e - 1, 1 - slot)
                    if fixed(e) and e == 0:
                        router(ft)
                        if ft == 2:
                            for b in range(B):
                                eng.wait_ge(s["u_ready"], 1)
                                eng.scalar_tensor_tensor(urow[:, b, :], ps[:, 6, b * P:(b + 1) * P], gth[:, 1:2], tbo[:],
                                                         ALU.mult, ALU.add).then_inc(s["urow_ready"], 1)
                    if fixed(e) and (e, ft) == (1, 1):
                        eng.wait_ge(s["ffnw_loaded"], 16)
                        eng.tensor_reduce(wmx[:, 0:6], wf_raw[:, 0:6 * D].rearrange("p (c d) -> p c d", d=D), AX, ALU.max,
                                          apply_absolute_value=True)
                        after(step(eng.tensor_reduce(wmx[:, 6:7], wf_raw[:, 6 * D:], AX, ALU.max, apply_absolute_value=True)))
                        after(step(eng.tensor_scalar(wsc[:], wmx[:], 1.0 / QMAX, None, ALU.mult)))
                        eng.reciprocal(winv[:], wsc[:]).then_inc(s["wmx_ready"], 1)

            def take_y(e, slot):
                eng.wait_ge(s[f"g_loaded{slot}"], 8 * (e - slot) + 16)
                for ci in range(2):
                    t = slice(ci * 512, (ci + 1) * 512)
                    eng.wait_ge(s["down_done"], 2 * (FT * e + FT - 1) + ci + 1)
                    if not fixed(e) or e >= 1:
                        eng.wait_ge(s["y_done"], 2 * (e - 1) + ci + 1)
                    eng.scalar_tensor_tensor(ytmp[:, ci, :], ps[:, y_bank(slot, ci), :], b2T[:, bass.ds(e, 1)],
                                             G[:, slot, t], ALU.add, ALU.mult).then_inc(s["y_mul"], 1)
                    eng.wait_ge(s["y_mul"], 2 * e + ci + 1)
                    eng.tensor_tensor(acc[:, t], acc[:, t], ytmp[:, ci, :], ALU.add).then_inc(s["y_done"], 1)

            eng.wait_ge(s["acc_zero"], 1)
            bias_of(0, 0)
            bias_of(1, 1)
            expert(0, 0)
            expert(1, 1)
            with eng.Fori(2, E - 3, 2) as e:
                for slot in range(2):
                    expert(e + slot, slot)
            expert(E - 2, 0)
            expert(E - 1, 1)
            take_y(E - 1, 1)

            eng.wait_ge(s["row_added"], 2)
            for n, (t0, t1) in enumerate(((0, 2), (2, 4), (4, 8))):
                eng.wait_ge(s["acct_ready"], 1 if t1 <= 4 else 2)
                eng.scalar_tensor_tensor(xs[:, t0:t1, :], ps[:, 2 + t0 // 4, (t0 % 4) * P:(t0 % 4 + t1 - t0) * P].rearrange(
                    "p (t d) -> p t d", d=D), gth[:, 2:3], xs[:, t0:t1, :], ALU.mult, ALU.add).then_inc(s["x2_ready"], 1)
                if n == 0:
                    eng.wait_ge(s["x2_ready"], 1)
                    norm_stats(0)
            eng.wait_ge(s["x2_ready"], 3)
            norm_stats(1)
            normalise(0, 7).then_inc(s["xn_ready"], 1)
            norm_stats(2)
            eng.wait_ge(s["xn_ready"], 7)
            x2b = step(eng.tensor_tensor(xs[:, 0:2, :], xs[:, 0:2, :], tbo[:].unsqueeze(1).broadcast_to([P, 2, D]), ALU.add))

            eng.wait_ge(s["mask_ready"], 1)

            def masked(b):
                for gi, (h0, nh) in enumerate(HG):
                    eng.wait_ge(s["sc1_ready"], 3 * b + gi + 1)
                    eng.tensor_tensor(SC[:, b, h0:h0 + nh, :], ps[:, SCB[b][gi], 0:nh * S].rearrange("p (h s) -> p h s", s=S),
                                      maskadd[:, b, :].unsqueeze(1).broadcast_to([P, nh, S]), ALU.add).then_inc(
                        s["sc1_masked"], 1)
                eng.wait_ge(s["sc1_masked"], 3 * b + 3)

            def heads(t):
                return t.unsqueeze(2).broadcast_to([P, H1, S])

            masked(0)
            eng.tensor_reduce(nmx1[:, 0, :], SC[:, 0, :, :], AX, ALU.max, negate=True).then_inc(s["nmx1_ready"], 1)
            masked(1)
            after(step(eng.tensor_reduce(nmx1[:, 1, :], SC[:, 1, :, :], AX, ALU.max)))
            eng.tensor_tensor(SC[:, 1, :, :], SC[:, 1, :, :], heads(nmx1[:, 1, :]), ALU.subtract).then_inc(s["nmx1_ready"], 1)
            normalise(1, 8)
            after(step(normalise(2, 9)))
            n_xmx = step(eng.tensor_reduce(xmx[:, 0:1], xn[:, 2:8, :], mybir.AxisListType.XY, ALU.max,
                                           apply_absolute_value=True))
            for b in range(B):
                prv = PR[:, b, :].rearrange("p (h s) -> p h s", s=S)
                eng.wait_ge(s["exp1_ready"], b + 1)
                if b == 1:
                    after(step(eng.tensor_reduce(se1[:, 1, :], prv, AX, ALU.add)))
                after(step(eng.reciprocal(rc1[:, b, :], se1[:, b, :])))
                eng.tensor_tensor(prv, prv, heads(rc1[:, b, :]), ALU.mult).then_inc(s["pr_ready"], 1)
            after(x2b)
            for b in range(B):
                eng.wait_ge(s["pt_ready"], b + 1)
                if b == 1:
                    eng.wait_ge(s["pv1_ready"], 1)
                eng.tensor_copy(PT[:, 4:8, :].rearrange("p j d -> p (j d)"), ps[:, 3, :]).then_inc(s["pt_evac_d"], 1)
                eng.wait_ge(s["pv1_ready"], b + 1)
                eng.scalar_tensor_tensor(xs[:, b, :], ps[:, b, 0:P], gth[:, 1:2], xs[:, b, :], ALU.mult, ALU.add).then_inc(
                    s["x3_ready"], 1)
            eng.wait_ge(s["x3_ready"], B)
            norm_stats(0)
            after(step(normalise(0, 10)))

            after(n_xmx)
            eng.tensor_reduce(xmx[:, 1:2], xn[:, 0:2, :], mybir.AxisListType.XY, ALU.max, apply_absolute_value=True).then_inc(
                s["xmx_ready"], 1)
            eng.wait_ge(s["xmxa_ready"], 1)
            after(step(eng.scalar_tensor_tensor(sx[:], xmxa[:, 0:1], xmxa[:, 1:2], sig127[:, 0:1], ALU.max, ALU.mult)))
            eng.reciprocal(sxi[:], sx[:]).then_inc(s["sxi_ready"], 1)
            eng.wait_ge(s["sxi_ready"], 1)
            eng.tensor_scalar(xn[:, 0:4, :], xn[:, 0:4, :], sxi[:], MAGIC, ALU.mult, ALU.add).then_inc(s["qf_d"], 1)
            eng.tensor_scalar(gsx[:], wsc[:, 0:6], sx[:], None, ALU.mult)
            eng.memset(hmx[:], 0.0)
            for half in range(2):
                eng.wait_ge(s["qt_ready"], half + 1)
                q = qT[:, half * 512:(half + 1) * 512]
                after(step(eng.tensor_scalar(q, ps[:, half, :], MAGIC, QMAX, ALU.subtract, ALU.min)))
                eng.tensor_scalar(q, q, -QMAX - 1.0, None, ALU.max).then_inc(s["q_ready"], 1)
            for u in range(2 * IT):
                half, it = divmod(u, IT)
                rows = P if it < 2 else ILAST
                hv = hq[0:rows, it, half * 512:(half + 1) * 512]
                eng.wait_ge(s["sl_ready"], u + 1)
                eng.scalar_tensor_tensor(hv, ps[0:rows, 2 * (u % 3) + GUB + 1, :], gsx[0:rows, 3 + it:4 + it],
                                         sl[0:rows, u % 2, :], ALU.mult, ALU.mult).then_inc(s["h_ready"], 1)
                eng.wait_ge(s["h_ready"], u + 1)
                n = step(eng.tensor_reduce(hmx[0:rows, u:u + 1], hv, AX, ALU.max, apply_absolute_value=True))
            after(n)
            eng.tensor_reduce(hmxr[:], hmx[:], AX, ALU.max).then_inc(s["hmx_ready"], 1)
            eng.wait_ge(s["hmxa_ready"], 1)
            after(step(eng.tensor_tensor(sh[:], hmxa[:], sig127[:, 1:2], ALU.mult)))
            eng.reciprocal(shi[:], sh[:]).then_inc(s["shi_ready"], 1)
            eng.wait_ge(s["sd_evac"], 1)
            sd_step = step(eng.tensor_scalar(sdgs[:], sdg[:], sh[:], None, ALU.mult))
            for half in range(2):
                for it in range(IT):
                    rows = P if it < 2 else ILAST
                    t = slice(half * 512, (half + 1) * 512)
                    eng.wait_ge(s["hqf_ready"], IT * half + it + 1)
                    after(step(eng.tensor_scalar(hqb[0:rows, it, t], hq[0:rows, it, t], MAGIC, QMAX, ALU.subtract, ALU.min)))
                    eng.tensor_scalar(hqb[0:rows, it, t], hqb[0:rows, it, t], -QMAX - 1.0, None, ALU.max).then_inc(
                        s["hqb_ready"], 1)
            after(sd_step)
            for half in range(2):
                eng.wait_ge(s["dn_ready"], half + 1)
                o = otmp[:, 4 * half:4 * half + 4, :]
                eng.tensor_tensor(o, ps[:, half, :].rearrange("p (t d) -> p t d", d=D),
                                  sdgs[:].unsqueeze(1).broadcast_to([P, 4, D]), ALU.mult).then_inc(s["o_ready"], 1)
            eng.wait_ge(s["o_ready"], 2)
            eng.tensor_tensor(xs[:, 4:8, :], xs[:, 4:8, :], otmp[:, 4:8, :], ALU.add).then_inc(s["out_ready_d"], 1)


def kernel(**inputs):
    import numpy as _np
    import concourse.bacc as _bacc
    from concourse import mybir as _mybir
    from concourse.bass_utils import run_bass_kernel_spmd as _run

    a = {k: _np.asarray(v) for k, v in inputs.items()}

    def rows(v):
        v = v.reshape(1, -1)
        return _np.broadcast_to(v, (P, v.shape[1]))

    def tiles(w):
        return w.reshape(-1, P, w.shape[1]).transpose(1, 0, 2).reshape(P, -1)

    def padded(w):
        return tiles(_np.concatenate([w, _np.ones((IT * P - I, D), w.dtype)]))

    early = dict(ctxT=a["ctx_1024"].reshape(B * S, D).T, wkT2=_np.concatenate([a["L0_xattn_Wk"].T] * 2, axis=1),
                 wvT=a["L0_xattn_Wv"].T, woT=a["L0_xattn_Wo"].T, wq=a["L0_xattn_Wq"])
    late = dict(b1T=a["L0_ffn_b1"].reshape(E * FT, P).T, b2T=a["L0_ffn_b2"].T, wr=a["L0_ffn_Wr"],
                gsc=rows(_np.concatenate([a["g_xattn"], a["g_ffn"], a["L1_ffn_clip_x"], a["L1_ffn_clip_down"]])),
                br=rows(a["L0_ffn_br"]), bo=rows(a["L1_xattn_bo"]),
                lam=rows(_np.concatenate([a[f"L0_xattn_lambda_{n}"] for n in ("q1", "q2", "k1", "k2")])))
    experts = _np.concatenate([a["L0_ffn_W1"], a["L0_ffn_W2"].reshape(E, FT, P, D).transpose(0, 2, 1, 3).reshape(E, P, FT * D)],
                              axis=2)
    sent = dict(
        x=a["x"],
        early=_np.concatenate([early[n] for n in EARLY], axis=1),
        late=_np.concatenate([late[n] for n in LATE], axis=1),
        mask=rows(a["mask_BxS2_bk0"]),
        l1w=_np.concatenate([tiles(a["L1_xattn_Wq"].T), a["L1_xattn_Wkv"], tiles(a["L1_xattn_Wo"])], axis=1),
        ffnw=_np.concatenate([padded(a["L1_ffn_w_gate"]), padded(a["L1_ffn_w_up"]), a["L1_ffn_w_down"]], axis=1),
        experts=experts,
    )
    nc = _bacc.Bacc("TRN2", target_bir_lowering=False, num_devices=1)
    arrays, args = {}, []
    for name, v in sent.items():
        v = _np.ascontiguousarray(v)
        arrays[f"in_{name}"] = v
        args.append(nc.dram_tensor(f"in_{name}", v.shape, _mybir.dt.from_np(v.dtype), kind="ExternalInput").ap())
    args.append(nc.dram_tensor("out_0", (B, N, D), F32, kind="ExternalOutput").ap())
    build(nc, *args)
    r = _run(nc, [arrays], core_ids=[0])
    return r.results[0]["out_0"]
```

```python
import math
from contextlib import ExitStack

import concourse.bass as bass
from concourse import mybir

F32 = mybir.dt.float32
F32R = mybir.dt.float32r
BF16 = mybir.dt.bfloat16
U8 = mybir.dt.uint8
ALU = mybir.AluOpType
ACT = mybir.ActivationFunctionType
AX = mybir.AxisListType.X

P = 128
B, N, D = 2, 512, 128
S = 77
T = B * N
NTILE = T // P
HD = D // 2
E, F = 8, 512
FT = F // P
H1, DH = 16, 64
INNER = H1 * DH
NI = INNER // P
HS = H1 * S
NB = -(-HS // P)
I = 352
IT = 3
ILAST = I - 2 * P

LAMBDA_INIT = 0.8 - 0.6 * math.exp(-0.3 * 12)
EPS = 1e-5
TOP_P = 0.8
QMAX = 127.0
MAGIC = 1.5 * 2.0 ** 23
NEG = -3.4028234663852886e38

CH_T0 = [0, 2, 5]
CH_NT = [2, 3, 3]
CAUSAL = S - N + 1
assert (N // P - 1) * P - 1 + CAUSAL <= 0, "rows before the last tile see no context token"

HG = [(0, 6), (6, 6), (12, 4)]
G3 = [(0, 3), (3, 3), (6, 2)]

EARLY = dict(ctxT=B * S, wkT2=2 * HD, wvT=D, woT=D, wq=D)
LATE = dict(b1T=E * FT, b2T=E, wr=E, gsc=6, br=E, bo=D, lam=4 * HD)


def ranges(widths):
    at, found = 0, {}
    for name, w in widths.items():
        found[name] = (at, at + w)
        at += w
    return found, at


def build(nc, x, early, late, mask, l1w_in, ffnw_in, experts, out):
    st = ExitStack()
    with st:
        def sb(name, shape, dt=F32):
            return st.enter_context(nc.sbuf_tensor(name, shape, dt))

        def sem(name):
            return st.enter_context(nc.semaphore(name))

        ps = st.enter_context(nc.psum_tensor("ps", [P, 8, 512], F32))
        gates_dram = nc.dram_tensor("gates_dram", (E, T), F32).ap()

        ident = sb("ident", [P, P])
        tie = sb("tie", [P, E, E])
        mhalf = sb("mhalf", [P, NTILE])
        early_at, early_w = ranges(EARLY)
        late_at, late_w = ranges(LATE)
        early_sb = sb("early_sb", [P, early_w])
        late_sb = sb("late_sb", [P, late_w])

        def of(t, at, name):
            return t[:, at[name][0]:at[name][1]]

        ctxT, wkT2, wvT, woT, wq0_sb = (of(early_sb, early_at, n) for n in EARLY)
        b1T, b2T, wr_sb, gsc, br_bc, bo_bc, lam_flat = (of(late_sb, late_at, n) for n in LATE)
        lam_in = lam_flat.rearrange("p (a d) -> p a d", a=4)
        gth = sb("gth", [P, 6])
        tgli = sb("tgli", [P, 1])
        sig127 = sb("sig127", [P, 2])
        lam_pr = sb("lam_pr", [P, 2, HD])
        lam_s = sb("lam_s", [P, 2])
        lam_e = sb("lam_e", [P, 2])
        nlam = sb("nlam", [P, 1])
        mask_u8 = sb("mask_u8", [P, B, S], U8)
        maskadd = sb("maskadd", [P, B, S])

        xs = sb("xs", [P, NTILE, D])
        xn = sb("xn", [P, NTILE, D])
        stats = sb("stats", [P, NTILE, 6])
        mv = sb("mv", [P, NTILE, 2])
        ve = sb("ve", [P, NTILE])
        rstd = sb("rstd", [P, NTILE])

        kv0T = sb("kv0T", [P, 2, B * S])
        A0 = sb("A0", [P, B, 2, S])
        VV = sb("VV", [S, B, 2, D])
        xT = sb("xT", [P, T])
        nmx0 = sb("nmx0", [P, NTILE * 2])
        se0 = sb("se0", [P, NTILE * 2])
        rc0 = sb("rc0", [P, NTILE * 2])
        ss = sb("ss", [P, NTILE])
        ms = sb("ms", [P, NTILE])
        rms = sb("rms", [P, NTILE])

        xhi = sb("xhi", [P, T], F32R)
        xlo = sb("xlo", [P, T], F32R)
        lg = sb("lg", [P, NTILE, E])
        lmx = sb("lmx", [P, NTILE])
        lsum = sb("lsum", [P, NTILE])
        pr = sb("pr", [P, NTILE, E])
        dif = sb("dif", [P, NTILE, E, E])
        cum = sb("cum", [P, NTILE, E])
        lone = sb("lone", [P, NTILE, E])
        gate = sb("gate", [P, NTILE, E])
        gateT = sb("gateT", [E, T])
        G = sb("G", [P, 2, T])
        raw = sb("raw", [P, 2, F + FT * D])
        w1hi = sb("w1hi", [P, 2, F], F32R)
        w1lo = sb("w1lo", [P, 2, F], F32R)
        w2hi = sb("w2hi", [P, 2, FT * D], F32R)
        w2lo = sb("w2lo", [P, 2, FT * D], F32R)
        b1cur = sb("b1cur", [P, 2, FT])
        h32 = sb("h32", [P, 4, 512])
        hhi = sb("hhi", [P, 4, 512], F32R)
        hlo = sb("hlo", [P, 4, 512], F32R)
        ytmp = sb("ytmp", [P, 2, 512])
        acc = sb("acc", [P, T])

        l1w = sb("l1w", [P, 4 * INNER])
        wq1T = l1w[:, 0:INNER].rearrange("p (i d) -> p i d", i=NI)
        wkv1_sb = l1w[:, INNER:3 * INNER]
        wo1_sb = l1w[:, 3 * INNER:].rearrange("p (i d) -> p i d", i=NI)
        kv1T = sb("kv1T", [P, 2, NI, B * S])
        kT1, vT1 = kv1T[:, 0, :, :], kv1T[:, 1, :, :]
        A1 = sb("A1", [P, B, H1, S])
        VOT = sb("VOT", [P, B, H1 * S])
        VO = sb("VO", [P, B, NB, D])
        usum = sb("usum", [P, B])
        urow = sb("urow", [P, B, D])
        tbo = sb("tbo", [P, D])
        SC = sb("SC", [P, B, H1, S])
        PR = sb("PR", [P, B, H1 * S])
        PT = sb("PT", [P, NB, P])
        E0 = SC[:, 0, :, :].rearrange("p (t two) s -> p t two s", two=2)
        Wt = PR[:, 1, 0:NTILE * S].rearrange("p (t s) -> p t s", s=S)
        wT = VO[0:S, 0, 0:NTILE, :]
        sq = VO[:, 1, 0:NTILE, :]
        PTB = [PT, SC[:].rearrange("p b h s -> p (b h s)")[:, 0:NB * P].rearrange("p (j d) -> p j d", d=P)]
        nmx1 = sb("nmx1", [P, B, H1])
        se1 = sb("se1", [P, B, H1])
        rc1 = sb("rc1", [P, B, H1])

        wf_raw = sb("wf_raw", [P, 2 * IT * D + I])
        wmx = sb("wmx", [P, 7])
        wsc = sb("wsc", [P, 7])
        winv = sb("winv", [P, 7])
        wqf = sb("wqf", [P, 2 * IT * D + I])
        wguT = sb("wguT", [P, 2, IT, P], BF16)
        wdT = sb("wdT", [P, IT, D], BF16)
        sdg = sb("sdg", [P, D])
        sdgs = sb("sdgs", [P, D])
        xmx = sb("xmx", [P, 2])
        xmxa = sb("xmxa", [P, 2])
        sx = sb("sx", [P, 1])
        sxi = sb("sxi", [P, 1])
        qT = sb("qT", [P, T], BF16)
        gsx = sb("gsx", [P, 6])
        sl = ytmp
        hq = l1w[:, 0:IT * T].rearrange("p (i t) -> p i t", i=IT)
        hmx = sb("hmx", [P, IT * 2])
        hmxr = sb("hmxr", [P, 1])
        hmxa = sb("hmxa", [P, 1])
        sh = sb("sh", [P, 1])
        shi = sb("shi", [P, 1])
        hqb = kv1T[:].rearrange("p a i b -> p (a i b)")[:, 0:IT * T // 2].bitcast(BF16).rearrange(
            "p (i t) -> p i t", i=IT)
        otmp = xT[:].rearrange("p (t d) -> p t d", d=D)

        names = """acc_zero x_loaded0 x_loaded1 x_loaded2 early_loaded late_loaded mask_loaded l1wa_loaded l1wb_loaded
            ffnw_loaded pool_const mask_ready dve_step pool_step
            lam_summed tanh_ready lam_exp tgli_ready kv0_ready kv0_evac a0_ready a0_evac_a a0_evac_d vv_evac
            ve_ready rstd_ready xn_ready xt_ready xt_evac sc0_ready nmx0_ready exp0_ready w_ready wt_ready wt_evac
            pv_ready sq_ready rms_ready x1_ready x2t_ready xhi_ready xlo_ready xt2_evac
            logit_ready lgsub_ready lgexp_ready gate_ready gt_ready gt_evac gt_stored
            prep_ready pevac_a pevac_d usum_ready u_ready urow_evac row_added
            vw_ready vw_evac acct_ready x2_ready vo_ready vo_evac
            wmx_ready wqf_ready wgu_ready wgu_evac wq_ready wq_evac sd_ready sd_evac
            sc1_ready sc1_masked nmx1_ready exp1_ready pr_ready pt_ready pt_evac_a pt_evac_d pv1_ready x3_ready
            xmx_ready xmxa_ready sxi_ready qf_a qf_d qt_ready q_ready gu_ready sl_ready h_ready hmx_ready hmxa_ready
            shi_ready hqf_ready hqf_ready_p hqb_ready dn_ready o_ready out_ready out_stored
            raw_loaded0 raw_loaded1 g_loaded0 g_loaded1 whi_ready w1_split w2_split up_done h32_ready hi_ready
            b1_ready lo_dve lo_pool down_done y_mul y_done y_added""".split()
        s = {n: sem(n) for n in names}

        LAG = 2
        POOL_LO = [(0, 1), (1, 1), (3, 1)]

        def lo_count(e, ft, ci):
            pool = (ft, ci) in POOL_LO
            before = [(f, c) for f in range(FT) for c in range(2) if (f, c) < (ft, ci) and ((f, c) in POOL_LO) == pool]
            each = len(POOL_LO) if pool else 2 * FT - len(POOL_LO)
            return s["lo_pool" if pool else "lo_dve"], each * e + len(before) + 1

        def h_slot(ft, ci):
            return (ft % 2) * 2 + ci

        def y_bank(slot, ci):
            return 4 + slot * 2 + ci

        def earlier(e, ft, back):
            m = ft - back
            return e + m // FT, m % FT, not (isinstance(e, int) and FT * e + m < 0)

        def fixed(e):
            return isinstance(e, int)

        def tok(c):
            return CH_T0[c] * P, CH_NT[c] * P

        PVB = [(3, 0), (4, 1), (5, 2)]
        X2B = [3, 4, 5]
        SCB = [[2, 3, 4], [5, 6, 7]]
        VOU = [(b, j0, nj) for b in range(B) for j0, nj in ((0, 4), (4, 4), (8, 2))]
        VOB = [0, 1]
        GUB = 2
        HQ_DVE, HQ_POOL = 0, 4
        PREP = ([("kT", a, n, 0) for a, n in G3] + [("A", a, n, par) for par in range(2) for a, n in G3]
                + [("vT", a, n, 0) for a, n in G3])
        VWORK = [("VOT", a, n, par) for par in range(2) for a, n in G3]

        def prep_copies(unit, bank, copy):
            kind, n0, cnt, par = unit
            if kind in ("kT", "vT"):
                dst = (kT1 if kind == "kT" else vT1)[:, n0:n0 + cnt, :]
                return copy(dst.rearrange("p i d -> p (i d)"), ps[:, bank, 0:cnt * B * S], 1.0)
            src = ps[:, bank, 0:cnt * B * S].rearrange("p (i b s) -> p i b s", b=B, s=S)
            dst = A1[:] if kind == "A" else VOT[:].rearrange("p b (h s) -> p b h s", s=S)
            dst = dst.rearrange("p b (i two) s -> p i two b s", two=2)[:, n0:n0 + cnt, par, :, :]
            return copy(dst, src, DH ** -0.5 if kind == "A" else 1.0)

        def vo_copies(v, copy):
            b, j0, nj = VOU[v]
            full = min(nj, HS // P - j0)
            last = copy(VO[:, b, j0:j0 + full, :].rearrange("p j d -> p (j d)"), ps[:, VOB[v % 2], 0:full * P], 1.0)
            if full < nj:
                w = HS % P
                last = copy(VO[0:w, b, j0 + full, :], ps[0:w, VOB[v % 2], full * P:(full + 1) * P], 1.0)
            return last

        def pt_copies_a(b, copy):
            dst, w = PTB[b], HS % P
            copy(dst[:, 0:4, :].rearrange("p j d -> p (j d)"), ps[:, 2, :], 1.0)
            if b == 0:
                copy(dst[:, 4:8, :].rearrange("p j d -> p (j d)"), ps[:, 3, :], 1.0)
            copy(dst[:, 8, :], ps[:, 4, 0:P], 1.0)
            return copy(dst[0:w, 9, :], ps[0:w, 4, P:2 * P], 1.0)

        def pt_copy_d(copy):
            return copy(PTB[1][:, 4:8, :].rearrange("p j d -> p (j d)"), ps[:, 3, :], 1.0)

        block = st.enter_context(nc.Block())

        @block.sync
        def _(eng):
            xv = x.rearrange("b (t p) d -> p b t d", p=P)
            eng.dma_start(xs[:, 0:2, :], xv[:, :, 3, :]).then_inc(s["x_loaded0"], 16)
            eng.dma_start(early_sb[:], early).then_inc(s["early_loaded"], 16)
            eng.dma_start(xs[:, 2:5, :], xv[:, 0, 0:3, :]).then_inc(s["x_loaded1"], 16)
            eng.dma_start(xs[:, 5:8, :], xv[:, 1, 0:3, :]).then_inc(s["x_loaded2"], 16)
            eng.dma_start(late_sb[:], late).then_inc(s["late_loaded"], 16)
            eng.dma_start(l1w[:, 0:2 * INNER], l1w_in[:, 0:2 * INNER]).then_inc(s["l1wa_loaded"], 16)

            def load_expert(e, slot):
                if not fixed(e) or e >= 2:
                    eng.wait_ge(s["w2_split"], e - 1)
                eng.dma_start(raw[:, slot, :], experts[bass.ds(e, 1), :, :].rearrange("a p f -> p (a f)")).then_inc(
                    s[f"raw_loaded{slot}"], 16)

            def load_gates(e, slot):
                if not fixed(e) or e >= 2:
                    eng.wait_ge(s["y_mul"], 2 * (e - 1))
                eng.dma_start(G[:, slot, :], gates_dram[bass.ds(e, 1), :].broadcast_to([P, T])).then_inc(
                    s[f"g_loaded{slot}"], 16)

            load_expert(0, 0)
            eng.dma_start(l1w[:, 2 * INNER:], l1w_in[:, 2 * INNER:]).then_inc(s["l1wb_loaded"], 16)
            load_expert(1, 1)
            eng.dma_start(mask_u8[:].rearrange("p b s -> p (b s)"), mask).then_inc(s["mask_loaded"], 16)
            eng.dma_start(wf_raw[:], ffnw_in).then_inc(s["ffnw_loaded"], 16)
            load_expert(2, 0)
            load_expert(3, 1)

            eng.wait_ge(s["gt_evac"], 2)
            eng.dma_start(gates_dram, gateT[:]).then_inc(s["gt_stored"], 16)
            eng.wait_ge(s["gt_stored"], 16)
            load_gates(0, 0)
            load_gates(1, 1)
            with eng.Fori(2, E - 3, 2) as e:
                for slot in range(2):
                    load_gates(e + slot, slot)
                    load_expert(e + slot + 2, slot)
            load_gates(E - 2, 0)
            load_gates(E - 1, 1)

            ov = out.rearrange("b (t p) d -> p b t d", p=P)
            eng.wait_ge(s["out_ready"], 1)
            eng.dma_start(ov[:, :, 3, :], xs[:, 0:2, :]).then_inc(s["out_stored"], 16)
            eng.dma_start(ov[:, 0, 0:2, :], xs[:, 2:4, :]).then_inc(s["out_stored"], 16)
            eng.wait_ge(s["out_ready"], 2)
            eng.dma_start(ov[:, 0, 2, :], xs[:, 4, :]).then_inc(s["out_stored"], 16)
            eng.wait_ge(s["out_stored"], 64)

        @block.gpsimd
        def _(eng):
            steps = [0]

            def step(ins):
                steps[0] += 1
                ins.then_inc(s["pool_step"], 1)
                eng.wait_ge(s["pool_step"], steps[0])

            def inv_root(c, n):
                t0, nt = CH_T0[c], CH_NT[c]
                eng.wait_ge(s["ve_ready"], n)
                eng.tensor_tensor(rstd[:, t0:t0 + nt], ve[:, t0:t0 + nt], mhalf[:, t0:t0 + nt], ALU.pow).then_inc(
                    s["rstd_ready"], 1)

            step(eng.memset(mhalf[:], -0.5))
            step(eng.memset(ident[:], 0.0))
            eng.affine_select(out=ident[:], in_=ident[:], compare_op=ALU.not_equal, fill=1.0, base=0,
                              pattern=[[-1, P]], channel_multiplier=1).then_inc(s["pool_const"], 1)
            for c in range(3):
                inv_root(c, c + 1)
            eng.memset(acc[:], 0.0).then_inc(s["acc_zero"], 1)
            step(eng.memset(tie[:], -1e-37))
            eng.affine_select(out=tie[:], in_=tie[:], compare_op=ALU.is_ge, fill=0.0, base=0,
                              pattern=[[1, E], [-1, E]], channel_multiplier=0).then_inc(s["pool_const"], 1)

            def split_low(e, slot):
                eng.wait_ge(s["whi_ready"], 2 * e + 1)
                if not fixed(e) or e >= 2:
                    eng.wait_ge(s["up_done"], 2 * FT * (e - 1))
                eng.tensor_tensor(w1lo[:, slot, :], raw[:, slot, 0:F], w1hi[:, slot, :].bitcast(F32),
                                  ALU.subtract).then_inc(s["w1_split"], 1)
                eng.wait_ge(s["whi_ready"], 2 * e + 2)
                if not fixed(e) or e >= 2:
                    eng.wait_ge(s["down_done"], 2 * FT * (e - 1))
                eng.tensor_tensor(w2lo[:, slot, :], raw[:, slot, F:], w2hi[:, slot, :].bitcast(F32),
                                  ALU.subtract).then_inc(s["w2_split"], 1)

            def inv_rms(c):
                t0, nt = CH_T0[c], CH_NT[c]
                eng.wait_ge(s["sq_ready"], c + 1)
                step(eng.tensor_scalar(ms[:, t0:t0 + nt], ss[:, t0:t0 + nt], 1.0 / D, EPS, ALU.mult, ALU.add))
                eng.tensor_tensor(rms[:, t0:t0 + nt], ms[:, t0:t0 + nt], mhalf[:, t0:t0 + nt], ALU.pow).then_inc(
                    s["rms_ready"], 1)

            inv_rms(0)
            inv_rms(1)
            inv_root(0, 4)
            inv_rms(2)
            inv_root(1, 5)
            inv_root(2, 6)
            split_low(0, 0)
            split_low(1, 1)
            eng.wait_ge(s["mask_loaded"], 16)
            step(eng.tensor_scalar(maskadd[:], mask_u8[:], -1.0, -NEG, ALU.add, ALU.mult))
            eng.affine_select(out=maskadd[:], in_=maskadd[:], compare_op=ALU.is_ge, fill=NEG,
                              base=(N // P - 1) * P + CAUSAL - 1, pattern=[[0, B], [-1, S]],
                              channel_multiplier=1).then_inc(s["mask_ready"], 1)

            def expert(e, slot):
                for ft in range(FT):
                    if ft == 2 and (1 <= e < E - 1 if fixed(e) else True):
                        split_low(e + 1, 1 - slot)
                    if ft == 2 and fixed(e) and e == E - 1:
                        eng.wait_ge(s["wmx_ready"], 1)
                        for c in range(7):
                            w = D if c < 6 else I
                            last = eng.tensor_scalar(wqf[:, c * D:c * D + w], wf_raw[:, c * D:c * D + w], winv[:, c:c + 1],
                                                     MAGIC, ALU.mult, ALU.add)
                        last.then_inc(s["wqf_ready"], 1)
                    for ci in range(2):
                        if (ft, ci) in POOL_LO:
                            hs = h_slot(ft, ci)
                            eng.wait_ge(s["hi_ready"], 2 * (FT * e + ft) + ci + 1)
                            eng.tensor_tensor(hlo[:, hs, :], h32[:, hs, :], hhi[:, hs, :].bitcast(F32),
                                              ALU.subtract).then_inc(s["lo_pool"], 1)

            expert(0, 0)
            expert(1, 1)
            with eng.Fori(2, E - 3, 2) as e:
                for slot in range(2):
                    expert(e + slot, slot)
            expert(E - 2, 0)
            expert(E - 1, 1)
            for ci in range(2):
                t = slice(ci * 512, (ci + 1) * 512)
                eng.wait_ge(s["y_mul"], 2 * (E - 2) + ci + 1)
                eng.wait_ge(s["y_done"], 2 * (E - 3) + ci + 1)
                eng.tensor_tensor(acc[:, t], acc[:, t], ytmp[:, ci, :], ALU.add).then_inc(s["y_added"], 1)
            inv_root(0, 7)
            eng.wait_ge(s["urow_evac"], 1)
            step(eng.tensor_tensor(urow[:], urow[:], tbo[:].unsqueeze(1).broadcast_to([P, B, D]), ALU.add))
            eng.wait_ge(s["x2_ready"], 3)
            for b in range(B):
                t0, nt = CH_T0[1 + b], CH_NT[1 + b]
                eng.tensor_tensor(xs[:, t0:t0 + nt, :], xs[:, t0:t0 + nt, :],
                                  urow[:, b, :].unsqueeze(1).broadcast_to([P, nt, D]), ALU.add).then_inc(s["row_added"], 1)
            inv_root(1, 8)
            inv_root(2, 9)
            inv_root(0, 10)

            RMAX = bass.bass_isa.ReduceOp.absmax
            eng.wait_ge(s["xmx_ready"], 1)
            eng.partition_all_reduce(xmxa[:], xmx[:], P, RMAX).then_inc(s["xmxa_ready"], 1)
            eng.wait_ge(s["hmx_ready"], 1)
            eng.partition_all_reduce(hmxa[:], hmxr[:], P, RMAX).then_inc(s["hmxa_ready"], 1)
            eng.wait_ge(s["shi_ready"], 1)
            half, it = divmod(HQ_POOL, IT)
            t = slice(half * 512, (half + 1) * 512)
            eng.tensor_scalar(hq[:, it, t], hq[:, it, t], shi[:], MAGIC, ALU.mult, ALU.add).then_inc(s["hqf_ready_p"], 1)

        @block.scalar
        def _(eng):
            eng.wait_ge(s["kv0_ready"], 1)
            eng.activation(kv0T[:].rearrange("p a b -> p (a b)"), ps[:, 7, 0:2 * B * S], ACT.Copy).then_inc(s["kv0_evac"], 1)
            eng.wait_ge(s["late_loaded"], 16)
            eng.activation(gth[:, 0:4], gsc[:, 0:4], ACT.Tanh)
            eng.activation(gth[:, 4:6], gsc[:, 4:6], ACT.Tanh, scale=0.5).then_inc(s["tanh_ready"], 1)
            eng.wait_ge(s["a0_ready"], 1)
            eng.activation(A0[:, :, 0, :], ps[:, 6, 0:B * S].rearrange("p (b s) -> p b s", b=B), ACT.Copy,
                           scale=HD ** -0.5).then_inc(s["a0_evac_a"], 1)

            def xt_evac(c):
                t0, w = tok(c)
                eng.wait_ge(s["xt_ready"], c + 1)
                eng.activation(xT[:, t0:t0 + w], ps[:, c, 0:w], ACT.Copy).then_inc(s["xt_evac"], 1)

            def exps(c):
                eng.wait_ge(s["nmx0_ready"], c + 1)
                for j in range(CH_NT[c]):
                    for h in range(2):
                        i = 2 * (CH_T0[c] + j) + h
                        last = eng.activation(E0[:, CH_T0[c] + j, h, :], ps[:, 3 + c, (2 * j + h) * S:(2 * j + h + 1) * S],
                                              ACT.Exp, bias=nmx0[:, i:i + 1], accum_out=se0[:, i:i + 1])
                last.then_inc(s["exp0_ready"], 1)

            def wt_evac(c):
                t0, nt = CH_T0[c], CH_NT[c]
                eng.wait_ge(s["wt_ready"], c + 1)
                eng.activation(wT[:, t0:t0 + nt, :].rearrange("p t d -> p (t d)"), ps[0:S, c, 0:nt * P],
                               ACT.Copy).then_inc(s["wt_evac"], 1)

            def squares(c):
                eng.wait_ge(s["pv_ready"], c + 1)
                for j in range(CH_NT[c]):
                    t = CH_T0[c] + j
                    last = eng.activation(sq[:, t, :], ps[:, PVB[c][0], j * D:(j + 1) * D], ACT.Square,
                                          accum_out=ss[:, t:t + 1])
                last.then_inc(s["sq_ready"], 1)

            def split_high(e, slot):
                eng.wait_ge(s[f"raw_loaded{slot}"], 8 * (e - slot) + 16)
                if not fixed(e) or e >= 2:
                    eng.wait_ge(s["up_done"], 2 * FT * (e - 1))
                eng.activation(w1hi[:, slot, :], raw[:, slot, 0:F], ACT.Copy).then_inc(s["whi_ready"], 1)
                if not fixed(e) or e >= 2:
                    eng.wait_ge(s["down_done"], 2 * FT * (e - 1))
                eng.activation(w2hi[:, slot, :], raw[:, slot, F:], ACT.Copy).then_inc(s["whi_ready"], 1)

            def copy(dst, src, scale):
                return eng.activation(dst, src, ACT.Copy, scale=scale)

            def prep_evacs(lo, hi):
                for u in range(lo, hi):
                    if u % 2 == 0:
                        eng.wait_ge(s["prep_ready"], u + 1)
                        prep_copies(PREP[u], 6, copy).then_inc(s["pevac_a"], 1)

            for c in range(3):
                xt_evac(c)
            vvp = ps[0:S, 5, :].rearrange("p (b a d) -> p b a d", b=B, a=2)
            eng.activation(VV[:, :, 0, :], vvp[:, :, 0, :], ACT.Copy)
            eng.wait_ge(s["tgli_ready"], 1)
            eng.activation(VV[:, :, 1, :], vvp[:, :, 1, :], ACT.Copy, scale=tgli[0:S, :]).then_inc(s["vv_evac"], 1)
            eng.wait_ge(s["lam_summed"], 1)
            eng.activation(lam_e[:], lam_s[:], ACT.Exp).then_inc(s["lam_exp"], 1)
            exps(0)
            exps(1)
            prep_evacs(0, 3)
            wt_evac(0)
            exps(2)
            squares(0)
            wt_evac(1)
            prep_evacs(3, 5)
            squares(1)
            wt_evac(2)
            prep_evacs(5, 7)
            squares(2)
            prep_evacs(7, 9)
            split_high(0, 0)
            split_high(1, 1)
            for c in range(3):
                t0, w = tok(c)
                eng.wait_ge(s["x2t_ready"], c + 1)
                eng.activation(xhi[:, t0:t0 + w], ps[:, X2B[c], 0:w], ACT.Copy).then_inc(s["xhi_ready"], 1)
            for c in range(3):
                t0, w = tok(c)
                eng.wait_ge(s["xlo_ready"], c + 1)
                eng.activation(xT[:, t0:t0 + w], ps[:, X2B[c], 0:w], ACT.Copy).then_inc(s["xt2_evac"], 1)

            def expert(e, slot):
                eng.wait_ge(s["b1_ready"], e + 1)
                for ft in range(FT):
                    for ci in range(2):
                        hs = h_slot(ft, ci)
                        eng.wait_ge(s["up_done"], 2 * (FT * e + ft) + ci + 1)
                        e0, f0, there = earlier(e, ft, 2)
                        if there:
                            eng.wait_ge(*lo_count(e0, f0, ci))
                        eng.activation(h32[:, hs, :], ps[:, hs, :], ACT.Relu,
                                       bias=b1cur[:, slot, ft:ft + 1]).then_inc(s["h32_ready"], 1)
                    if fixed(e) and (e, ft) == (0, 0):
                        prep_evacs(9, 12)
                    if fixed(e) and (e, ft) == (0, 1):
                        eng.wait_ge(s["lgsub_ready"], 1)
                        eng.activation(pr[:], lg[:], ACT.Exp).then_inc(s["lgexp_ready"], 1)
                    if fixed(e) and (e, ft) == (1, 1):
                        for i in range(2):
                            eng.wait_ge(s["gt_ready"], i + 1)
                            eng.activation(gateT[:, i * 512:(i + 1) * 512], ps[0:E, 6 + i, :], ACT.Copy).then_inc(
                                s["gt_evac"], 1)
                    if ft == 2 and (1 <= e < E - 1 if fixed(e) else True):
                        split_high(e + 1, 1 - slot)

            expert(0, 0)
            expert(1, 1)
            with eng.Fori(2, E - 3, 2) as e:
                for slot in range(2):
                    expert(e + slot, slot)
            expert(E - 2, 0)
            expert(E - 1, 1)

            for u, unit in enumerate(VWORK):
                eng.wait_ge(s["vw_ready"], u + 1)
                prep_copies(unit, u % 2, copy).then_inc(s["vw_evac"], 1)
            eng.wait_ge(s["wgu_ready"], 1)
            for n in range(2):
                last = eng.activation(wguT[:, n, :, :].rearrange("p t d -> p (t d)"), ps[:, 6 + n, 0:IT * P], ACT.Copy,
                                      bias=-MAGIC)
            last.then_inc(s["wgu_evac"], 1)
            eng.wait_ge(s["xt_ready"], 4)
            eng.activation(xT[:, 0:2 * P], ps[:, 5, 0:2 * P], ACT.Copy).then_inc(s["xt_evac"], 1)
            eng.wait_ge(s["vw_evac"], len(VWORK))
            for b in range(B):
                eng.activation(PR[:, b, :], VOT[:, b, :], ACT.Copy, scale=1.0 / S, accum_out=usum[:, b:b + 1]).then_inc(
                    s["usum_ready"], 1)
            def vo_evacs(lo, hi):
                for v in range(lo, hi):
                    eng.wait_ge(s["vo_ready"], v + 1)
                    vo_copies(v, copy).then_inc(s["vo_evac"], 1)

            eng.wait_ge(s["usum_ready"], B)
            for h in range(H1):
                if h == HG[-1][0]:
                    vo_evacs(0, 2)
                if h in [h0 for h0, nh in HG]:
                    eng.wait_ge(s["nmx1_ready"], [h0 for h0, nh in HG].index(h) + 1)
                last = eng.activation(PR[:, 0, h * S:(h + 1) * S], SC[:, 0, h, :], ACT.Exp, bias=nmx1[:, 0, h:h + 1],
                                      accum_out=se1[:, 0, h:h + 1])
            last.then_inc(s["exp1_ready"], 1)

            eng.wait_ge(s["u_ready"], 1)
            eng.activation(urow[:].rearrange("p b d -> p (b d)"), ps[:, 2, 0:B * P], ACT.Copy, scale=gth[:, 1:2]).then_inc(
                s["urow_evac"], 1)
            eng.wait_ge(s["nmx1_ready"], len(HG) + 1)
            eng.activation(PR[:, 1, :], SC[:, 1, :, :].rearrange("p h s -> p (h s)"), ACT.Exp).then_inc(s["exp1_ready"], 1)
            vo_evacs(2, 4)
            eng.wait_ge(s["pt_ready"], 1)
            pt_copies_a(0, copy).then_inc(s["pt_evac_a"], 1)
            vo_evacs(4, 6)
            eng.wait_ge(s["pt_ready"], 2)
            pt_copies_a(1, copy).then_inc(s["pt_evac_a"], 1)
            eng.wait_ge(s["wq_ready"], 1)
            eng.activation(wdT[:, 0:2, :].rearrange("p t d -> p (t d)"), ps[:, 5, 0:2 * P], ACT.Copy, bias=-MAGIC)
            eng.activation(wdT[0:ILAST, 2, :], ps[0:ILAST, 5, 2 * P:3 * P], ACT.Copy, bias=-MAGIC).then_inc(s["wq_evac"], 1)
            eng.wait_ge(s["sd_ready"], 1)
            eng.activation(sdg[:], ps[:, 5, 3 * P:4 * P], ACT.Copy, scale=gth[:, 3:4]).then_inc(s["sd_evac"], 1)

            eng.wait_ge(s["sxi_ready"], 1)
            eng.activation(xn[:, 4:8, :], xn[:, 4:8, :], ACT.Copy, scale=sxi[:], bias=MAGIC).then_inc(s["qf_a"], 1)
            for u in range(2 * IT):
                half, it = divmod(u, IT)
                rows = P if it < 2 else ILAST
                eng.wait_ge(s["gu_ready"], u + 1)
                if u >= 2:
                    eng.wait_ge(s["h_ready"], u - 1)
                eng.activation(sl[0:rows, u % 2, :], ps[0:rows, 2 * (u % 3) + GUB, :], ACT.Silu,
                               scale=gsx[0:rows, it:it + 1]).then_inc(s["sl_ready"], 1)
            eng.wait_ge(s["shi_ready"], 1)
            for u in range(2 * IT):
                if u not in (HQ_DVE, HQ_POOL):
                    half, it = divmod(u, IT)
                    rows = P if it < 2 else ILAST
                    hv = hq[0:rows, it, half * 512:(half + 1) * 512]
                    eng.activation(hv, hv, ACT.Copy, scale=shi[0:rows, :], bias=MAGIC).then_inc(s["hqf_ready"], 1)
            eng.wait_ge(s["out_ready"], 2)
            eng.dma_start(out.rearrange("b (t p) d -> p b t d", p=P)[:, 1, 0:3, :], xs[:, 5:8, :]).then_inc(
                s["out_stored"], 16)

        @block.tensor
        def _(eng):
            def tr(dst, src, n=P):
                return eng.transpose(dst, src, ident[0:n, 0:n])

            def mm(dst, lhsT, rhs, start=True, stop=True):
                return eng.matmul(dst, lhsT, rhs, start=start, stop=stop)

            eng.wait_ge(s["early_loaded"], 16)
            mm(ps[:, 7, 0:B * S], wkT2, ctxT)
            mm(ps[:, 7, B * S:2 * B * S], wvT, ctxT).then_inc(s["kv0_ready"], 1)
            for b in range(B):
                mm(ps[0:S, 5, b * 256:b * 256 + P], ctxT[:, b * S:(b + 1) * S], wvT)
            eng.wait_ge(s["kv0_evac"], 1)
            for h in range(2):
                mm(ps[:, 6 + h, 0:B * S], wq0_sb[h * HD:(h + 1) * HD, :], kv0T[h * HD:(h + 1) * HD, 0, :])
            for b in range(B):
                last = mm(ps[0:S, 5, b * 256 + P:b * 256 + 2 * P], kv0T[:, 1, b * S:(b + 1) * S], woT)
            last.then_inc(s["a0_ready"], 1)

            eng.wait_ge(s["pool_const"], 1)

            def transposes(c, bank, n):
                eng.wait_ge(s["xn_ready"], n)
                for j in range(CH_NT[c]):
                    last = tr(ps[:, bank, j * P:(j + 1) * P], xn[:, CH_T0[c] + j, :])
                return last

            def batch(c, j):
                return j if c == 0 else c - 1

            def scores(c):
                eng.wait_ge(s["xt_evac"], c + 1)
                for j in range(CH_NT[c]):
                    t = CH_T0[c] + j
                    last = mm(ps[:, 3 + c, j * 2 * S:(j + 1) * 2 * S], xT[:, t * P:(t + 1) * P],
                              A0[:, batch(c, j), :, :].rearrange("p h s -> p (h s)"))
                last.then_inc(s["sc0_ready"], 1)

            def attend(c):
                eng.wait_ge(s["w_ready"], c + 1)
                for j in range(CH_NT[c]):
                    last = tr(ps[0:S, c, j * P:(j + 1) * P], Wt[:, CH_T0[c] + j, :])
                last.then_inc(s["wt_ready"], 1)
                prep(3 + c, 4 + c)
                eng.wait_ge(s["wt_evac"], c + 1)
                for a in range(2):
                    for j in range(CH_NT[c]):
                        last = mm(ps[:, PVB[c][a], j * P:(j + 1) * P], wT[:, CH_T0[c] + j, :], VV[:, batch(c, j), a, :])
                last.then_inc(s["pv_ready"], 1)

            def products(unit, bank):
                kind, n0, cnt, par = unit
                rows = slice(par * DH, (par + 1) * DH)
                for m in range(cnt):
                    i = n0 + m
                    dst = ps[:, bank, m * B * S:(m + 1) * B * S]
                    if kind in ("kT", "vT"):
                        o = (INNER if kind == "vT" else 0) + i * P
                        last = mm(dst, wkv1_sb[:, o:o + P], ctxT)
                    elif kind == "A":
                        last = mm(dst, wq1T[rows, i, :], kT1[rows, i, :])
                    else:
                        last = mm(dst, wo1_sb[rows, i, :], vT1[rows, i, :])
                return last

            def prep(lo, hi):
                for u in range(lo, hi):
                    if u == 0:
                        eng.wait_ge(s["l1wa_loaded"], 16)
                    if u == 3 * len(G3):
                        eng.wait_ge(s["l1wb_loaded"], 16)
                    if u == len(G3):
                        eng.wait_ge(s["pevac_a"], (u + 1) // 2)
                        eng.wait_ge(s["pevac_d"], u // 2)
                    elif u >= 2:
                        eng.wait_ge(s["pevac_a" if u % 2 == 0 else "pevac_d"], (u - 2) // 2 + 1)
                    products(PREP[u], 6 + u % 2).then_inc(s["prep_ready"], 1)

            def vwork(lo, hi):
                for u in range(lo, hi):
                    if u == 0:
                        eng.wait_ge(s["h32_ready"], 2 * (FT * (E - 1) + 3))
                    if u >= 2:
                        eng.wait_ge(s["vw_evac"], u - 1)
                    products(VWORK[u], u % 2).then_inc(s["vw_ready"], 1)

            for c in range(3):
                transposes(c, c, c + 1).then_inc(s["xt_ready"], 1)
            eng.wait_ge(s["a0_evac_a"], 1)
            eng.wait_ge(s["a0_evac_d"], 1)
            scores(0)
            scores(1)
            eng.wait_ge(s["vv_evac"], 1)
            scores(2)
            prep(0, 3)
            for c in range(3):
                attend(c)
            prep(6, 7)
            eng.wait_ge(s["x1_ready"], 1)
            transposes(0, X2B[0], 4).then_inc(s["x2t_ready"], 1)
            prep(7, 10)
            transposes(1, X2B[1], 5).then_inc(s["x2t_ready"], 1)
            transposes(2, X2B[2], 6).then_inc(s["x2t_ready"], 1)
            prep(10, 12)

            def up(e, ft, slot):
                if ft == 0:
                    eng.wait_ge(s["w1_split"], e + 1)
                if fixed(e) and e == 0 and ft < 2:
                    eng.wait_ge(s["x1_ready"], 3)
                    eng.wait_ge(s["xlo_ready"], 3)
                    if ft == 1:
                        eng.wait_ge(s["xt2_evac"], 3)
                e0, f0, there = earlier(e, ft, 2)
                if there:
                    eng.wait_ge(s["h32_ready"], 2 * (FT * e0 + f0 + 1))
                wh, wl = w1hi[:, slot, ft * P:(ft + 1) * P], w1lo[:, slot, ft * P:(ft + 1) * P]
                for ci in range(2):
                    t = slice(ci * 512, (ci + 1) * 512)
                    dst = ps[:, h_slot(ft, ci), :]
                    mm(dst, wh, xhi[:, t], True, False)
                    mm(dst, wh, xlo[:, t], False, False)
                    mm(dst, wl, xhi[:, t], False, True).then_inc(s["up_done"], 1)

            def down(e, ft, slot):
                if ft == 0:
                    eng.wait_ge(s["w2_split"], e + 1)
                    if not fixed(e) or e >= 2:
                        eng.wait_ge(s["y_mul"], 2 * (e - 1))
                    if fixed(e) and e == 1:
                        eng.wait_ge(s["gt_evac"], 2)
                wh, wl = w2hi[:, slot, ft * D:(ft + 1) * D], w2lo[:, slot, ft * D:(ft + 1) * D]
                for ci in range(2):
                    hs = h_slot(ft, ci)
                    dst = ps[:, y_bank(slot, ci), :]
                    eng.wait_ge(*lo_count(e, ft, ci))
                    mm(dst, wh, hhi[:, hs, :], ft == 0, False)
                    mm(dst, wh, hlo[:, hs, :], False, False)
                    mm(dst, wl, hhi[:, hs, :], False, ft == FT - 1).then_inc(s["down_done"], 1)

            def expert(e, slot):
                for ft in range(FT):
                    up(e, ft, slot)
                    e0, f0, there = earlier(e, ft, LAG)
                    if there:
                        down(e0, f0, slot if ft >= LAG else 1 - slot)
                    if fixed(e) and (e, ft) == (0, 1):
                        eng.wait_ge(s["pevac_d"], len(PREP) // 2)
                        for t in range(NTILE):
                            last = mm(ps[:, 7, t * E:(t + 1) * E], xT[:, t * P:(t + 1) * P], wr_sb)
                        last.then_inc(s["logit_ready"], 1)
                    if fixed(e) and (e, ft) == (1, 1):
                        eng.wait_ge(s["gate_ready"], 1)
                        for t in range(NTILE):
                            last = tr(ps[0:E, 6 + t // 4, (t % 4) * P:(t % 4 + 1) * P], gate[:, t, :])
                            if t % 4 == 3:
                                last.then_inc(s["gt_ready"], 1)

            expert(0, 0)
            expert(1, 1)
            with eng.Fori(2, E - 1, 2) as e:
                for slot in range(2):
                    expert(e + slot, slot)
            down(E - 1, FT - 2, 1)
            vwork(0, 2)
            down(E - 1, FT - 1, 1)
            vwork(2, 4)
            for half in range(2):
                eng.wait_ge(s["y_done"], 2 * (E - 2) + half + 1)
                for j in range(4):
                    t = 4 * half + j
                    last = tr(ps[:, 2 + half, j * P:(j + 1) * P], acc[:, t * P:(t + 1) * P])
                last.then_inc(s["acct_ready"], 1)
                vwork(4 + half, 5 + half)

            def vo(lo, hi):
                for v in range(lo, hi):
                    b, j0, nj = VOU[v]
                    if v < 2:
                        eng.wait_ge(s["vw_evac"], len(VWORK))
                    else:
                        eng.wait_ge(s["vo_evac"], v - 1)
                    for m in range(nj):
                        w = min(P, HS - (j0 + m) * P)
                        last = tr(ps[0:w, VOB[v % 2], m * P:(m + 1) * P], VOT[:, b, (j0 + m) * P:(j0 + m) * P + w])
                    last.then_inc(s["vo_ready"], 1)

            def transposed_probs(b):
                eng.wait_ge(s["pr_ready"], 2 * b + 1)
                if b == 1:
                    eng.wait_ge(s["pt_evac_a"], 1)
                for j in range(NB):
                    if j == HS // 2 // P:
                        eng.wait_ge(s["pr_ready"], 2 * b + 2)
                    w = min(P, HS - j * P)
                    last = tr(ps[0:w, 2 + j // 4, (j % 4) * P:(j % 4 + 1) * P], PR[:, b, j * P:j * P + w])
                last.then_inc(s["pt_ready"], 1)

            eng.wait_ge(s["wqf_ready"], 1)
            for n in range(2):
                for t in range(IT):
                    c = n * IT + t
                    last = tr(ps[:, 6 + n, t * P:(t + 1) * P], wqf[:, c * D:(c + 1) * D])
            last.then_inc(s["wgu_ready"], 1)
            transposes(0, 5, 7).then_inc(s["xt_ready"], 1)
            eng.wait_ge(s["xt_evac"], 4)
            eng.wait_ge(s["x2_ready"], 3)
            for b in range(B):
                if b == 1:
                    eng.wait_ge(s["wgu_evac"], 1)
                for gi, (h0, nh) in enumerate(HG):
                    mm(ps[:, SCB[b][gi], 0:nh * S], xT[:, b * P:(b + 1) * P],
                       A1[:, b, h0:h0 + nh, :].rearrange("p h s -> p (h s)")).then_inc(s["sc1_ready"], 1)
            eng.wait_ge(s["usum_ready"], B)
            eng.wait_ge(s["sc1_masked"], 3)
            for b in range(B):
                last = mm(ps[:, 2, b * P:(b + 1) * P], usum[:, b:b + 1].broadcast_to([P, P]), ident[:])
            last.then_inc(s["u_ready"], 1)
            vo(0, 2)
            eng.wait_ge(s["sc1_masked"], 6)
            for t in range(IT):
                w = P if t < 2 else ILAST
                last = tr(ps[0:w, 5, t * P:(t + 1) * P], wqf[:, 6 * D + t * P:6 * D + t * P + w])
            last.then_inc(s["wq_ready"], 1)
            mm(ps[:, 5, 3 * P:4 * P], wsc[:, 6:7].broadcast_to([P, P]), ident[:]).then_inc(s["sd_ready"], 1)
            vo(2, 4)
            eng.wait_ge(s["urow_evac"], 1)
            transposed_probs(0)
            vo(4, 6)
            transposed_probs(1)
            eng.wait_ge(s["vo_evac"], len(VOU))
            for b in range(B):
                eng.wait_ge(s["pt_evac_a"], b + 1)
                if b == 1:
                    eng.wait_ge(s["pt_evac_d"], 1)
                for j in range(NB):
                    w = min(P, HS - j * P)
                    last = mm(ps[:, b, 0:P], PTB[b][0:w, j, :], VO[0:w, b, j, :], j == 0, j == NB - 1)
                last.then_inc(s["pv1_ready"], 1)

            eng.wait_ge(s["wgu_evac"], 1)
            eng.wait_ge(s["wq_evac"], 1)
            eng.wait_ge(s["sd_evac"], 1)
            eng.wait_ge(s["x3_ready"], B)
            for half in range(2):
                eng.wait_ge(s["qf_d" if half == 0 else "qf_a"], 1)
                for j in range(4):
                    last = tr(ps[:, half, j * P:(j + 1) * P], xn[:, 4 * half + j, :])
                last.then_inc(s["qt_ready"], 1)
            for u in range(2 * IT):
                half, it = divmod(u, IT)
                rows = P if it < 2 else ILAST
                eng.wait_ge(s["q_ready"], half + 1)
                if u >= 3:
                    eng.wait_ge(s["h_ready"], u - 2)
                for n in range(2):
                    last = mm(ps[0:rows, 2 * (u % 3) + GUB + n, :], wguT[:, n, it, 0:rows], qT[:, half * 512:(half + 1) * 512])
                last.then_inc(s["gu_ready"], 1)
            for half in range(2):
                eng.wait_ge(s["hqb_ready"], IT * (half + 1))
                for t in range(4 * half, 4 * half + 4):
                    for it in range(IT):
                        rows = P if it < 2 else ILAST
                        last = mm(ps[:, half, (t % 4) * P:(t % 4 + 1) * P], hqb[0:rows, it, t * P:(t + 1) * P],
                                  wdT[0:rows, it, :], it == 0, it == IT - 1)
                last.then_inc(s["dn_ready"], 1)

        @block.vector
        def _(eng):
            steps = [0]

            def step(ins):
                steps[0] += 1
                ins.then_inc(s["dve_step"], 1)
                return steps[0]

            def after(n):
                eng.wait_ge(s["dve_step"], n)

            def norm_stats(c):
                t0, nt = CH_T0[c], CH_NT[c]
                for j in range(t0, t0 + nt):
                    last = eng.bn_stats(stats[:, j, :], xs[:, j, :])
                after(step(last))
                for j in range(t0, t0 + nt):
                    last = eng.bn_aggr(mv[:, j, :], stats[:, j, :])
                after(step(last))
                eng.tensor_scalar(ve[:, t0:t0 + nt], mv[:, t0:t0 + nt, 1], EPS, None, ALU.add).then_inc(s["ve_ready"], 1)

            def normalise(c, n):
                eng.wait_ge(s["rstd_ready"], n)
                for j in range(CH_T0[c], CH_T0[c] + CH_NT[c]):
                    last = eng.tensor_scalar(xn[:, j, :], xs[:, j, :], mv[:, j, 0:1], rstd[:, j:j + 1],
                                             ALU.subtract, ALU.mult)
                return last

            def copy(dst, src, scale):
                if scale != 1.0:
                    return eng.tensor_scalar(dst, src, scale, None, ALU.mult)
                return eng.tensor_copy(dst, src)

            def prep_evacs(lo, hi):
                for u in range(lo, hi):
                    if u % 2 == 1:
                        eng.wait_ge(s["prep_ready"], u + 1)
                        prep_copies(PREP[u], 7, copy).then_inc(s["pevac_d"], 1)

            for c in range(3):
                eng.wait_ge(s[f"x_loaded{c}"], 16)
                norm_stats(c)
            for c in range(2):
                normalise(c, c + 1).then_inc(s["xn_ready"], 1)
            eng.wait_ge(s["late_loaded"], 16)
            after(step(eng.tensor_tensor(lam_pr[:], lam_in[:, 0:2, :], lam_in[:, 2:4, :], ALU.mult)))
            eng.tensor_reduce(lam_s[:], lam_pr[:], AX, ALU.add).then_inc(s["lam_summed"], 1)
            eng.wait_ge(s["tanh_ready"], 1)
            eng.tensor_scalar(sig127[:], gth[:, 4:6], 0.5 / QMAX, 0.5 / QMAX, ALU.mult, ALU.add)
            tbo_step = step(eng.tensor_scalar(tbo[:], bo_bc, gth[:, 1:2], None, ALU.mult))
            eng.tensor_scalar(tgli[:], gth[:, 0:1], 1.0 - LAMBDA_INIT, None, ALU.mult).then_inc(s["tgli_ready"], 1)
            eng.wait_ge(s["a0_ready"], 1)
            eng.tensor_scalar(A0[:, :, 1, :], ps[:, 7, 0:B * S].rearrange("p (b s) -> p b s", b=B), HD ** -0.5, None,
                              ALU.mult).then_inc(s["a0_evac_d"], 1)
            normalise(2, 3).then_inc(s["xn_ready"], 1)

            def row_max(c):
                nt = CH_NT[c]
                eng.wait_ge(s["sc0_ready"], c + 1)
                eng.tensor_reduce(nmx0[:, 2 * CH_T0[c]:2 * (CH_T0[c] + nt)],
                                  ps[:, 3 + c, 0:nt * 2 * S].rearrange("p (h s) -> p h s", s=S), AX, ALU.max,
                                  negate=True).then_inc(s["nmx0_ready"], 1)

            def weights(c):
                t0, nt = CH_T0[c], CH_NT[c]
                eng.wait_ge(s["exp0_ready"], c + 1)
                after(step(eng.reciprocal(rc0[:, 2 * t0:2 * (t0 + nt)], se0[:, 2 * t0:2 * (t0 + nt)])))
                ev = E0[:, t0:t0 + nt, :, :].rearrange("p t h s -> p (t h) s")
                after(step(eng.tensor_tensor(ev, ev, rc0[:, 2 * t0:2 * (t0 + nt)].unsqueeze(2).broadcast_to([P, 2 * nt, S]),
                                             ALU.mult)))
                eng.scalar_tensor_tensor(Wt[:, t0:t0 + nt, :], E0[:, t0:t0 + nt, 1, :], nlam[:],
                                         E0[:, t0:t0 + nt, 0, :], ALU.mult, ALU.add).then_inc(s["w_ready"], 1)

            def residual1(c):
                eng.wait_ge(s["rms_ready"], c + 1)
                for j in range(CH_NT[c]):
                    t = CH_T0[c] + j
                    last = eng.scalar_tensor_tensor(xs[:, t, :], ps[:, PVB[c][1], j * P:(j + 1) * P], rms[:, t:t + 1],
                                                    xs[:, t, :], ALU.mult, ALU.add)
                last.then_inc(s["x1_ready"], 1)
                eng.wait_ge(s["x1_ready"], c + 1)
                norm_stats(c)

            row_max(0)
            row_max(1)
            eng.wait_ge(s["lam_exp"], 1)
            after(step(eng.tensor_tensor(nlam[:], lam_e[:, 1:2], lam_e[:, 0:1], ALU.subtract)))
            after(step(eng.tensor_scalar(nlam[:], nlam[:], LAMBDA_INIT, None, ALU.subtract)))
            weights(0)
            row_max(2)
            prep_evacs(0, 3)
            weights(1)
            prep_evacs(3, 5)
            weights(2)
            residual1(0)
            prep_evacs(5, 7)
            residual1(1)
            normalise(0, 4).then_inc(s["xn_ready"], 1)
            residual1(2)
            prep_evacs(7, 9)
            normalise(1, 5).then_inc(s["xn_ready"], 1)

            def low_input(c):
                t0, w = tok(c)
                eng.wait_ge(s["xhi_ready"], c + 1)
                eng.tensor_tensor(xlo[:, t0:t0 + w], ps[:, X2B[c], 0:w], xhi[:, t0:t0 + w].bitcast(F32),
                                  ALU.subtract).then_inc(s["xlo_ready"], 1)

            normalise(2, 6).then_inc(s["xn_ready"], 1)
            prep_evacs(9, 10)
            for c in range(3):
                low_input(c)
            prep_evacs(10, 12)

            pk = pr[:].unsqueeze(2).broadcast_to([P, NTILE, E, E])
            pe_ = pr[:].unsqueeze(3).broadcast_to([P, NTILE, E, E])

            def router(part):
                if part == 1:
                    eng.wait_ge(s["logit_ready"], 1)
                    after(step(eng.tensor_tensor(lg[:], ps[:, 7, 0:NTILE * E].rearrange("p (t e) -> p t e", e=E),
                                                 br_bc.unsqueeze(1).broadcast_to([P, NTILE, E]), ALU.add)))
                    after(step(eng.tensor_reduce(lmx[:], lg[:], AX, ALU.max)))
                    eng.tensor_tensor(lg[:], lg[:], lmx[:].unsqueeze(2).broadcast_to([P, NTILE, E]),
                                      ALU.subtract).then_inc(s["lgsub_ready"], 1)
                if part == 2:
                    eng.wait_ge(s["lgexp_ready"], 1)
                    after(step(eng.tensor_reduce(lsum[:], pr[:], AX, ALU.add)))
                    after(step(eng.reciprocal(lmx[:], lsum[:])))
                    after(step(eng.tensor_tensor(pr[:], pr[:], lmx[:].unsqueeze(2).broadcast_to([P, NTILE, E]), ALU.mult)))
                    eng.wait_ge(s["pool_const"], 2)
                    after(step(eng.tensor_tensor(dif[:], pk, pe_, ALU.subtract)))
                    after(step(eng.tensor_tensor(dif[:], dif[:], tie[:].unsqueeze(1).broadcast_to([P, NTILE, E, E]),
                                                 ALU.is_gt)))
                if part == 3:
                    after(step(eng.tensor_tensor(dif[:], dif[:], pk, ALU.mult)))
                    after(step(eng.tensor_reduce(cum[:], dif[:], AX, ALU.add)))
                    after(step(eng.tensor_tensor(lone[:], cum[:], pr[:], ALU.is_le)))
                    after(step(eng.scalar_tensor_tensor(cum[:], cum[:], TOP_P, lone[:], ALU.is_lt, ALU.max)))
                    eng.tensor_tensor(gate[:], cum[:], pr[:], ALU.mult).then_inc(s["gate_ready"], 1)

            def bias_of(e, slot):
                eng.tensor_scalar(b1cur[:, slot, :], b1T[:, bass.ds(FT * e, FT)], 1.0, None, ALU.mult).then_inc(
                    s["b1_ready"], 1)

            def expert(e, slot):
                for ft in range(FT):
                    for ci in range(2):
                        hs = h_slot(ft, ci)
                        n = 2 * (FT * e + ft) + ci + 1
                        eng.wait_ge(s["h32_ready"], n)
                        e0, f0, there = earlier(e, ft, 2)
                        if there:
                            eng.wait_ge(s["down_done"], 2 * (FT * e0 + f0) + ci + 1)
                        eng.tensor_copy(hhi[:, hs, :], h32[:, hs, :]).then_inc(s["hi_ready"], 1)
                        if (ft, ci) not in POOL_LO:
                            eng.wait_ge(s["hi_ready"], n)
                            eng.tensor_tensor(hlo[:, hs, :], h32[:, hs, :], hhi[:, hs, :].bitcast(F32),
                                              ALU.subtract).then_inc(s["lo_dve"], 1)
                    if ft == 2 and (1 <= e < E - 1 if fixed(e) else True):
                        bias_of(e + 1, 1 - slot)
                    late = fixed(e) and e in (1, E - 1)
                    if not (fixed(e) and e == 0):
                        if ft == FT - 2 and not late:
                            take_y(e - 1, 1 - slot, 0)
                        if ft == FT - 1:
                            if late:
                                take_y(e - 1, 1 - slot, 0)
                            take_y(e - 1, 1 - slot, 1)
                    if fixed(e) and e == 0:
                        router(ft)
                    if fixed(e) and (e, ft) == (1, 1):
                        eng.wait_ge(s["ffnw_loaded"], 16)
                        eng.tensor_reduce(wmx[:, 0:6], wf_raw[:, 0:6 * D].rearrange("p (c d) -> p c d", d=D), AX, ALU.max,
                                          apply_absolute_value=True)
                        after(step(eng.tensor_reduce(wmx[:, 6:7], wf_raw[:, 6 * D:], AX, ALU.max, apply_absolute_value=True)))
                        after(step(eng.tensor_scalar(wsc[:], wmx[:], 1.0 / QMAX, None, ALU.mult)))
                        eng.reciprocal(winv[:], wsc[:]).then_inc(s["wmx_ready"], 1)

            def times_gate(e, slot, ci, dst):
                eng.wait_ge(s[f"g_loaded{slot}"], 8 * (e - slot) + 16)
                eng.wait_ge(s["down_done"], 2 * (FT * e + FT - 1) + ci + 1)
                eng.scalar_tensor_tensor(dst, ps[:, y_bank(slot, ci), :], b2T[:, bass.ds(e, 1)],
                                         G[:, slot, ci * 512:(ci + 1) * 512], ALU.add, ALU.mult).then_inc(s["y_mul"], 1)

            def take_y(e, slot, ci):
                if not fixed(e) or e >= 1:
                    eng.wait_ge(s["y_done"], 2 * (e - 1) + ci + 1)
                times_gate(e, slot, ci, ytmp[:, ci, :])
                if fixed(e) and e == E - 2:
                    return
                t = slice(ci * 512, (ci + 1) * 512)
                eng.wait_ge(s["y_mul"], 2 * e + ci + 1)
                eng.tensor_tensor(acc[:, t], acc[:, t], ytmp[:, ci, :], ALU.add).then_inc(s["y_done"], 1)

            eng.wait_ge(s["acc_zero"], 1)
            bias_of(0, 0)
            bias_of(1, 1)
            expert(0, 0)
            expert(1, 1)
            with eng.Fori(2, E - 3, 2) as e:
                for slot in range(2):
                    expert(e + slot, slot)
            expert(E - 2, 0)
            expert(E - 1, 1)
            for ci in range(2):
                eng.wait_ge(*lo_count(E - 1, 2, ci))
                times_gate(E - 1, 1, ci, h32[:, h_slot(2, ci), :])
            for ci in range(2):
                t = slice(ci * 512, (ci + 1) * 512)
                eng.wait_ge(s["y_mul"], 2 * (E - 1) + ci + 1)
                eng.wait_ge(s["y_added"], ci + 1)
                eng.tensor_tensor(acc[:, t], acc[:, t], h32[:, h_slot(2, ci), :], ALU.add).then_inc(s["y_done"], 1)

            for n, (t0, t1) in enumerate(((0, 2), (2, 4), (4, 8))):
                eng.wait_ge(s["acct_ready"], 1 if t1 <= 4 else 2)
                eng.scalar_tensor_tensor(xs[:, t0:t1, :], ps[:, 2 + t0 // 4, (t0 % 4) * P:(t0 % 4 + t1 - t0) * P].rearrange(
                    "p (t d) -> p t d", d=D), gth[:, 2:3], xs[:, t0:t1, :], ALU.mult, ALU.add).then_inc(s["x2_ready"], 1)
                if n == 0:
                    eng.wait_ge(s["x2_ready"], 1)
                    norm_stats(0)
            normalise(0, 7).then_inc(s["xn_ready"], 1)
            eng.wait_ge(s["xn_ready"], 7)
            x2b = step(eng.tensor_tensor(xs[:, 0:2, :], xs[:, 0:2, :], tbo[:].unsqueeze(1).broadcast_to([P, 2, D]), ALU.add))

            eng.wait_ge(s["mask_ready"], 1)

            def masked(b, gi):
                h0, nh = HG[gi]
                eng.wait_ge(s["sc1_ready"], 3 * b + gi + 1)
                eng.tensor_tensor(SC[:, b, h0:h0 + nh, :], ps[:, SCB[b][gi], 0:nh * S].rearrange("p (h s) -> p h s", s=S),
                                  maskadd[:, b, :].unsqueeze(1).broadcast_to([P, nh, S]), ALU.add).then_inc(
                    s["sc1_masked"], 1)

            def normalised_probs(b):
                eng.wait_ge(s["exp1_ready"], b + 1)
                after(step(eng.reciprocal(rc1[:, b, :], se1[:, b, :])))
                for h0 in (0, H1 // 2):
                    prv = PR[:, b, :].rearrange("p (h s) -> p h s", s=S)[:, h0:h0 + H1 // 2, :]
                    eng.tensor_tensor(prv, prv, rc1[:, b, h0:h0 + H1 // 2].unsqueeze(2).broadcast_to([P, H1 // 2, S]),
                                      ALU.mult).then_inc(s["pr_ready"], 1)

            for gi, (h0, nh) in enumerate(HG):
                masked(0, gi)
                eng.wait_ge(s["sc1_masked"], gi + 1)
                eng.tensor_reduce(nmx1[:, 0, h0:h0 + nh], SC[:, 0, h0:h0 + nh, :], AX, ALU.max, negate=True).then_inc(
                    s["nmx1_ready"], 1)
            for gi in range(len(HG)):
                masked(1, gi)
            eng.wait_ge(s["sc1_masked"], 2 * len(HG))
            after(step(eng.tensor_reduce(nmx1[:, 1, :], SC[:, 1, :, :], AX, ALU.max)))
            eng.tensor_tensor(SC[:, 1, :, :], SC[:, 1, :, :], nmx1[:, 1, :].unsqueeze(2).broadcast_to([P, H1, S]),
                              ALU.subtract).then_inc(s["nmx1_ready"], 1)
            normalised_probs(0)
            eng.wait_ge(s["exp1_ready"], 2)
            after(step(eng.tensor_reduce(se1[:, 1, :], PR[:, 1, :].rearrange("p (h s) -> p h s", s=S), AX, ALU.add)))
            normalised_probs(1)
            for c in (1, 2):
                eng.wait_ge(s["row_added"], c)
                norm_stats(c)
            eng.wait_ge(s["pt_ready"], 2)
            pt_copy_d(copy).then_inc(s["pt_evac_d"], 1)
            normalise(1, 8)
            after(step(normalise(2, 9)))
            n_xmx = step(eng.tensor_reduce(xmx[:, 0:1], xn[:, 2:8, :], mybir.AxisListType.XY, ALU.max,
                                           apply_absolute_value=True))
            after(x2b)
            for b in range(B):
                eng.wait_ge(s["pv1_ready"], b + 1)
                eng.scalar_tensor_tensor(xs[:, b, :], ps[:, b, 0:P], gth[:, 1:2], xs[:, b, :], ALU.mult, ALU.add).then_inc(
                    s["x3_ready"], 1)
            eng.wait_ge(s["x3_ready"], B)
            norm_stats(0)
            after(step(normalise(0, 10)))

            after(n_xmx)
            eng.tensor_reduce(xmx[:, 1:2], xn[:, 0:2, :], mybir.AxisListType.XY, ALU.max, apply_absolute_value=True).then_inc(
                s["xmx_ready"], 1)
            eng.wait_ge(s["xmxa_ready"], 1)
            after(step(eng.scalar_tensor_tensor(sx[:], xmxa[:, 0:1], xmxa[:, 1:2], sig127[:, 0:1], ALU.max, ALU.mult)))
            eng.reciprocal(sxi[:], sx[:]).then_inc(s["sxi_ready"], 1)
            eng.wait_ge(s["sxi_ready"], 1)
            eng.tensor_scalar(xn[:, 0:4, :], xn[:, 0:4, :], sxi[:], MAGIC, ALU.mult, ALU.add).then_inc(s["qf_d"], 1)
            eng.tensor_scalar(gsx[:], wsc[:, 0:6], sx[:], None, ALU.mult)
            eng.memset(hmx[:], 0.0)
            for half in range(2):
                eng.wait_ge(s["qt_ready"], half + 1)
                q = qT[:, half * 512:(half + 1) * 512]
                after(step(eng.tensor_scalar(q, ps[:, half, :], MAGIC, QMAX, ALU.subtract, ALU.min)))
                eng.tensor_scalar(q, q, -QMAX - 1.0, None, ALU.max).then_inc(s["q_ready"], 1)

            def largest(u):
                half, it = divmod(u, IT)
                rows = P if it < 2 else ILAST
                eng.wait_ge(s["h_ready"], u + 1)
                return step(eng.tensor_reduce(hmx[0:rows, u:u + 1], hq[0:rows, it, half * 512:(half + 1) * 512], AX, ALU.max,
                                              apply_absolute_value=True))

            for u in range(2 * IT):
                half, it = divmod(u, IT)
                rows = P if it < 2 else ILAST
                hv = hq[0:rows, it, half * 512:(half + 1) * 512]
                eng.wait_ge(s["sl_ready"], u + 1)
                eng.scalar_tensor_tensor(hv, ps[0:rows, 2 * (u % 3) + GUB + 1, :], gsx[0:rows, 3 + it:4 + it],
                                         sl[0:rows, u % 2, :], ALU.mult, ALU.mult).then_inc(s["h_ready"], 1)
                if u >= 1:
                    n = largest(u - 1)
            n = largest(2 * IT - 1)
            after(n)
            eng.tensor_reduce(hmxr[:], hmx[:], AX, ALU.max).then_inc(s["hmx_ready"], 1)
            eng.wait_ge(s["hmxa_ready"], 1)
            after(step(eng.tensor_tensor(sh[:], hmxa[:], sig127[:, 1:2], ALU.mult)))
            eng.reciprocal(shi[:], sh[:]).then_inc(s["shi_ready"], 1)
            eng.wait_ge(s["sd_evac"], 1)
            sd_step = step(eng.tensor_scalar(sdgs[:], sdg[:], sh[:], None, ALU.mult))
            eng.wait_ge(s["shi_ready"], 1)

            def h_part(u):
                half, it = divmod(u, IT)
                return slice(0, P if it < 2 else ILAST), it, slice(half * 512, (half + 1) * 512)

            def clipped_below(u, n):
                after(n)
                h = hqb[h_part(u)]
                eng.tensor_scalar(h, h, -QMAX - 1.0, None, ALU.max).then_inc(s["hqb_ready"], 1)

            scaled = 0
            for u in range(2 * IT):
                part = h_part(u)
                if u == HQ_DVE:
                    after(step(eng.tensor_scalar(hq[part], hq[part], shi[:], MAGIC, ALU.mult, ALU.add)))
                elif u == HQ_POOL:
                    eng.wait_ge(s["hqf_ready_p"], 1)
                else:
                    scaled += 1
                    eng.wait_ge(s["hqf_ready"], scaled)
                n = step(eng.tensor_scalar(hqb[part], hq[part], MAGIC, QMAX, ALU.subtract, ALU.min))
                if u >= 1:
                    clipped_below(u - 1, n - 1)
            clipped_below(2 * IT - 1, n)
            after(sd_step)
            for half in range(2):
                eng.wait_ge(s["dn_ready"], half + 1)
                o = otmp[:, 4 * half:4 * half + 4, :]
                eng.tensor_tensor(o, ps[:, half, :].rearrange("p (t d) -> p t d", d=D),
                                  sdgs[:].unsqueeze(1).broadcast_to([P, 4, D]), ALU.mult).then_inc(s["o_ready"], 1)
                eng.wait_ge(s["o_ready"], half + 1)
                xh = xs[:, 4 * half:4 * half + 4, :]
                eng.tensor_tensor(xh, xh, o, ALU.add).then_inc(s["out_ready"], 1)


def kernel(**inputs):
    import numpy as _np
    import concourse.bacc as _bacc
    from concourse import mybir as _mybir
    from concourse.bass_utils import run_bass_kernel_spmd as _run

    a = {k: _np.asarray(v) for k, v in inputs.items()}

    def rows(v):
        v = v.reshape(1, -1)
        return _np.broadcast_to(v, (P, v.shape[1]))

    def tiles(w):
        return w.reshape(-1, P, w.shape[1]).transpose(1, 0, 2).reshape(P, -1)

    def padded(w):
        return tiles(_np.concatenate([w, _np.ones((IT * P - I, D), w.dtype)]))

    early = dict(ctxT=a["ctx_1024"].reshape(B * S, D).T, wkT2=_np.concatenate([a["L0_xattn_Wk"].T] * 2, axis=1),
                 wvT=a["L0_xattn_Wv"].T, woT=a["L0_xattn_Wo"].T, wq=a["L0_xattn_Wq"])
    late = dict(b1T=a["L0_ffn_b1"].reshape(E * FT, P).T, b2T=a["L0_ffn_b2"].T, wr=a["L0_ffn_Wr"],
                gsc=rows(_np.concatenate([a["g_xattn"], a["g_ffn"], a["L1_ffn_clip_x"], a["L1_ffn_clip_down"]])),
                br=rows(a["L0_ffn_br"]), bo=rows(a["L1_xattn_bo"]),
                lam=rows(_np.concatenate([a[f"L0_xattn_lambda_{n}"] for n in ("q1", "q2", "k1", "k2")])))
    experts = _np.concatenate([a["L0_ffn_W1"], a["L0_ffn_W2"].reshape(E, FT, P, D).transpose(0, 2, 1, 3).reshape(E, P, FT * D)],
                              axis=2)
    sent = dict(
        x=a["x"],
        early=_np.concatenate([early[n] for n in EARLY], axis=1),
        late=_np.concatenate([late[n] for n in LATE], axis=1),
        mask=rows(a["mask_BxS2_bk0"]),
        l1w=_np.concatenate([tiles(a["L1_xattn_Wq"].T), a["L1_xattn_Wkv"], tiles(a["L1_xattn_Wo"])], axis=1),
        ffnw=_np.concatenate([padded(a["L1_ffn_w_gate"]), padded(a["L1_ffn_w_up"]), a["L1_ffn_w_down"]], axis=1),
        experts=experts,
    )
    nc = _bacc.Bacc("TRN2", target_bir_lowering=False, num_devices=1)
    arrays, args = {}, []
    for name, v in sent.items():
        v = _np.ascontiguousarray(v)
        arrays[f"in_{name}"] = v
        args.append(nc.dram_tensor(f"in_{name}", v.shape, _mybir.dt.from_np(v.dtype), kind="ExternalInput").ap())
    args.append(nc.dram_tensor("out_0", (B, N, D), F32, kind="ExternalOutput").ap())
    build(nc, *args)
    r = _run(nc, [arrays], core_ids=[0])
    return r.results[0]["out_0"]
```
